# Optimizing a Trainium2 kernel written in Bass

```python
import numpy as np
import jax
import jax.numpy as jnp

def _softmax(x, axis=-1):
    return jax.nn.softmax(x, axis=axis)

def _gelu(x):
    return jax.nn.gelu(x, approximate=True)

def _silu(x):
    return jax.nn.silu(x)

def _sigmoid(x):
    return jax.nn.sigmoid(x)

def _layernorm(x, axis=-1, eps=1e-05):
    m = jnp.mean(x, axis=axis, keepdims=True)
    v = jnp.var(x, axis=axis, keepdims=True)
    return (x - m) / jnp.sqrt(v + eps)

def _scatter_add(tgt, idx, src, axis=0):
    return tgt.at[idx].add(src)

def _segment_sum(src, seg, n):
    return jax.ops.segment_sum(src, seg, n)
kernel_name = 'mk_adj_ffn_d1_adj_r2_e3c1ee'

def setup_inputs(seed: int=0):
    np.random.seed(seed)
    _w = jnp.asarray

    def _rec_inputs():
        import jax
        import jax.numpy as jnp
        _gk = jax.random.key(seed)
        x = -0.0002928 + 1 * jax.random.normal(jax.random.fold_in(_gk, 1), (16, 512, 128), jnp.float32)
        _w = (1.0 + jnp.arange(512, dtype=jnp.float32)) ** (-0.5)
        _w = _w / _w.mean()
        _pij = jnp.clip(0.00390625 * _w[:, None] * _w[None, :], 0.0, 1.0)
        _a = jax.random.uniform(jax.random.fold_in(_gk, 2), (16, 512, 512)) < _pij
        _af = _a.astype(jnp.float32)
        _af = _af * jax.random.uniform(jax.random.fold_in(_gk, 3), (16, 512, 512), jnp.float32, 0.05, 0.999995)
        adj = _af
        return (x, adj)
    x, adj = _rec_inputs()

    def _L0_gnn_setup():
        import jax, jax.numpy as jnp
        import numpy as np
        B, N, D = (4, 2048, 128)
        DENSITY = 0.02
        key = jax.random.key(seed)
        kx, ka1, ka2, kwt, kbt, kwh, kth = jax.random.split(key, 7)
        x = jax.random.normal(kx, (B, N, D), dtype=jnp.float32)
        mask = jax.random.uniform(ka1, (B, N, N)) < DENSITY
        vals = jax.random.uniform(ka2, (B, N, N), dtype=jnp.float32)
        adj = jnp.where(mask, vals, 0.0).astype(jnp.float32)
        s = 0.02
        W_t = s * jax.random.normal(kwt, (D, D), dtype=jnp.float32)
        b_t = s * jax.random.normal(kbt, (D,), dtype=jnp.float32)
        W_h = s * jax.random.normal(kwh, (D, D), dtype=jnp.float32)
        theta = s * jax.random.normal(kth, (D, D), dtype=jnp.float32)
        return {'x': x, 'adj': adj, 'W_t': W_t, 'b_t': b_t, 'W_h': W_h, 'theta': theta}
    _L0_gnn_all = _L0_gnn_setup()
    _L0_gnn_in = {k: v for k, v in _L0_gnn_all.items() if k in ('W_t', 'b_t', 'W_h', 'theta')}
    del _L0_gnn_all

    def _L0_ffn_setup():
        import jax, jax.numpy as jnp
        import numpy as np
        B, S, D, F, E, K = (8, 1024, 128, 512, 8, 2)
        key = jax.random.key(seed)
        ks = jax.random.split(key, 10)
        s = 0.02
        return {'x': jax.random.normal(ks[0], (B, S, D), dtype=jnp.float32), 'Wr': jax.random.normal(ks[1], (D, E), dtype=jnp.float32) * s, 'W1s': jax.random.normal(ks[2], (D, F), dtype=jnp.float32) * s, 'b1s': jnp.zeros((F,), dtype=jnp.float32), 'W2s': jax.random.normal(ks[3], (F, D), dtype=jnp.float32) * s, 'b2s': jnp.zeros((D,), dtype=jnp.float32), 'W1p': jax.random.normal(ks[4], (E, D, F), dtype=jnp.float32) * s, 'b1p': jnp.zeros((E, F), dtype=jnp.float32), 'W2p': jax.random.normal(ks[5], (E, F, D), dtype=jnp.float32) * s, 'b2p': jnp.zeros((E, D), dtype=jnp.float32)}
    _L0_ffn_all = _L0_ffn_setup()
    _L0_ffn_in = {k: v for k, v in _L0_ffn_all.items() if k in ('Wr', 'W1s', 'b1s', 'W2s', 'b2s', 'W1p', 'b1p', 'W2p', 'b2p')}
    del _L0_ffn_all
    return {'x': x, 'adj': adj, 'L0_gnn_W_t': _L0_gnn_in['W_t'], 'L0_gnn_b_t': _L0_gnn_in['b_t'], 'L0_gnn_W_h': _L0_gnn_in['W_h'], 'L0_gnn_theta': _L0_gnn_in['theta'], 'L0_ffn_Wr': _L0_ffn_in['Wr'], 'L0_ffn_W1s': _L0_ffn_in['W1s'], 'L0_ffn_b1s': _L0_ffn_in['b1s'], 'L0_ffn_W2s': _L0_ffn_in['W2s'], 'L0_ffn_b2s': _L0_ffn_in['b2s'], 'L0_ffn_W1p': _L0_ffn_in['W1p'], 'L0_ffn_b1p': _L0_ffn_in['b1p'], 'L0_ffn_W2p': _L0_ffn_in['W2p'], 'L0_ffn_b2p': _L0_ffn_in['b2p']}

def reference(x, adj, L0_gnn_W_t, L0_gnn_b_t, L0_gnn_W_h, L0_gnn_theta, L0_ffn_Wr, L0_ffn_W1s, L0_ffn_b1s, L0_ffn_W2s, L0_ffn_b2s, L0_ffn_W1p, L0_ffn_b1p, L0_ffn_W2p, L0_ffn_b2p):
    import jax
    import jax.numpy as jnp

    def _L0_gnn_ref(x, adj, W_t, b_t, W_h, theta):
        import jax, jax.numpy as jnp
        import numpy as np
        B, N, D = (4, 2048, 128)
        DENSITY = 0.02
        in_degrees = jnp.sum(adj, axis=-1)
        norm = jnp.power(in_degrees + 1e-06, -0.5)[..., None]
        f_hom = jnp.einsum('bnd,de->bne', x, theta) * norm
        f_hom = jnp.einsum('bnm,bmd->bnd', adj, f_hom) * norm
        f_het = jnp.einsum('bnd,de->bne', x, W_h)
        gate = jax.nn.sigmoid(jnp.einsum('bnd,de->bne', x, W_t) + b_t)
        out = gate * f_hom + (1.0 - gate) * f_het
        return jax.nn.elu(out)

    def _L0_ffn_ref(x, Wr, W1s, b1s, W2s, b2s, W1p, b1p, W2p, b2p):
        import jax, jax.numpy as jnp
        import numpy as np
        B, S, D, F, E, K = (8, 1024, 128, 512, 8, 2)
        gelu = lambda t: jax.nn.gelu(t, approximate=False)
        shared = gelu(x @ W1s + b1s) @ W2s + b2s
        rw = jax.nn.softmax(x @ Wr, axis=-1)
        topw, topi = jax.lax.top_k(rw, K)
        topw = topw / jnp.sum(topw, axis=-1, keepdims=True)
        mask = jnp.sum(jax.nn.one_hot(topi, E, dtype=topw.dtype) * topw[..., None], axis=-2)
        h = gelu(jnp.einsum('bsd,edf->bsef', x, W1p) + b1p)
        priv = jnp.einsum('bsef,efd->bsed', h, W2p) + b2p
        routed = jnp.einsum('bsed,bse->bsd', priv, mask)
        return shared + routed
    x = x + _L0_gnn_ref(_layernorm(x, axis=-1), adj, L0_gnn_W_t, L0_gnn_b_t, L0_gnn_W_h, L0_gnn_theta)
    x = x + _L0_ffn_ref(_layernorm(x, axis=-1), L0_ffn_Wr, L0_ffn_W1s, L0_ffn_b1s, L0_ffn_W2s, L0_ffn_b2s, L0_ffn_W1p, L0_ffn_b1p, L0_ffn_W2p, L0_ffn_b2p)
    return x

_drawn_inputs = setup_inputs


def setup_inputs(seed=0):
    import zlib

    import numpy as np

    out = dict(_drawn_inputs(seed))
    spreads = {'L0_ffn_b1s': (0.0, 0.8),
     'L0_ffn_b2s': (0.0, 0.8),
     'L0_ffn_b1p': (0.0, 0.8),
     'L0_ffn_b2p': (0.0, 2.0)}
    factors = {'L0_gnn_b_t': 5.716,
     'L0_gnn_W_h': 8.0,
     'L0_ffn_Wr': 8.0,
     'L0_ffn_W1s': 8.0,
     'L0_ffn_W2s': 8.0,
     'L0_ffn_W1p': 8.0,
     'L0_ffn_W2p': 8.0}
    for name, (base, spread) in spreads.items():
        noise = np.random.default_rng([zlib.crc32(name.encode()), seed]).standard_normal(out[name].shape)
        drawn = base * np.exp(spread * noise) if base else spread * noise
        out[name] = jnp.asarray(drawn.astype(out[name].dtype))
    for name, factor in factors.items():
        out[name] = (out[name] * factor).astype(out[name].dtype)
    return out
```

```python
from contextlib import ExitStack

import concourse.bass as bass
from concourse import mybir

ALU = mybir.AluOpType
ACT = mybir.ActivationFunctionType
AX = mybir.AxisListType
F32 = mybir.dt.float32
F16 = mybir.dt.float16
I32 = mybir.dt.int32

P = 128
WS = 64.0
BLK = 256
GROUPS = 2
RING = 4
AHEAD = 6
BIG = 1.0e30
LN_EPS, DEG_EPS = 1e-5, 1e-6
MIX_GATE, MIX_HET, MIX_HOM, MIX_X2, MIX = 1, 5, 9, 13, 15
R_M1, R_M2, R_ONE2, R_MASK, R_GAP, R_PREFIX, ROUTE = 1, 7, 11, 12, 13, 15, 22


def build(nc, x, adj, W_t, b_t, W_h, theta, Wr, W1s, b1s, W2s, b2s, W1p, b1p, W2p, b2p, out):
    NB, S, D = x.shape
    T = S // P
    F = W1s.shape[1]
    FC = F // P
    E = Wr.shape[1]
    assert D == P and S == 512 and F == 512 and E == 8 and NB % (2 * GROUPS * RING) == 0
    BG = NB // GROUPS
    GT = BG * S
    REG = GT + BLK
    NBLK = (2 * GT - E) // BLK + E
    NBLK += NBLK % 2
    NK = GROUPS * NBLK
    PADROW = GROUPS * E * REG
    MAXB = GT // BLK

    rows = nc.dram_tensor("expert_rows", (PADROW + BLK, 2 * D), F16, kind="Internal").ap()
    ys = [nc.dram_tensor(f"expert_out{g}", (NBLK * BLK, D), F32, kind="Internal").ap() for g in range(GROUPS)]
    xc_dram = nc.dram_tensor("xn2_t", (NB * P, 2 * S), F16, kind="Internal").ap()

    with ExitStack() as ctx:
        def sb(name, shape, dt=F32):
            return ctx.enter_context(nc.sbuf_tensor(name, shape, dt))

        def sem(name):
            return ctx.enter_context(nc.semaphore(name))

        def sem2(name):
            return [sem(name + "_even"), sem(name + "_odd")]

        ps = ctx.enter_context(nc.psum_tensor("ps", [P, 8, 512], F32))

        ident = sb("ident", [P, P])
        ident16 = sb("ident16", [P, P], F16)
        before = sb("before", [P, P], F16)
        ones16 = sb("ones16", [P, P], F16)
        ones_row = sb("ones_row", [1, P])
        zeros16 = sb("zeros16", [P, 2, 2 * D], F16)
        eps = sb("eps", [P, T, 2])
        mhalf = sb("mhalf", [P, T, 2])
        iota_e = sb("iota_e", [P, T, E])
        blk_iota = sb("blk_iota", [P, NBLK])
        cap_iota = sb("cap_iota", [P, MAXB])
        lower = sb("lower", [P, E, E])
        reg_base = [sb(f"reg_base{g}", [P, E]) for g in range(GROUPS)]
        w_gnn = sb("w_gnn", [P, 3 * D])
        bt_row = sb("bt_row", [1, D])
        wr_f = sb("wr_f", [P, E])
        wr16 = sb("wr16", [P, 2, E], F16)
        w_stage = sb("w_stage", [P, 2, 2, 512])
        w1 = sb("w1", [P, E + 1, 2, F], F16)
        w2 = sb("w2", [P, E + 1, 2, FC, D], F16)
        b1_rows = sb("b1_rows", [P, P])
        b1 = sb("b1", [P, (E + 1) * FC])
        b2 = sb("b2", [P, E, D])
        b2s_bc = sb("b2s_bc", [P, D])

        xin = sb("xin", [P, 2, T, D])
        adj_sb = sb("adj_sb", [P, 2, T, S])
        stats = sb("stats", [P, T, 6])
        mvd = sb("mvd", [P, 2, T, 3])
        pw1 = sb("pw1", [P, T, 2])
        rs1 = sb("rs1", [P, 2, T, 2])
        xn = sb("xn", [P, T, D])
        xn_t = sb("xn_t", [P, S])
        adj_t = sb("adj_t", [P, T, S])
        f_sb = sb("f_sb", [P, T, D])
        th = sb("th", [P, T, D])
        gate = sb("gate", [P, T, D])
        het = sb("het", [P, T, D])
        mix_o = sb("mix_o", [P, T, D])
        mix_m = sb("mix_m", [P, T, D])
        mix_e = sb("mix_e", [P, T, D])
        x2 = sb("x2", [P, 2, T, D])
        stats2 = sb("stats2", [P, T, 6])
        mv2 = sb("mv2", [P, 2, T, 2])
        pw2 = sb("pw2", [P, T])
        rs2 = sb("rs2", [P, 2, T])
        xn2 = sb("xn2", [P, T, D])
        xr = sb("xr", [P, 2, T, 2, D], F16)
        xc = sb("xc", [P, 2, 2, S], F16)
        r_top = sb("r_top", [P, 2, T])
        r_ne = sb("r_ne", [P, T, E])
        r_cand = sb("r_cand", [P, T, E])
        r_idx = sb("r_idx", [P, T])
        r_l2 = sb("r_l2", [P, T, E])
        r_mask = sb("r_mask", [P, 2, T, E], F16)
        r_red = sb("r_red", [P, E])
        prefix = [sb(f"prefix{g}", [P, 2, E], F16) for g in range(GROUPS)]
        r_gap = sb("r_gap", [P, T])
        r_exp = sb("r_exp", [P, T])
        r_sum = sb("r_sum", [P, T])
        r_pos = sb("r_pos", [P, T, E])
        r_prod = sb("r_prod", [P, 2 * T, E])
        kp = sb("kp", [P, 2, 80])
        idx = sb("idx", [P, 2, 2 * T], I32)
        keep = sb("keep", [P, NB, 80])
        x2_all = sb("x2_all", [P, NB, T * D])

        t_cnt = sb("t_cnt", [P, E])
        t_cmp = sb("t_cmp", [P, E, MAXB])
        t_nblk = sb("t_nblk", [P, E])
        t_low = sb("t_low", [P, E, E])
        t_start = sb("t_start", [P, E])
        t_end = sb("t_end", [P, E])
        t_delta = sb("t_delta", [P, E])
        t_past = sb("t_past", [P, NBLK, E])
        t_eraw = sb("t_eraw", [P, NBLK])
        t_used = sb("t_used", [P, NBLK])
        t_off = sb("t_off", [P, NBLK])
        t_row = sb("t_row", [P, NBLK])
        tab_e = sb("tab_e", [P, NK], I32)
        tab_row = sb("tab_row", [P, NK], I32)
        tab_pad = sb("tab_pad", [P, GROUPS * E], I32)
        y_prod = sb("y_prod", [P, BG * 2 * T, E])
        y_off = sb("y_off", [P, BG * 2 * T])
        y_idx = sb("y_idx", [P, GROUPS, BG * 2 * T], I32)

        h_sb = adj_sb
        h_hi = sb("h_hi", [P, 2, FC, 512], F16)
        h_lo = sb("h_lo", [P, 2, FC, 512], F16)
        deg_junk = h_hi[:, 0]
        rows_sb = sb("rows_sb", [P, 2, 2, 2 * D], F16)
        xb = sb("xb", [P, 2, 2, BLK], F16)
        y_sb = sb("y_sb", [P, 2, 2, D])
        xcb = sb("xcb", [P, 2, 2, S], F16)
        yg = sb("yg", [P, RING, 2 * T, D])
        wb = sb("wb", [P, 2, 2 * T])
        acc = sb("acc", [P, 2, T * D])

        const_in, bias_in, w_in = sem("const_in"), sem("bias_in"), sem2("w_in")
        const_made, w_high, w_low, setup_v = sem("const_made"), sem("w_high"), sem("w_low"), sem("setup_v")
        b1_turned, pad_zeroed, empty_zeroed = sem("b1_turned"), sem("pad_zeroed"), sem("empty_zeroed")
        x_in, adj_in = sem2("x_in"), sem2("adj_in")
        x2_saved, xc_saved, keep_saved, scattered = sem2("x2_saved"), sem2("xc_saved"), sem2("keep_saved"), sem2("scattered")
        stats1, eps1, rsq1, xn_done, deg_done = sem("stats1"), sem("eps1"), sem("rsq1"), sem("xn_done"), sem("deg_done")
        adj_turned, adj_out, xn_turned, xn_out = sem("adj_turned"), sem("adj_out"), sem("xn_turned"), sem("xn_out")
        proj_done, th_done, hom_done, mix, elu_exp = sem("proj_done"), sem("th_done"), sem("hom_done"), sem("mix"), sem("elu_exp")
        eps2, rsq2, xn2_done, high_done, low_done = sem("eps2"), sem("rsq2"), sem("xn2_done"), sem("high_done"), sem("low_done")
        xc_turned, xc_out, logits_done, gap_exp, rank_done, route, rows_go = (
            sem("xc_turned"), sem("xc_out"), sem("logits_done"), sem("gap_exp"), sem("rank_done"), sem("route"), sem("rows_go"))
        count_done, tables = sem("count_done"), sem("tables")
        rows_in, y_saved, rows_turned, xb_out = sem2("rows_in"), sem2("y_saved"), sem("rows_turned"), sem("xb_out")
        up_done, h_done, split_hi, split_done, down_done, y_done = (
            sem("up_done"), sem("h_done"), sem("split_hi"), sem("split_done"), sem("down_done"), sem("y_done"))
        xcb_in, out_saved, gathered = sem2("xcb_in"), sem2("out_saved"), [sem(f"gathered{r}") for r in range(RING)]
        sh_up, sh_h, sh_hi, sh_split, sh_down, sh_acc, wb_done = (
            sem("sh_up"), sem("sh_h"), sem("sh_hi"), sem("sh_split"), sem("sh_down"), sem("sh_acc"), sem("wb_done"))

        TABLES = 14

        def back(half, par, n):
            q = (par - n) % 2
            h = half + (par - n - q) // 2
            return 2 * h + q, h, q

        def known(b):
            return isinstance(b, int)

        def steps(eng, body):
            for half in range(2):
                body(half, 0)
            for g in range(GROUPS):
                lo = 2 if g == 0 else g * BG // 2 + 1
                with eng.Fori(lo, (g + 1) * BG // 2 + (g < GROUPS - 1)) as half:
                    body(half, g)
            body(NB // 2, GROUPS - 1)

        block = ctx.enter_context(nc.Block())

        @block.sync
        def _(sp):
            def load(half, par):
                b, turn, p = back(half, par, 0)
                if not (known(b) and b < 2):
                    sp.wait_ge(mix, MIX * (b - 2) + MIX_X2)
                sp.dma_start(xin[:, p], x[bass.ds(b, 1)].rearrange("a (t p) d -> p (a t) d", p=P)).then_inc(x_in[p], 16)
                if not (known(b) and b < 2):
                    sp.wait_ge(adj_turned, T * (b - 1))
                    sp.wait_ge(deg_done, b - 1)
                sp.dma_start(adj_sb[:, p], adj[bass.ds(b, 1)].rearrange("a (t p) m -> p (a t) m", p=P)).then_inc(adj_in[p], 16)

            def save(half, par):
                b, turn, p = back(half, par, 1)
                if not (known(b) and not 0 <= b < NB):
                    sp.wait_ge(mix, MIX * b + MIX_X2)
                    sp.dma_start(x2_all[:, bass.ds(b, 1), :], x2[:, p].rearrange("p t d -> p (t d)")).then_inc(x2_saved[p], 16)
                b, turn, p = back(half, par, 2)
                if not (known(b) and not 0 <= b < NB):
                    sp.wait_ge(xc_out, b + 1)
                    sp.dma_start(xc_dram[bass.ds(b * P, P), :], xc[:, p].rearrange("p h s -> p (h s)")).then_inc(xc_saved[p], 16)
                    sp.wait_ge(route, ROUTE * (b + 1))
                    sp.dma_start(keep[:, bass.ds(b, 1), :], kp[:, p]).then_inc(keep_saved[p], 16)

            def body(half, g):
                for par in range(2):
                    b = back(half, par, 0)[0]
                    if not (known(b) and b >= NB):
                        load(half, par)
                    save(half, par)

            for src, dst in ((W_t, w_gnn[:, 0:D]), (W_h, w_gnn[:, D:2 * D]), (theta, w_gnn[:, 2 * D:3 * D]), (Wr, wr_f[:])):
                sp.dma_start(dst, src).then_inc(const_in, 16)
            sp.dma_start(bt_row[:], b_t.rearrange("(a d) -> a d", a=1)).then_inc(const_in, 16)
            steps(sp, body)

            for g in range(GROUPS):
                sp.wait_ge(tables, TABLES * (g + 1))
                for e in range(E):
                    row = sp.value_load(tab_pad[0:1, g * E + e:g * E + e + 1], min_val=0, max_val=PADROW - BLK)
                    sp.dma_start(rows[bass.ds(row, BLK), :].rearrange("(s p) c -> p s c", p=P), zeros16[:]).then_inc(pad_zeroed, 16)
            sp.wait_ge(pad_zeroed, 16 * GROUPS * E)
            sp.wait_ge(empty_zeroed, 16)
            for q in range(2):
                sp.wait_ge(scattered[q], 16 * 2 * T * NB // 2)

            def block_in(k, q, first):
                row = sp.value_load(tab_row[0:1, bass.ds(k, 1)], min_val=0, max_val=PADROW)
                if not first:
                    sp.wait_ge(rows_turned, k - 1)
                sp.dma_start(rows_sb[:, q], rows[bass.ds(row, BLK), :].rearrange("(s p) c -> p s c", p=P)).then_inc(rows_in[q], 16)

            def block_out(g, n, q):
                sp.wait_ge(y_done, g * NBLK + n + 1)
                sp.dma_start(ys[g][bass.ds(n * BLK, BLK), :].rearrange("(s p) d -> p s d", p=P), y_sb[:, q]).then_inc(y_saved[q], 16)

            for k in range(AHEAD):
                block_in(k, k % 2, k < 2)
            for g in range(GROUPS):
                tail = AHEAD if g == GROUPS - 1 else 0
                with sp.Fori(0, (NBLK - tail) // 2) as half:
                    for q in range(2):
                        block_in(g * NBLK + 2 * half + q + AHEAD, q, False)
                        block_out(g, 2 * half + q, q)
                for n in range(NBLK - tail, NBLK):
                    block_out(g, n, n % 2)

            def xc_in(b, q):
                sp.dma_start(xcb[:, q].rearrange("p h s -> p (h s)"), xc_dram[bass.ds(b * P, P), :]).then_inc(xcb_in[q], 16)

            def out_to(b, q):
                sp.wait_ge(sh_acc, 9 * (b + 1))
                sp.dma_start(out[bass.ds(b, 1)].rearrange("a (t p) d -> p (a t) d", p=P), acc[:, q].rearrange("p (t d) -> p t d", d=D)
                             ).then_inc(out_saved[q], 16)

            for q in range(2):
                sp.wait_ge(xc_saved[q], 16 * NB // 2)
            xc_in(0, 0)
            xc_in(1, 1)
            with sp.Fori(0, NB // 2 - 1) as half:
                for q in range(2):
                    b = 2 * half + q
                    sp.wait_ge(sh_up, FC * (b + 1))
                    xc_in(b + 2, q)
                    out_to(b, q)
            for q in range(2):
                out_to(NB - 2 + q, q)
            for q in range(2):
                sp.wait_ge(out_saved[q], 16 * NB // 2)

        @block.gpsimd
        def _(pool):
            pool.memset(zeros16[:], 0.0).then_inc(const_made, 1)
            pool.memset(b1_rows[:], 0.0).then_inc(const_made, 1)
            pool.wait_ge(const_made, 2)
            pool.dma_start(b1_rows[0:E * FC, :], b1p.rearrange("e (c p) -> (e c) p", p=P)).then_inc(bias_in, 16)
            pool.dma_start(b1_rows[E * FC:(E + 1) * FC, :], b1s.rearrange("(c p) -> c p", p=P)).then_inc(bias_in, 16)
            pool.dma_start(b2[:], b2p.rearrange("(a e) d -> a e d", a=1).to_broadcast([P, E, D])).then_inc(bias_in, 16)
            pool.dma_start(b2s_bc[:], b2s.rearrange("(a d) -> a d", a=1).to_broadcast([P, D])).then_inc(bias_in, 16)
            pool.dma_start(rows[PADROW:PADROW + BLK, :].rearrange("(s p) c -> p s c", p=P), zeros16[:]).then_inc(empty_zeroed, 16)
            pool.memset(ident[:], 0.0).then_inc(const_made, 1)
            pool.memset(before[:], 1.0).then_inc(const_made, 1)
            pool.memset(ones16[:], 1.0).then_inc(const_made, 1)
            pool.memset(ones_row[:], 1.0).then_inc(const_made, 1)
            pool.memset(mhalf[:], -0.5).then_inc(const_made, 1)
            pool.memset(eps[:, :, 0:1], LN_EPS).then_inc(const_made, 1)
            pool.memset(eps[:, :, 1:2], DEG_EPS).then_inc(const_made, 1)
            pool.iota(iota_e[:], [[0, T], [1, E]], base=0, channel_multiplier=0, allow_small_or_imprecise_dtypes=True).then_inc(const_made, 1)
            pool.wait_ge(const_made, 10)
            pool.affine_select(out=ident[:], in_=ident[:], compare_op=ALU.not_equal, fill=1.0, base=0,
                               pattern=[[-1, P]], channel_multiplier=1).then_inc(const_made, 1)
            pool.affine_select(out=before[:], in_=before[:], compare_op=ALU.is_gt, fill=0.0, base=0,
                               pattern=[[1, P]], channel_multiplier=-1).then_inc(const_made, 1)
            pool.wait_ge(const_made, 12)
            pool.tensor_copy(ident16[:], ident[:]).then_inc(const_made, 1)

            def weights_in(e, q):
                if e >= 2:
                    pool.wait_ge(w_low, e - 1)
                u, d = (W1p[e], W2p[e]) if e < E else (W1s, W2s)
                pool.dma_start(w_stage[:, q, 0, :], u).then_inc(w_in[q], 16)
                pool.dma_start(w_stage[:, q, 1, :].rearrange("p (c d) -> p c d", c=FC), d.rearrange("(c p) d -> p c d", p=P)).then_inc(w_in[q], 16)

            for e in range(E + 1):
                weights_in(e, e % 2)
            pool.iota(blk_iota[:], [[1, NBLK]], base=0, channel_multiplier=0, allow_small_or_imprecise_dtypes=True).then_inc(const_made, 1)
            pool.iota(cap_iota[:], [[BLK, MAXB]], base=0, channel_multiplier=0, allow_small_or_imprecise_dtypes=True).then_inc(const_made, 1)
            for g in range(GROUPS):
                pool.iota(reg_base[g][:], [[REG, E]], base=g * E * REG, channel_multiplier=0, allow_small_or_imprecise_dtypes=True).then_inc(const_made, 1)
                pool.memset(prefix[g][:], 0.0).then_inc(const_made, 1)
            pool.memset(lower[:], 0.0).then_inc(const_made, 1)
            pool.wait_ge(const_made, 16 + 2 * GROUPS)
            for e in range(1, E):
                pool.memset(lower[:, e, 0:e], 1.0).then_inc(const_made, 1)

            def rsqrt1(half, par):
                b, turn, p = back(half, par, 0)
                pool.wait_ge(stats1, 2 * (b + 1))
                pool.wait_ge(deg_done, b + 1)
                pool.tensor_tensor(pw1[:], mvd[:, p, :, 1:3], eps[:], ALU.add).then_inc(eps1, 1)
                pool.wait_ge(eps1, b + 1)
                if not (known(b) and b < 2):
                    pool.wait_ge(mix, MIX * (b - 2) + MIX_HOM)
                pool.tensor_tensor(rs1[:, p], pw1[:], mhalf[:], ALU.pow).then_inc(rsq1, 1)

            def rsqrt2(half, par):
                b, turn, p = back(half, par, 1)
                pool.wait_ge(mix, MIX * (b + 1))
                pool.tensor_tensor(pw2[:], mv2[:, p, :, 1], eps[:, :, 0], ALU.add).then_inc(eps2, 1)
                pool.wait_ge(eps2, b + 1)
                pool.tensor_tensor(rs2[:, p], pw2[:], mhalf[:, :, 0], ALU.pow).then_inc(rsq2, 1)

            def scatter(half, par):
                b, turn, p = back(half, par, 2)
                pool.wait_ge(low_done, b + 1)
                pool.wait_ge(high_done, b + 1)
                pool.wait_ge(route, ROUTE * (b + 1))
                pool.sem_inc(rows_go, 1)
                for j in range(2 * T):
                    pool.indirect_dma_start(rows, bass.IndirectOffsetOnAxis(ap=idx[:, p, j:j + 1], axis=0),
                                            xr[:, p, j % T].rearrange("p h d -> p (h d)"), None).then_inc(scattered[p], 16)

            def body(half, g):
                for par in range(2):
                    b = back(half, par, 0)[0]
                    if not (known(b) and b >= NB):
                        rsqrt1(half, par)
                    if not (known(b) and not 0 <= b - 1 < NB):
                        rsqrt2(half, par)
                    if not (known(b) and not 0 <= b - 2):
                        scatter(half, par)

            steps(pool, body)

            for g in range(GROUPS):
                for q in range(2):
                    pool.wait_ge(y_saved[q], 16 * (g + 1) * NBLK // 2)
                for b in range(g * BG, (g + 1) * BG):
                    r = b % RING
                    if b >= RING:
                        pool.wait_ge(sh_acc, 9 * (b - RING + 1))
                    for j in range(2 * T):
                        n = (b - g * BG) * 2 * T + j
                        pool.indirect_dma_start(yg[:, r, j], None, ys[g],
                                                bass.IndirectOffsetOnAxis(ap=y_idx[:, g, n:n + 1], axis=0)).then_inc(gathered[r], 16)

        @block.scalar
        def _(act):
            def adj_to_sbuf(half, par, j):
                b, turn, p = back(half, par, 1)
                act.wait_ge(adj_turned, T * b + j + 1)
                if j == 0 and not (known(b) and b < 1):
                    act.wait_ge(hom_done, b)
                act.activation(adj_t[:, j], ps[:, j % 2], ACT.Copy).then_inc(adj_out, 1)

            def high(half, par):
                b, turn, p = back(half, par, 2)
                act.wait_ge(xn2_done, b + 1)
                if not (known(b) and b < 2):
                    act.wait_ge(scattered[p], 16 * 2 * T * turn)
                    act.wait_ge(xc_turned, b - 1)
                act.activation(xr[:, p, :, 0, :], xn2[:], ACT.Copy).then_inc(high_done, 1)

            def xn_to_sbuf(half, par):
                b, turn, p = back(half, par, 1)
                act.wait_ge(xn_turned, b + 1)
                if not (known(b) and b < 1):
                    act.wait_ge(proj_done, T * b)
                act.activation(xn_t[:], ps[:, 2], ACT.Copy).then_inc(xn_out, 1)

            def messages(half, par):
                b, turn, p = back(half, par, 1)
                act.wait_ge(rsq1, b + 1)
                if not (known(b) and b < 1):
                    act.wait_ge(hom_done, b)
                    act.wait_ge(mix, MIX * (b - 1) + MIX_HET)
                for t in range(T):
                    act.wait_ge(proj_done, T * b + t + 1)
                    act.activation(f_sb[:, t], ps[:, 3 + t % 2, 2 * D:3 * D], ACT.Copy, scale=rs1[:, p, t, 1:2])
                    act.activation(th[:, t], ps[:, 3 + t % 2, 0:D], ACT.Tanh, scale=0.5).then_inc(th_done, 1)

            def degrees(half, par):
                b, turn, p = back(half, par, 0)
                act.wait_ge(adj_in[p], 16 * (turn + 1))
                if not (known(b) and b < 2):
                    act.wait_ge(eps1, b - 1)
                if not (known(b) and b < 1):
                    act.wait_ge(deg_done, b)
                for t in range(T):
                    last = act.activation(deg_junk[:, t], adj_sb[:, p, t], ACT.Copy, accum_out=mvd[:, p, t, 2:3])
                last.then_inc(deg_done, 1)

            def gap(half, par):
                b, turn, p = back(half, par, 2)
                act.wait_ge(route, ROUTE * b + R_GAP)
                act.activation(r_exp[:], r_gap[:], ACT.Exp, scale=1.0 / WS).then_inc(gap_exp, 1)

            def elu(half, par):
                b, turn, p = back(half, par, 1)
                act.wait_ge(mix, MIX * b + 11)
                act.activation(mix_e[:], mix_m[:], ACT.Exp).then_inc(elu_exp, 1)

            def body(half, g):
                for par in range(2):
                    b = back(half, par, 0)[0]
                    s0, s1, s2 = (not (known(b) and not 0 <= b - n < NB) for n in range(3))
                    if s1:
                        adj_to_sbuf(half, par, 0)
                        adj_to_sbuf(half, par, 1)
                    if s2:
                        high(half, par)
                    if s1:
                        xn_to_sbuf(half, par)
                        adj_to_sbuf(half, par, 2)
                        adj_to_sbuf(half, par, 3)
                        messages(half, par)
                    if s0:
                        degrees(half, par)
                    if s2:
                        gap(half, par)
                    if s1:
                        elu(half, par)
                    if known(b) and b == 0:
                        act.wait_ge(b1_turned, 1)
                        act.activation(b1[:], ps[:, 7, 0:(E + 1) * FC], ACT.Copy).then_inc(b1_turned, 1)
                        for e in range(E + 1):
                            act.wait_ge(w_in[e % 2], 32 * (e // 2 + 1))
                            act.activation(w1[:, e, 0, :], w_stage[:, e % 2, 0, :], ACT.Copy, scale=WS)
                            act.activation(w2[:, e, 0].rearrange("p c d -> p (c d)"), w_stage[:, e % 2, 1, :], ACT.Copy, scale=WS).then_inc(w_high, 1)

            steps(act, body)

            act.wait_ge(tables, TABLES * GROUPS)
            act.wait_ge(adj_turned, T * NB)

            def gelu(k, q, first):
                e = act.value_load(tab_e[0:1, bass.ds(k, 1)], min_val=0, max_val=E - 1)
                if not first:
                    act.wait_ge(split_done, k - 1)
                for c in range(FC):
                    if c % 2 == 0:
                        act.wait_ge(up_done, 2 * k + c // 2 + 1)
                    last = act.activation(h_sb[:, q, c, 0:BLK], ps[:, 2 * q + c // 2, (c % 2) * BLK:(c % 2 + 1) * BLK], ACT.Gelu,
                                          bias=b1[:, bass.ds(e * FC + c, 1)], scale=1.0 / WS)
                    if c % 2:
                        last.then_inc(h_done, 1)

            def xb_to_sbuf(k, q, first):
                act.wait_ge(rows_turned, k + 1)
                if not first:
                    act.wait_ge(up_done, 2 * (k - 1))
                act.activation(xb[:, q].rearrange("p h s -> p (h s)"), ps[:, 6 + q].bitcast(F16)[:, 0:2 * BLK], ACT.Copy).then_inc(xb_out, 1)

            xb_to_sbuf(0, 0, True)
            xb_to_sbuf(1, 1, True)
            for k in range(2):
                gelu(k, k, True)
                xb_to_sbuf(k + 2, k, False)
            with act.Fori(1, NK // 2 - 1) as half:
                for q in range(2):
                    gelu(2 * half + q, q, False)
                    xb_to_sbuf(2 * half + q + 2, q, False)
            for q in range(2):
                gelu(NK - 2 + q, q, False)

            act.wait_ge(split_done, NK)

            def shared_gelu(b, q, first):
                for c in range(FC):
                    act.wait_ge(sh_up, FC * b + c + 1)
                    if c == 0 and not first:
                        act.wait_ge(sh_split, b - 1)
                    act.activation(h_sb[:, q, c], ps[:, c], ACT.Gelu, bias=b1[:, E * FC + c:E * FC + c + 1],
                                   scale=1.0 / WS).then_inc(sh_h, 1)

            shared_gelu(0, 0, True)
            shared_gelu(1, 1, True)
            with act.Fori(1, NB // 2) as half:
                for q in range(2):
                    shared_gelu(2 * half + q, q, False)

        @block.vector
        def _(dve):
            def normalise(half, par):
                b, turn, p = back(half, par, 1)
                dve.wait_ge(rsq1, b + 1)
                if not (known(b) and b < 1):
                    dve.wait_ge(xn_turned, b)
                for t in range(T):
                    last = dve.tensor_scalar(xn[:, t], xin[:, p, t], mvd[:, p, t, 0:1], rs1[:, p, t, 0:1], ALU.subtract, ALU.mult)
                last.then_inc(xn_done, 1)

            def normalise2(half, par):
                b, turn, p = back(half, par, 2)
                dve.wait_ge(rsq2, b + 1)
                if not (known(b) and b < 1):
                    dve.wait_ge(high_done, b)
                for t in range(T):
                    last = dve.tensor_scalar(xn2[:, t], x2[:, p, t], mv2[:, p, t, 0:1], rs2[:, p, t:t + 1], ALU.subtract, ALU.mult)
                last.then_inc(xn2_done, 1)

            def low(half, par):
                b, turn, p = back(half, par, 2)
                dve.wait_ge(high_done, b + 1)
                dve.tensor_tensor(xr[:, p, :, 1, :], xn2[:], xr[:, p, :, 0, :], ALU.subtract).then_inc(low_done, 1)

            def first_stats(half, par):
                b, turn, p = back(half, par, 0)
                dve.wait_ge(x_in[p], 16 * (turn + 1))
                for t in range(T):
                    last = dve.bn_stats(stats[:, t], xin[:, p, t])
                last.then_inc(stats1, 1)

            def first_stats_ready(half, par):
                b = back(half, par, 0)[0]
                dve.wait_ge(stats1, 2 * b + 1)
                if not (known(b) and b < 2):
                    dve.wait_ge(eps1, b - 1)

            def first_variances(half, par):
                b, turn, p = back(half, par, 0)
                for t in range(T):
                    last = dve.bn_aggr(mvd[:, p, t, 0:2], stats[:, t])
                last.then_inc(stats1, 1)

            def xc_to_sbuf(half, par):
                b, turn, p = back(half, par, 2)
                dve.wait_ge(xc_turned, b + 1)
                if not (known(b) and b < 2):
                    dve.wait_ge(xc_saved[p], 16 * turn)
                dve.tensor_copy(xc[:, p].rearrange("p h s -> p (h s)"), ps[:, 6].bitcast(F16)).then_inc(xc_out, 1)

            def gates(half, par):
                b, turn, p = back(half, par, 1)
                for t in range(T):
                    dve.wait_ge(th_done, T * b + t + 1)
                    dve.scalar_tensor_tensor(out=het[:, t], in0=th[:, t], scalar=1.0, in1=ps[:, 3 + t % 2, D:2 * D],
                                             op0=ALU.subtract, op1=ALU.mult).then_inc(mix, 1)
                dve.tensor_scalar(gate[:], th[:], 0.5, 0.5, ALU.mult, ALU.add).then_inc(mix, 1)

            def combine(half, par):
                b, turn, p = back(half, par, 1)
                m = MIX * b
                dve.wait_ge(hom_done, b + 1)
                dve.wait_ge(mix, m + 5)
                for t in range(T):
                    dve.scalar_tensor_tensor(out=mix_o[:, t], in0=ps[:, 5, t * D:(t + 1) * D], scalar=rs1[:, p, t, 1:2],
                                             in1=gate[:, t], op0=ALU.mult, op1=ALU.mult).then_inc(mix, 1)
                dve.wait_ge(mix, m + 9)
                dve.scalar_tensor_tensor(out=mix_o[:], in0=het[:], scalar=-0.5, in1=mix_o[:], op0=ALU.mult, op1=ALU.add).then_inc(mix, 1)
                dve.wait_ge(mix, m + 10)
                dve.tensor_scalar(mix_m[:], mix_o[:], 0.0, None, ALU.min).then_inc(mix, 1)
                dve.wait_ge(elu_exp, b + 1)
                dve.scalar_tensor_tensor(out=mix_o[:], in0=mix_e[:], scalar=-1.0, in1=mix_o[:], op0=ALU.add, op1=ALU.max).then_inc(mix, 1)
                dve.wait_ge(mix, m + 12)
                if not (known(b) and b < 2):
                    dve.wait_ge(x2_saved[p], 16 * turn)
                dve.tensor_tensor(x2[:, p], xin[:, p], mix_o[:], ALU.add).then_inc(mix, 1)
                dve.wait_ge(mix, m + 13)
                for t in range(T):
                    last = dve.bn_stats(stats2[:, t], x2[:, p, t])
                last.then_inc(mix, 1)
                dve.wait_ge(mix, m + 14)
                if not (known(b) and b < 2):
                    dve.wait_ge(eps2, b - 1)

            def second_variances(half, par):
                b, turn, p = back(half, par, 1)
                for t in range(T):
                    last = dve.bn_aggr(mv2[:, p, t], stats2[:, t])
                last.then_inc(mix, 1)

            def route_top(half, par, g):
                b, turn, p = back(half, par, 2)
                r = ROUTE * b
                lg = ps[:, 7, 0:T * E].rearrange("p (t e) -> p t e", e=E)
                hot = [kp[:, p, k * T * E:(k + 1) * T * E].rearrange("p (t e) -> p t e", e=E) for k in range(2)]
                dve.wait_ge(logits_done, b + 1)
                if not (known(b) and b < 2):
                    dve.wait_ge(keep_saved[p], 16 * turn)
                dve.tensor_reduce(r_top[:, 0], lg, AX.X, ALU.max).then_inc(route, 1)
                dve.wait_ge(route, r + 1)
                dve.tensor_tensor(r_ne[:], lg, r_top[:, 0].unsqueeze(2).to_broadcast([P, T, E]), ALU.is_lt).then_inc(route, 1)
                dve.wait_ge(route, r + 2)
                dve.scalar_tensor_tensor(out=r_cand[:], in0=r_ne[:], scalar=64.0, in1=iota_e[:], op0=ALU.mult, op1=ALU.add).then_inc(route, 1)
                dve.wait_ge(route, r + 3)
                dve.tensor_reduce(r_idx[:], r_cand[:], AX.X, ALU.min).then_inc(route, 1)
                dve.wait_ge(route, r + 4)
                dve.tensor_tensor(hot[0], iota_e[:], r_idx[:].unsqueeze(2).to_broadcast([P, T, E]), ALU.is_equal).then_inc(route, 1)
                dve.wait_ge(route, r + 5)
                dve.scalar_tensor_tensor(out=r_l2[:], in0=hot[0], scalar=-BIG, in1=lg, op0=ALU.mult, op1=ALU.add).then_inc(route, 1)
                dve.wait_ge(route, r + 6)
                dve.tensor_reduce(r_top[:, 1], r_l2[:], AX.X, ALU.max).then_inc(route, 1)
                dve.wait_ge(route, r + 7)
                dve.tensor_tensor(r_ne[:], r_l2[:], r_top[:, 1].unsqueeze(2).to_broadcast([P, T, E]), ALU.is_lt).then_inc(route, 1)
                dve.wait_ge(route, r + 8)
                dve.scalar_tensor_tensor(out=r_cand[:], in0=r_ne[:], scalar=64.0, in1=iota_e[:], op0=ALU.mult, op1=ALU.add).then_inc(route, 1)
                dve.wait_ge(route, r + 9)
                dve.tensor_reduce(r_idx[:], r_cand[:], AX.X, ALU.min).then_inc(route, 1)
                dve.wait_ge(route, r + 10)
                dve.tensor_tensor(hot[1], iota_e[:], r_idx[:].unsqueeze(2).to_broadcast([P, T, E]), ALU.is_equal).then_inc(route, 1)
                dve.wait_ge(route, r + 11)
                dve.tensor_tensor(r_mask[:, p], hot[0], hot[1], ALU.add).then_inc(route, 1)
                dve.tensor_tensor(r_gap[:], r_top[:, 1], r_top[:, 0], ALU.subtract).then_inc(route, 1)
                dve.wait_ge(route, r + 12)
                dve.tensor_reduce(r_red[:], r_mask[:, p].rearrange("p t e -> p e t"), AX.X, ALU.add).then_inc(route, 1)
                dve.wait_ge(route, r + 14)
                dve.tensor_tensor(prefix[g][:, 1 - p], prefix[g][:, p], r_red[:], ALU.add).then_inc(route, 1)

            def gate_sum(half, par):
                b = back(half, par, 2)[0]
                dve.wait_ge(gap_exp, b + 1)
                dve.tensor_scalar(r_sum[:], r_exp[:], 1.0, WS, ALU.add, ALU.mult).then_inc(route, 1)

            def route_rows(half, par, g):
                b, turn, p = back(half, par, 2)
                r = ROUTE * b
                hot2 = kp[:, p, 0:2 * T * E].rearrange("p (k j) -> p k j", k=2)
                pos, w = kp[:, p, 64:72], kp[:, p, 72:80]
                dve.wait_ge(route, r + 16)
                dve.reciprocal(w[:, 0:T], r_sum[:]).then_inc(route, 1)
                dve.wait_ge(rank_done, b + 1)
                dve.tensor_tensor(r_pos[:], ps[:, 7, 64:64 + T * E].rearrange("p (t e) -> p t e", e=E),
                                  reg_base[g][:].unsqueeze(1).to_broadcast([P, T, E]), ALU.add).then_inc(route, 1)
                dve.wait_ge(route, r + 17)
                dve.tensor_tensor(w[:, T:2 * T], w[:, 0:T], r_exp[:], ALU.mult).then_inc(route, 1)
                dve.wait_ge(route, r + 18)
                dve.tensor_tensor(r_prod[:].rearrange("p (k t) e -> p k (t e)", k=2), hot2,
                                  r_pos[:].rearrange("p t e -> p (t e)").unsqueeze(1).to_broadcast([P, 2, T * E]), ALU.mult).then_inc(route, 1)
                dve.wait_ge(route, r + 20)
                dve.tensor_reduce(pos, r_prod[:], AX.X, ALU.add).then_inc(route, 1)
                dve.wait_ge(route, r + 21)
                if not (known(b) and b < 2):
                    dve.wait_ge(scattered[p], 16 * 2 * T * turn)
                dve.tensor_copy(idx[:, p], pos).then_inc(route, 1)

            def body(half, g):
                for par in range(2):
                    b = back(half, par, 0)[0]
                    s0, s1, s2 = (not (known(b) and not 0 <= b - n < NB) for n in range(3))
                    g3 = (b - 2) // BG if known(b) and s2 else g
                    if s1:
                        normalise(half, par)
                    if s2:
                        normalise2(half, par)
                    if s0:
                        first_stats(half, par)
                        first_stats_ready(half, par)
                    if s2:
                        low(half, par)
                    if s0:
                        first_variances(half, par)
                    if s2:
                        xc_to_sbuf(half, par)
                    if s1:
                        gates(half, par)
                    if s2:
                        route_top(half, par, g3)
                    if s1:
                        combine(half, par)
                    if s2:
                        gate_sum(half, par)
                    if s1:
                        second_variances(half, par)
                    if s2:
                        route_rows(half, par, g3)
                    if known(b) and b == 0:
                        cut_weights()

            def cut_weights():
                dve.wait_ge(const_in, 16 * 5)
                dve.wait_ge(bias_in, 16 * 4)
                dve.tensor_scalar(wr16[:, 0], wr_f[:], WS, None, ALU.mult).then_inc(setup_v, 1)
                dve.tensor_tensor(b2[:], b2[:], b2s_bc[:].unsqueeze(1).to_broadcast([P, E, D]), ALU.add).then_inc(setup_v, 1)
                dve.wait_ge(setup_v, 1)
                dve.scalar_tensor_tensor(out=wr16[:, 1], in0=wr_f[:], scalar=WS, in1=wr16[:, 0], op0=ALU.mult, op1=ALU.subtract).then_inc(setup_v, 1)
                dve.wait_ge(setup_v, 3)
                dve.tensor_scalar(b2[:], b2[:], WS, None, ALU.mult).then_inc(setup_v, 1)
                for e in range(E + 1):
                    dve.wait_ge(w_high, e + 1)
                    dve.scalar_tensor_tensor(out=w1[:, e, 1, :], in0=w_stage[:, e % 2, 0, :], scalar=WS, in1=w1[:, e, 0, :],
                                             op0=ALU.mult, op1=ALU.subtract)
                    dve.scalar_tensor_tensor(out=w2[:, e, 1].rearrange("p c d -> p (c d)"), in0=w_stage[:, e % 2, 1, :], scalar=WS,
                                             in1=w2[:, e, 0].rearrange("p c d -> p (c d)"), op0=ALU.mult, op1=ALU.subtract).then_inc(w_low, 1)

            steps(dve, body)

            def make_tables(g):
                m = TABLES * g
                own = [g * NBLK, (g + 1) * NBLK]
                dve.wait_ge(count_done, 1)
                dve.tensor_copy(t_cnt[:], ps[:, 7, 128 + g * E:128 + (g + 1) * E]).then_inc(tables, 1)
                dve.wait_ge(tables, m + 1)
                dve.tensor_tensor(t_cmp[:], cap_iota[:].unsqueeze(1).to_broadcast([P, E, MAXB]),
                                  t_cnt[:].unsqueeze(2).to_broadcast([P, E, MAXB]), ALU.is_lt).then_inc(tables, 1)
                dve.tensor_tensor(tab_pad[:, g * E:(g + 1) * E], t_cnt[:], reg_base[g][:], ALU.add).then_inc(tables, 1)
                dve.wait_ge(tables, m + 2)
                dve.tensor_reduce(t_nblk[:], t_cmp[:], AX.X, ALU.add).then_inc(tables, 1)
                dve.wait_ge(tables, m + 4)
                dve.tensor_tensor(t_low[:], lower[:], t_nblk[:].unsqueeze(1).to_broadcast([P, E, E]), ALU.mult).then_inc(tables, 1)
                dve.wait_ge(tables, m + 5)
                dve.tensor_reduce(t_start[:], t_low[:], AX.X, ALU.add).then_inc(tables, 1)
                dve.wait_ge(tables, m + 6)
                dve.tensor_tensor(t_end[:], t_start[:], t_nblk[:], ALU.add).then_inc(tables, 1)
                dve.scalar_tensor_tensor(out=t_delta[:], in0=t_start[:], scalar=float(BLK), in1=reg_base[g][:], op0=ALU.mult, op1=ALU.subtract).then_inc(tables, 1)
                dve.wait_ge(tables, m + 8)
                dve.tensor_tensor(t_past[:], t_end[:].unsqueeze(1).to_broadcast([P, NBLK, E]),
                                  blk_iota[:].unsqueeze(2).to_broadcast([P, NBLK, E]), ALU.is_le)
                last = dve.tensor_tensor(y_prod[:].rearrange("p (b k) e -> p b k e", b=BG),
                                         keep[:, g * BG:(g + 1) * BG, 0:2 * T * E].rearrange("p b (k e) -> p b k e", e=E),
                                         t_delta[:].unsqueeze(1).unsqueeze(1).to_broadcast([P, BG, 2 * T, E]), ALU.mult)
                last.then_inc(tables, 1)
                dve.wait_ge(tables, m + 9)
                dve.tensor_reduce(t_eraw[:], t_past[:], AX.X, ALU.add)
                dve.tensor_reduce(y_off[:], y_prod[:], AX.X, ALU.add).then_inc(tables, 1)
                dve.wait_ge(tables, m + 10)
                dve.tensor_scalar(t_used[:], t_eraw[:], float(E), None, ALU.is_lt)
                dve.tensor_scalar(tab_e[:, own[0]:own[1]], t_eraw[:], float(E - 1), None, ALU.min)
                dve.tensor_tensor(y_idx[:, g].rearrange("p (b k) -> p b k", b=BG), y_off[:].rearrange("p (b k) -> p b k", b=BG),
                                  keep[:, g * BG:(g + 1) * BG, 64:72], ALU.add)
                dve.tensor_tensor(t_past[:], t_eraw[:].unsqueeze(2).to_broadcast([P, NBLK, E]),
                                  iota_e[:, 0, :].unsqueeze(1).to_broadcast([P, NBLK, E]), ALU.is_equal)
                dve.tensor_scalar(t_row[:], blk_iota[:], float(BLK), float(-PADROW), ALU.mult, ALU.add).then_inc(tables, 1)
                dve.wait_ge(tables, m + 11)
                dve.tensor_tensor(t_past[:], t_past[:], t_delta[:].unsqueeze(1).to_broadcast([P, NBLK, E]), ALU.mult)
                dve.tensor_tensor(t_row[:], t_row[:], t_used[:], ALU.mult).then_inc(tables, 1)
                dve.wait_ge(tables, m + 12)
                dve.tensor_reduce(t_off[:], t_past[:], AX.X, ALU.add).then_inc(tables, 1)
                dve.wait_ge(tables, m + 13)
                dve.scalar_tensor_tensor(out=tab_row[:, own[0]:own[1]], in0=t_row[:], scalar=float(PADROW), in1=t_off[:],
                                         op0=ALU.add, op1=ALU.subtract).then_inc(tables, 1)

            for q in range(2):
                dve.wait_ge(keep_saved[q], 16 * NB // 2)
            for g in range(GROUPS):
                make_tables(g)

            def split(k, q, first):
                dve.wait_ge(h_done, 2 * (k + 1))
                if not first:
                    dve.wait_ge(down_done, k - 1)
                dve.tensor_copy(h_hi[:, q, :, 0:BLK], h_sb[:, q, :, 0:BLK]).then_inc(split_hi, 1)
                dve.wait_ge(split_hi, k + 1)
                dve.tensor_tensor(h_lo[:, q, :, 0:BLK], h_sb[:, q, :, 0:BLK], h_hi[:, q, :, 0:BLK], ALU.subtract).then_inc(split_done, 1)

            def y_to_sbuf(k, turn, q, first):
                e = dve.value_load(tab_e[0:1, bass.ds(k, 1)], min_val=0, max_val=E - 1)
                dve.wait_ge(down_done, k + 1)
                if not first:
                    dve.wait_ge(y_saved[q], 16 * turn)
                dve.tensor_tensor(y_sb[:, q], ps[:, 4 + q, 0:2 * D].rearrange("p (s d) -> p s d", d=D),
                                  b2[:, bass.ds(e, 1), :].to_broadcast([P, 2, D]), ALU.add).then_inc(y_done, 1)

            split(0, 0, True)
            split(1, 1, True)
            y_to_sbuf(0, 0, 0, True)
            split(2, 0, False)
            y_to_sbuf(1, 0, 1, True)
            split(3, 1, False)
            y_to_sbuf(2, 1, 0, False)
            with dve.Fori(2, NK // 2) as half:
                split(2 * half, 0, False)
                y_to_sbuf(2 * half - 1, half - 1, 1, False)
                split(2 * half + 1, 1, False)
                y_to_sbuf(2 * half, half, 0, False)
            y_to_sbuf(NK - 1, NK // 2 - 1, 1, False)

            def shared_split(b, q, first):
                dve.wait_ge(sh_h, FC * (b + 1))
                if not first:
                    dve.wait_ge(sh_down, b - 1)
                dve.tensor_copy(h_hi[:, q], h_sb[:, q]).then_inc(sh_hi, 1)
                dve.wait_ge(sh_hi, b + 1)
                dve.tensor_tensor(h_lo[:, q], h_sb[:, q], h_hi[:, q], ALU.subtract).then_inc(sh_split, 1)

            def add_up(b, turn, r, rturn):
                q = r % 2
                dve.tensor_copy(wb[:, q], keep[:, bass.ds(b, 1), 72:80]).then_inc(wb_done, 1)
                dve.wait_ge(sh_down, b + 1)
                if not (known(b) and b < 2):
                    dve.wait_ge(out_saved[q], 16 * turn)
                dve.scalar_tensor_tensor(out=acc[:, q], in0=ps[:, 4 + q], scalar=1.0 / WS, in1=x2_all[:, bass.ds(b, 1), :],
                                         op0=ALU.mult, op1=ALU.add).then_inc(sh_acc, 1)
                dve.wait_ge(wb_done, b + 1)
                dve.wait_ge(gathered[r], 16 * 2 * T * (rturn + 1))
                for k in range(2):
                    dve.wait_ge(sh_acc, 9 * b + 1 + k * T)
                    for t in range(T):
                        a = acc[:, q, t * D:(t + 1) * D]
                        dve.scalar_tensor_tensor(out=a, in0=yg[:, r, k * T + t], scalar=wb[:, q, k * T + t:k * T + t + 1], in1=a,
                                                 op0=ALU.mult, op1=ALU.add).then_inc(sh_acc, 1)

            for q in range(2):
                dve.wait_ge(x2_saved[q], 16 * NB // 2)
            dve.wait_ge(down_done, NK)
            shared_split(0, 0, True)
            shared_split(1, 1, True)
            add_up(0, 0, 0, 0)
            shared_split(2, 0, False)
            add_up(1, 0, 1, 0)
            shared_split(3, 1, False)
            add_up(2, 1, 2, 0)
            shared_split(4, 0, False)
            add_up(3, 1, 3, 0)
            with dve.Fori(1, NB // RING - 1) as ring:
                for r in range(RING):
                    b = RING * ring + r
                    shared_split(b + 1, (r + 1) % 2, False)
                    add_up(b, 2 * ring + r // 2, r, ring)
            for r in range(RING):
                b = NB - RING + r
                if b + 1 < NB:
                    shared_split(b + 1, (r + 1) % 2, False)
                add_up(b, b // 2, r, NB // RING - 1)

        @block.tensor
        def _(pe):
            def turn_adj(half, par, j):
                b, turn, p = back(half, par, 1)
                if j == 0:
                    pe.wait_ge(adj_in[p], 16 * (turn + 1))
                if not (known(b) and b == 0 and j < 2):
                    pe.wait_ge(adj_out, T * b + j - 1)
                for t in range(T):
                    last = pe.transpose(ps[:, j % 2, t * P:(t + 1) * P], adj_sb[:, p, t, j * P:(j + 1) * P], ident[:])
                last.then_inc(adj_turned, 1)

            def turn_xn(half, par):
                b, turn, p = back(half, par, 1)
                pe.wait_ge(xn_done, b + 1)
                if not (known(b) and b == 0):
                    pe.wait_ge(xn_out, b)
                for t in range(T):
                    last = pe.transpose(ps[:, 2, t * P:(t + 1) * P], xn[:, t], ident[:])
                last.then_inc(xn_turned, 1)

            def turn_xc(half, par):
                b, turn, p = back(half, par, 2)
                pe.wait_ge(low_done, b + 1)
                if not (known(b) and b == 0):
                    pe.wait_ge(xc_out, b)
                for h in range(2):
                    for t in range(T):
                        last = pe.transpose(ps[:, 6].bitcast(F16)[:, h * S + t * P:h * S + (t + 1) * P], xr[:, p, t, h], ident16[:])
                last.then_inc(xc_turned, 1)

            def project(half, par):
                b, turn, p = back(half, par, 1)
                pe.wait_ge(xn_out, b + 1)
                for t in range(T):
                    if not (known(b) and b == 0 and t < 2):
                        tb, tt = (b, t - 2) if t >= 2 else (b - 1, t + 2)
                        pe.wait_ge(mix, MIX * tb + tt + 1)
                    lhs = xn_t[:, t * P:(t + 1) * P]
                    pe.matmul(ps[:, 3 + t % 2, 0:3 * D], lhs, w_gnn[:], start=True, stop=False)
                    pe.matmul(ps[:, 3 + t % 2, 0:D], ones_row[:], bt_row[:], start=False, stop=True).then_inc(proj_done, 1)

            def logits(half, par):
                b, turn, p = back(half, par, 2)
                pe.wait_ge(xc_out, b + 1)
                if known(b) and b == 0:
                    pe.wait_ge(setup_v, 3)
                    pe.wait_ge(b1_turned, 2)
                else:
                    pe.wait_ge(route, ROUTE * (b - 1) + 18)
                for t in range(T):
                    o = ps[:, 7, t * E:(t + 1) * E]
                    hi, lo = (xc[:, p, h, t * P:(t + 1) * P] for h in range(2))
                    pe.matmul(o, hi, wr16[:, 0], start=True, stop=False)
                    pe.matmul(o, hi, wr16[:, 1], start=False, stop=False)
                    last = pe.matmul(o, lo, wr16[:, 0], start=False, stop=True)
                last.then_inc(logits_done, 1)

            def homophily(half, par):
                b, turn, p = back(half, par, 1)
                pe.wait_ge(adj_out, T * (b + 1))
                pe.wait_ge(th_done, T * (b + 1))
                if not (known(b) and b == 0):
                    pe.wait_ge(mix, MIX * (b - 1) + MIX_HOM)
                for t in range(T):
                    for j in range(T):
                        last = pe.matmul(ps[:, 5, t * D:(t + 1) * D], adj_t[:, j, t * P:(t + 1) * P], f_sb[:, j],
                                         start=(j == 0), stop=(j == T - 1))
                last.then_inc(hom_done, 1)

            def rank(half, par, g):
                b, turn, p = back(half, par, 2)
                pe.wait_ge(route, ROUTE * b + R_MASK)
                def o(t):
                    return ps[:, 7, 64 + t * E:64 + T * E]
                pe.matmul(o(0), before[:], r_mask[:, p].rearrange("p t e -> p (t e)"), start=True, stop=False)
                for t in range(T - 1):
                    for u in range(t + 1, T):
                        pe.matmul(ps[:, 7, 64 + u * E:64 + (u + 1) * E], ones16[:], r_mask[:, p, t], start=False, stop=False)
                for u in range(T):
                    last = pe.matmul(ps[:, 7, 64 + u * E:64 + (u + 1) * E], ones16[:], prefix[g][:, p], start=False, stop=(u == T - 1))
                last.then_inc(rank_done, 1)

            def body(half, g):
                for par in range(2):
                    b = back(half, par, 0)[0]
                    s0, s1, s2 = (not (known(b) and not 0 <= b - n < NB) for n in range(3))
                    g3 = (b - 2) // BG if known(b) and s2 else g
                    if s1:
                        turn_adj(half, par, 0)
                        turn_adj(half, par, 1)
                        turn_xn(half, par)
                    if s2:
                        turn_xc(half, par)
                    if s1:
                        turn_adj(half, par, 2)
                        turn_adj(half, par, 3)
                        project(half, par)
                    if s2:
                        logits(half, par)
                    if s1:
                        homophily(half, par)
                    if s2:
                        rank(half, par, g3)

            pe.wait_ge(const_made, 13)
            pe.wait_ge(const_in, 16 * 5)
            pe.wait_ge(bias_in, 16 * 4)
            pe.transpose(ps[:, 7, 0:P], b1_rows[:], ident[:]).then_inc(b1_turned, 1)
            steps(pe, body)

            pe.wait_ge(route, ROUTE * NB)
            for g in range(GROUPS):
                last = pe.matmul(ps[:, 7, 128 + g * E:128 + (g + 1) * E], ones16[:], prefix[g][:, 0], start=True, stop=True)
            last.then_inc(count_done, 1)

            pe.wait_ge(tables, TABLES * GROUPS)
            pe.wait_ge(w_low, E + 1)

            def expert(k):
                return pe.value_load(tab_e[0:1, bass.ds(k, 1)], min_val=0, max_val=E - 1)

            def turn_rows(k, turn, q, first):
                pe.wait_ge(rows_in[q], 16 * (turn + 1))
                if not first:
                    pe.wait_ge(xb_out, k - 1)
                for h in range(2):
                    for t in range(BLK // P):
                        last = pe.transpose(ps[:, 6 + q].bitcast(F16)[:, h * BLK + t * P:h * BLK + (t + 1) * P],
                                            rows_sb[:, q, t, h * D:(h + 1) * D], ident16[:])
                last.then_inc(rows_turned, 1)

            def up(e, k, q, first):
                pe.wait_ge(xb_out, k + 1)
                if not first:
                    pe.wait_ge(h_done, 2 * (k - 1))
                for c in range(FC):
                    o = ps[:, 2 * q + c // 2, (c % 2) * BLK:(c % 2 + 1) * BLK]
                    hi, lo = (w1[:, bass.ds(e, 1), h, c * P:(c + 1) * P].rearrange("p a f -> p (a f)") for h in range(2))
                    pe.matmul(o, hi, xb[:, q, 0], start=True, stop=False)
                    pe.matmul(o, hi, xb[:, q, 1], start=False, stop=False)
                    last = pe.matmul(o, lo, xb[:, q, 0], start=False, stop=True)
                    if c % 2:
                        last.then_inc(up_done, 1)

            def down(e, k, q, first):
                pe.wait_ge(split_done, k + 1)
                if not first:
                    pe.wait_ge(y_done, k - 1)
                hi, lo = (w2[:, bass.ds(e, 1), h].rearrange("p a c d -> p (a c) d") for h in range(2))
                for s in range(BLK // P):
                    o = ps[:, 4 + q, s * D:(s + 1) * D]
                    for c in range(FC):
                        hh, hl = h_hi[:, q, c, s * P:(s + 1) * P], h_lo[:, q, c, s * P:(s + 1) * P]
                        pe.matmul(o, hh, hi[:, c], start=(c == 0), stop=False)
                        pe.matmul(o, hh, lo[:, c], start=False, stop=False)
                        last = pe.matmul(o, hl, hi[:, c], start=False, stop=(c == FC - 1))
                last.then_inc(down_done, 1)

            turn_rows(0, 0, 0, True)
            turn_rows(1, 0, 1, True)
            for k in range(2):
                up(expert(k), k, k, True)
                turn_rows(k + 2, 1, k, False)
            for k in range(2):
                up(expert(k + 2), k + 2, k, False)
                turn_rows(k + 4, 2, k, False)
                down(expert(k), k, k, True)
            with pe.Fori(1, NK // 2 - 2) as half:
                for q in range(2):
                    k = 2 * half + q
                    up(expert(k + 2), k + 2, q, False)
                    turn_rows(k + 4, half + 2, q, False)
                    down(expert(k), k, q, False)
            for k in range(NK - 4, NK):
                if k + 2 < NK:
                    up(expert(k + 2), k + 2, k % 2, False)
                down(expert(k), k, k % 2, False)

            pe.wait_ge(h_done, 2 * NK)
            pe.wait_ge(y_done, NK)

            def shared_up(b, turn, q, first):
                pe.wait_ge(xcb_in[q], 16 * (turn + 1))
                for c in range(FC):
                    if not first:
                        pe.wait_ge(sh_h, FC * (b - 1) + c + 1)
                    hi, lo = (w1[:, E, h, c * P:(c + 1) * P] for h in range(2))
                    pe.matmul(ps[:, c], hi, xcb[:, q, 0], start=True, stop=False)
                    pe.matmul(ps[:, c], hi, xcb[:, q, 1], start=False, stop=False)
                    pe.matmul(ps[:, c], lo, xcb[:, q, 0], start=False, stop=True).then_inc(sh_up, 1)

            def shared_down(b, q, first):
                pe.wait_ge(sh_split, b + 1)
                if not first:
                    pe.wait_ge(sh_acc, 9 * (b - 2) + 1)
                for t in range(T):
                    o = ps[:, 4 + q, t * D:(t + 1) * D]
                    for c in range(FC):
                        hh, hl = h_hi[:, q, c, t * P:(t + 1) * P], h_lo[:, q, c, t * P:(t + 1) * P]
                        pe.matmul(o, hh, w2[:, E, 0, c], start=(c == 0), stop=False)
                        pe.matmul(o, hh, w2[:, E, 1, c], start=False, stop=False)
                        last = pe.matmul(o, hl, w2[:, E, 0, c], start=False, stop=(c == FC - 1))
                last.then_inc(sh_down, 1)

            shared_up(0, 0, 0, True)
            shared_up(1, 0, 1, False)
            shared_down(0, 0, True)
            shared_up(2, 1, 0, False)
            shared_down(1, 1, True)
            with pe.Fori(1, NB // 2 - 1) as half:
                shared_up(2 * half + 1, half, 1, False)
                shared_down(2 * half, 0, False)
                shared_up(2 * half + 2, half + 1, 0, False)
                shared_down(2 * half + 1, 1, False)
            shared_up(NB - 1, NB // 2 - 1, 1, False)
            shared_down(NB - 2, 0, False)
            shared_down(NB - 1, 1, False)


_INS = ['x', 'adj', 'L0_gnn_W_t', 'L0_gnn_b_t', 'L0_gnn_W_h', 'L0_gnn_theta', 'L0_ffn_Wr', 'L0_ffn_W1s', 'L0_ffn_b1s',
        'L0_ffn_W2s', 'L0_ffn_b2s', 'L0_ffn_W1p', 'L0_ffn_b1p', 'L0_ffn_W2p', 'L0_ffn_b2p']
_OUTS = [((16, 512, 128), 'float32')]


def kernel(**inputs):
    import numpy as _np
    import concourse.bacc as _bacc
    from concourse import mybir as _mybir
    from concourse.bass_utils import run_bass_kernel_spmd as _run

    nc = _bacc.Bacc("TRN2", target_bir_lowering=False, num_devices=1)
    arrays, args = {}, []
    for name in _INS:
        a = _np.ascontiguousarray(inputs[name])
        arrays[f"in_{name}_dram"] = a
        args.append(nc.dram_tensor(f"in_{name}_dram", a.shape, _mybir.dt.from_np(a.dtype), kind="ExternalInput").ap())
    for i, (shape, dtype) in enumerate(_OUTS):
        dt = _mybir.dt.from_np(_np.dtype(dtype))
        args.append(nc.dram_tensor(f"out_{i}_dram", shape, dt, kind="ExternalOutput").ap())
    build(nc, *args)
    r = _run(nc, [arrays], core_ids=[0])
    got = tuple(r.results[0][f"out_{i}_dram"] for i in range(len(_OUTS)))
    return got[0]
```

```python
from contextlib import ExitStack

import concourse.bass as bass
from concourse import mybir

ALU = mybir.AluOpType
ACT = mybir.ActivationFunctionType
AX = mybir.AxisListType
F32 = mybir.dt.float32
F16 = mybir.dt.float16
I32 = mybir.dt.int32

P = 128
WS = 64.0
BLK = 256
GROUPS = 2
RING = 8
AHEAD = 6
XRING = 4
EARLY = 4
BIG = 1.0e30
LN_EPS, DEG_EPS = 1e-5, 1e-6
HET = 5
MIX_HOM, MIX_OUT, MIX_ELU, MIX_X2, MIX_STATS, MIX = 4, 5, 6, 7, 8, 9
R_MASK, R_GAP, R_RANK_READ, R_IDX, ROUTE = 12, 13, 16, 20, 22


def build(nc, x, adj, W_t, b_t, W_h, theta, Wr, W1s, b1s, W2s, b2s, W1p, b1p, W2p, b2p, out):
    NB, S, D = x.shape
    T = S // P
    F = W1s.shape[1]
    FC = F // P
    E = Wr.shape[1]
    assert D == P and S == 512 and F == 512 and E == 8 and NB % RING == 0 and NB % (2 * GROUPS) == 0
    BG = NB // GROUPS
    GT = BG * S
    REG = NB * S + BLK
    NBLK = (2 * GT - E) // BLK + E
    NBLK += NBLK % 2
    assert EARLY == XRING == BG // 2
    NK = GROUPS * NBLK
    PADROW = E * REG
    MAXB = GT // BLK

    rows = nc.dram_tensor("expert_rows", (PADROW + BLK, 2 * D), F16, kind="Internal").ap()
    ys = [nc.dram_tensor(f"expert_out{g}", (NBLK * BLK, D), F32, kind="Internal").ap() for g in range(GROUPS)]
    xc_dram = nc.dram_tensor("xn2_t", (NB * P, 2 * S), F16, kind="Internal").ap()

    with ExitStack() as ctx:
        def sb(name, shape, dt=F32):
            return ctx.enter_context(nc.sbuf_tensor(name, shape, dt))

        def sem(name):
            return ctx.enter_context(nc.semaphore(name))

        def sem2(name):
            return [sem(name + "_even"), sem(name + "_odd")]

        ps = ctx.enter_context(nc.psum_tensor("ps", [P, 8, 512], F32))

        ident = sb("ident", [P, P])
        ident16 = sb("ident16", [P, P], F16)
        before = sb("before", [P, P], F16)
        ones16 = sb("ones16", [P, P], F16)
        ones_row = sb("ones_row", [1, P])
        zeros16 = sb("zeros16", [P, 2, 2 * D], F16)
        eps = sb("eps", [P, T, 2])
        mhalf = sb("mhalf", [P, T, 2])
        iota_e = sb("iota_e", [P, T, E])
        blk_iota = sb("blk_iota", [P, NBLK])
        cap_iota = sb("cap_iota", [P, MAXB])
        lower = sb("lower", [P, E, E])
        reg_base = sb("reg_base", [P, E])
        w_gnn = sb("w_gnn", [P, 3 * D])
        bt_row = sb("bt_row", [1, D])
        wr_f = sb("wr_f", [P, E])
        wr16 = sb("wr16", [P, 2, E], F16)
        w_stage = sb("w_stage", [P, 2, 2, 512])
        w1 = sb("w1", [P, E + 1, 2, F], F16)
        w2 = sb("w2", [P, E + 1, FC, 2, D], F16)
        b1_rows = sb("b1_rows", [P, P])
        b1 = sb("b1", [P, (E + 1) * FC])
        b2 = sb("b2", [P, E, D])
        b2s_bc = sb("b2s_bc", [P, D])

        work = sb("work", [P, 18 * T * D])
        xin = work[:, 0:1024].rearrange("p (a t d) -> p a t d", a=2, d=D)
        x2 = work[:, 1024:2048].rearrange("p (a t d) -> p a t d", a=2, d=D)
        adj_t = work[:, 2048:4096].rearrange("p (t s) -> p t s", t=T)
        xn, f_sb, th, gate, het, mix_o, mix_m, mix_e, xn2 = (
            work[:, (8 + i) * T * D:(9 + i) * T * D].rearrange("p (t d) -> p t d", d=D) for i in range(9))
        xn_t = work[:, 17 * T * D:18 * T * D]
        adj_sb = sb("adj_sb", [P, 2, T, S])
        stats = sb("stats", [P, T, 6])
        mvd = sb("mvd", [P, 2, T, 3])
        pw1 = sb("pw1", [P, T, 2])
        rs1 = sb("rs1", [P, 2, T, 2])
        stats2 = sb("stats2", [P, T, 6])
        mv2 = sb("mv2", [P, 2, T, 2])
        pw2 = sb("pw2", [P, T])
        rs2 = sb("rs2", [P, 2, T])
        xr = sb("xr", [P, 2, T, 2, D], F16)
        xc = sb("xc", [P, 2, 2, S], F16)
        r_top = sb("r_top", [P, 2, T])
        r_ne = sb("r_ne", [P, T, E])
        r_cand = sb("r_cand", [P, T, E])
        r_idx = sb("r_idx", [P, T])
        r_l2 = sb("r_l2", [P, T, E])
        r_mask = sb("r_mask", [P, 2, T, E], F16)
        r_red = sb("r_red", [P, E])
        prefix = sb("prefix", [P, 2, E], F16)
        r_gap = sb("r_gap", [P, T])
        r_exp = sb("r_exp", [P, T])
        r_sum = sb("r_sum", [P, T])
        r_pos = sb("r_pos", [P, T, E])
        r_prod = sb("r_prod", [P, 2 * T, E])
        kp = sb("kp", [P, 2, 80])
        idx = sb("idx", [P, 2, 2 * T], I32)
        keep = sb("keep", [P, NB, 80])
        x2_all = sb("x2_all", [P, NB, T * D])

        t_sum = sb("t_sum", [P, GROUPS, E])
        t_own = sb("t_own", [P, GROUPS, E], F16)
        t_cnt = sb("t_cnt", [P, GROUPS, E])
        t_first = sb("t_first", [P, GROUPS + 1, E])
        t_cmp = sb("t_cmp", [P, E, MAXB])
        t_nblk = sb("t_nblk", [P, E])
        t_low = sb("t_low", [P, E, E])
        t_start = sb("t_start", [P, E])
        t_end = sb("t_end", [P, E])
        t_delta = sb("t_delta", [P, GROUPS, E])
        t_past = sb("t_past", [P, NBLK, E])
        t_eraw = sb("t_eraw", [P, NBLK])
        t_used = sb("t_used", [P, NBLK])
        t_off = sb("t_off", [P, NBLK])
        t_row = sb("t_row", [P, NBLK])
        tab_e = sb("tab_e", [P, NK], I32)
        tab_four = sb("tab_four", [P, NK], I32)
        t_ef = sb("t_ef", [P, NK + 4])
        t_pair = sb("t_pair", [P, NK + 2])
        tab_row = sb("tab_row", [P, NK], I32)
        tab_pad = sb("tab_pad", [P, E], I32)
        y_prod = sb("y_prod", [P, BG * 2 * T, E])
        y_off = sb("y_off", [P, BG * 2 * T])
        y_idx = sb("y_idx", [P, GROUPS, BG * 2 * T], I32)

        h_sb = adj_sb
        h_hi = sb("h_hi", [P, 2, FC, 512], F16)
        h_lo = sb("h_lo", [P, 2, FC, 512], F16)
        deg_junk = h_hi[:, 0]
        rows_sb = sb("rows_sb", [P, 2, 2, 2 * D], F16)
        xb = sb("xb", [P, 2, 2, BLK], F16)
        y_sb = sb("y_sb", [P, 2, 2, D])
        y_half = sb("y_half", [P, 2, 2, D])
        xcb_own = sb("xcb", [P, 2, 2, S], F16)
        xcb = [xcb_own[:, 0], xcb_own[:, 1], xc[:, 0], xc[:, 1]]
        yg = work[:, 0:RING * 2 * T * D].rearrange("p (r j d) -> p r j d", r=RING, d=D)
        wb = sb("wb", [P, 2, 2 * T])
        acc = work[:, RING * 2 * T * D:(RING + 1) * 2 * T * D].rearrange("p (a x) -> p a x", a=2)

        const_in, bias_in, w_in = sem("const_in"), sem("bias_in"), sem2("w_in")
        const_made, w_high, w_low, setup_v = sem("const_made"), sem("w_high"), sem("w_low"), sem("setup_v")
        b1_turned, b1_out, pad_zeroed, empty_zeroed = sem("b1_turned"), sem("b1_out"), sem("pad_zeroed"), sem("empty_zeroed")
        x_in, adj_in, res_in = sem2("x_in"), sem2("adj_in"), sem2("res_in")
        x2_read = sem("x2_read")
        x2_saved, xc_saved, keep_saved, scattered = sem2("x2_saved"), sem2("xc_saved"), sem2("keep_saved"), sem2("scattered")
        stats1, eps1, rsq1, xn_done, deg_done = sem("stats1"), sem("eps1"), sem("rsq1"), sem("xn_done"), sem("deg_done")
        adj_turned, adj_out, xn_turned, xn_out = sem("adj_turned"), sem("adj_out"), sem("xn_turned"), sem("xn_out")
        proj_done, th_done, het_done, hom_done, mix, elu_min, elu_exp = (
            sem("proj_done"), sem("th_done"), sem("het_done"), sem("hom_done"), sem("mix"), sem("elu_min"), sem("elu_exp"))
        eps2, rsq2, xn2_done, high_done, low_done = sem("eps2"), sem("rsq2"), sem("xn2_done"), sem("high_done"), sem("low_done")
        xc_turned, xc_out, logits_done, gap_exp, rank_done, route, rows_go = (
            sem("xc_turned"), sem("xc_out"), sem("logits_done"), sem("gap_exp"), sem("rank_done"), sem("route"), sem("rows_go"))
        counted, count_done, pad_rows, tables, indices = sem("counted"), sem("count_done"), sem("pad_rows"), sem("tables"), sem("indices")
        rows_in, y_saved, rows_turned, xb_out = sem2("rows_in"), sem2("y_saved"), sem("rows_turned"), sem("xb_out")
        up_done, h_done, split_hi, split_done, down_done, y_part, y_done = (
            sem("up_done"), sem("h_done"), sem("split_hi"), sem("split_done"), sem("down_done"), sem("y_part"), sem("y_done"))
        xcb_in, out_saved, gathered = [sem(f"xcb_in{r}") for r in range(XRING)], sem2("out_saved"), [sem(f"gathered{r}") for r in range(RING)]
        sh_up, sh_h, sh_split, sh_down, sh_comb, sh_add, wb_done = (
            sem("sh_up"), sem("sh_h"), sem("sh_split"), sem("sh_down"), sem("sh_comb"), sem("sh_add"), sem("wb_done"))

        TABLES = 11

        def back(half, par, n):
            q = (par - n) % 2
            h = half + (par - n - q) // 2
            return 2 * h + q, h, q

        def known(b):
            return isinstance(b, int)

        def parts(b):
            return [not (known(b) and not 0 <= b - n < NB) for n in range(5)]

        def steps(eng, body):
            for half in (0, 1):
                body(half)
            with eng.Fori(2, NB // 2 - 1) as half:
                body(half)
            for half in range(NB // 2 - 1, NB // 2 + 2):
                body(half)

        def adds(i):
            return (2 * i, 2 * i + 1) if i < BG // 2 else (i + BG // 2,)

        def cut_in(step):
            first = 2 * (step - (NB - 1))
            return [n for n in (first, first + 1) if 0 <= n <= E and known(step)]

        def cut_order(n):
            return (n - 1) % (E + 1)

        block = ctx.enter_context(nc.Block())

        @block.sync
        def _(sp):
            def x_load(b, turn, p):
                if not (known(b) and b < 2):
                    sp.wait_ge(xn_done, b - 1)
                sp.dma_start(xin[:, p], x[bass.ds(b, 1)].rearrange("a (t p) d -> p (a t) d", p=P)).then_inc(x_in[p], 16)

            def adj_load(b, turn, p):
                if not (known(b) and b < 2):
                    sp.wait_ge(adj_turned, T * (b - 1))
                    sp.wait_ge(deg_done, b - 1)
                sp.dma_start(adj_sb[:, p], adj[bass.ds(b, 1)].rearrange("a (t p) m -> p (a t) m", p=P)).then_inc(adj_in[p], 16)

            def residual_load(b, turn, p):
                if not (known(b) and b < 2):
                    sp.wait_ge(xn2_done, b - 1)
                    sp.sem_inc(x2_read, 1)
                    sp.wait_ge(x2_saved[p], 16 * turn)
                sp.dma_start(x2[:, p], x[bass.ds(b, 1)].rearrange("a (t p) d -> p (a t) d", p=P)).then_inc(res_in[p], 16)

            def x2_save(b, turn, p):
                sp.wait_ge(mix, MIX * b + MIX_X2)
                sp.dma_start(x2_all[:, bass.ds(b, 1), :], x2[:, p].rearrange("p t d -> p (t d)")).then_inc(x2_saved[p], 16)

            def xc_save(b, turn, p):
                sp.wait_ge(xc_out, b + 1)
                sp.dma_start(xc_dram[bass.ds(b * P, P), :], xc[:, p].rearrange("p h s -> p (h s)")).then_inc(xc_saved[p], 16)

            def keep_save(b, turn, p):
                sp.wait_ge(route, ROUTE * (b + 1))
                sp.dma_start(keep[:, bass.ds(b, 1), :], kp[:, p]).then_inc(keep_saved[p], 16)

            def body(half):
                for par in range(2):
                    b = back(half, par, 0)[0]
                    s0, s1, s2, s3, s4 = parts(b)
                    ahead = parts(back(half, par, -1)[0])[0]
                    if ahead:
                        x_load(*back(half, par, -1))
                    if s1:
                        residual_load(*back(half, par, 1))
                    if s4:
                        keep_save(*back(half, par, 4))
                    if ahead:
                        adj_load(*back(half, par, -1))
                    if s3:
                        xc_save(*back(half, par, 3))
                    if s2:
                        x2_save(*back(half, par, 2))
                    if known(b):
                        for n in cut_in(b + 1):
                            weights_load(n)

            def weights_load(n):
                e, q = cut_order(n), n % 2
                if n >= 2:
                    sp.wait_ge(w_low, n - 1)
                u, d = (W1p[e], W2p[e]) if e < E else (W1s, W2s)
                sp.dma_start(w_stage[:, q, 0, :], u).then_inc(w_in[q], 16)
                sp.dma_start(w_stage[:, q, 1, :].rearrange("p (c d) -> p c d", c=FC), d.rearrange("(c p) d -> p c d", p=P)).then_inc(w_in[q], 16)

            x_load(0, 0, 0)
            adj_load(0, 0, 0)
            for src, dst in ((W_t, w_gnn[:, 0:D]), (W_h, w_gnn[:, D:2 * D]), (theta, w_gnn[:, 2 * D:3 * D]), (Wr, wr_f[:])):
                sp.dma_start(dst, src).then_inc(const_in, 16)
            sp.dma_start(bt_row[:], b_t.rearrange("(a d) -> a d", a=1)).then_inc(const_in, 16)
            steps(sp, body)

            def xc_in(b):
                sp.wait_ge(xc_saved[b % 2], 16 * (b // 2 + 1))
                sp.dma_start(xcb[b % XRING].rearrange("p h s -> p (h s)"), xc_dram[b * P:(b + 1) * P, :]).then_inc(xcb_in[b % XRING], 16)

            xc_in(0)
            xc_in(1)
            sp.wait_ge(pad_rows, 1)
            for e in range(E):
                row = sp.value_load(tab_pad[0:1, e:e + 1], min_val=0, max_val=PADROW - BLK)
                sp.dma_start(rows[bass.ds(row, BLK), :].rearrange("(s p) c -> p s c", p=P), zeros16[:]).then_inc(pad_zeroed, 16)
            sp.wait_ge(logits_done, NB)
            for q in range(2):
                sp.wait_ge(xc_saved[q], 16 * NB // 2)
            xc_in(2)
            xc_in(3)
            sp.wait_ge(tables, TABLES * GROUPS + 2)
            sp.wait_ge(pad_zeroed, 16 * E)
            sp.wait_ge(empty_zeroed, 16)
            for q in range(2):
                sp.wait_ge(scattered[q], 16 * 2 * T * NB // 2)

            def block_in(k, q, first):
                row = sp.value_load(tab_row[0:1, bass.ds(k, 1)], min_val=0, max_val=PADROW)
                if not first:
                    sp.wait_ge(rows_turned, k - 1)
                sp.dma_start(rows_sb[:, q], rows[bass.ds(row, BLK), :].rearrange("(s p) c -> p s c", p=P)).then_inc(rows_in[q], 16)

            def block_out(g, n, q):
                sp.wait_ge(y_done, g * NBLK + n + 1)
                sp.dma_start(ys[g][bass.ds(n * BLK, BLK), :].rearrange("(s p) d -> p s d", p=P), y_sb[:, q]).then_inc(y_saved[q], 16)

            for k in range(AHEAD):
                block_in(k, k % 2, k < 2)
                if k == 1:
                    for b in range(EARLY, EARLY + XRING):
                        sp.wait_ge(sh_up, FC * (b - XRING + 1))
                        xc_in(b)
            for g in range(GROUPS):
                tail = AHEAD if g == GROUPS - 1 else 0
                with sp.Fori(0, (NBLK - tail) // 2) as half:
                    for q in range(2):
                        block_in(g * NBLK + 2 * half + q + AHEAD, q, False)
                        block_out(g, 2 * half + q, q)
                for n in range(NBLK - tail, NBLK):
                    block_out(g, n, n % 2)

            def out_to(b, q):
                sp.wait_ge(sh_add, 2 * T * (b + 1))
                sp.dma_start(out[bass.ds(b, 1)].rearrange("a (t p) d -> p (a t) d", p=P), acc[:, q].rearrange("p (t d) -> p t d", d=D)
                             ).then_inc(out_saved[q], 16)

            for i in range(NB - EARLY):
                b = EARLY + i
                if b + XRING < NB:
                    sp.wait_ge(sh_up, FC * (b + 1))
                    xc_in(b + XRING)
                for n in adds(i):
                    out_to(n, n % 2)
            for q in range(2):
                sp.wait_ge(out_saved[q], 16 * NB // 2)

        @block.gpsimd
        def _(pool):
            pool.memset(zeros16[:], 0.0).then_inc(const_made, 1)
            pool.memset(b1_rows[:], 0.0).then_inc(const_made, 1)
            pool.wait_ge(const_made, 2)
            pool.dma_start(b1_rows[0:E * FC, :], b1p.rearrange("e (c p) -> (e c) p", p=P)).then_inc(bias_in, 16)
            pool.dma_start(b1_rows[E * FC:(E + 1) * FC, :], b1s.rearrange("(c p) -> c p", p=P)).then_inc(bias_in, 16)
            pool.dma_start(b2[:], b2p.rearrange("(a e) d -> a e d", a=1).to_broadcast([P, E, D])).then_inc(bias_in, 16)
            pool.dma_start(b2s_bc[:], b2s.rearrange("(a d) -> a d", a=1).to_broadcast([P, D])).then_inc(bias_in, 16)
            pool.dma_start(rows[PADROW:PADROW + BLK, :].rearrange("(s p) c -> p s c", p=P), zeros16[:]).then_inc(empty_zeroed, 16)
            pool.memset(ident[:], 0.0).then_inc(const_made, 1)
            pool.memset(before[:], 1.0).then_inc(const_made, 1)
            pool.memset(ones16[:], 1.0).then_inc(const_made, 1)
            pool.memset(ones_row[:], 1.0).then_inc(const_made, 1)
            pool.memset(mhalf[:], -0.5).then_inc(const_made, 1)
            pool.memset(eps[:, :, 0:1], LN_EPS).then_inc(const_made, 1)
            pool.memset(eps[:, :, 1:2], DEG_EPS).then_inc(const_made, 1)
            pool.iota(iota_e[:], [[0, T], [1, E]], base=0, channel_multiplier=0, allow_small_or_imprecise_dtypes=True).then_inc(const_made, 1)
            pool.wait_ge(const_made, 10)
            pool.affine_select(out=ident[:], in_=ident[:], compare_op=ALU.not_equal, fill=1.0, base=0,
                               pattern=[[-1, P]], channel_multiplier=1).then_inc(const_made, 1)
            pool.affine_select(out=before[:], in_=before[:], compare_op=ALU.is_gt, fill=0.0, base=0,
                               pattern=[[1, P]], channel_multiplier=-1).then_inc(const_made, 1)
            pool.wait_ge(const_made, 12)
            pool.tensor_copy(ident16[:], ident[:]).then_inc(const_made, 1)

            pool.iota(blk_iota[:], [[1, NBLK]], base=0, channel_multiplier=0, allow_small_or_imprecise_dtypes=True).then_inc(const_made, 1)
            pool.iota(cap_iota[:], [[BLK, MAXB]], base=0, channel_multiplier=0, allow_small_or_imprecise_dtypes=True).then_inc(const_made, 1)
            pool.iota(reg_base[:], [[REG, E]], base=0, channel_multiplier=0, allow_small_or_imprecise_dtypes=True).then_inc(const_made, 1)
            pool.memset(prefix[:], 0.0).then_inc(const_made, 1)
            pool.memset(lower[:], 0.0).then_inc(const_made, 1)
            pool.wait_ge(const_made, 18)
            for e in range(1, E):
                pool.memset(lower[:, e, 0:e], 1.0).then_inc(const_made, 1)

            def rsqrt1(half, par):
                b, turn, p = back(half, par, 0)
                pool.wait_ge(stats1, 2 * (b + 1))
                pool.wait_ge(deg_done, b + 1)
                pool.tensor_tensor(pw1[:], mvd[:, p, :, 1:3], eps[:], ALU.add).then_inc(eps1, 1)
                pool.wait_ge(eps1, b + 1)
                if not (known(b) and b < 2):
                    pool.wait_ge(mix, MIX * (b - 2) + MIX_HOM)
                pool.tensor_tensor(rs1[:, p], pw1[:], mhalf[:], ALU.pow).then_inc(rsq1, 1)

            def rsqrt2(half, par):
                b, turn, p = back(half, par, 2)
                pool.wait_ge(mix, MIX * (b + 1))
                pool.tensor_tensor(pw2[:], mv2[:, p, :, 1], eps[:, :, 0], ALU.add).then_inc(eps2, 1)
                pool.wait_ge(eps2, b + 1)
                pool.tensor_tensor(rs2[:, p], pw2[:], mhalf[:, :, 0], ALU.pow).then_inc(rsq2, 1)

            def scatter(half, par):
                b, turn, p = back(half, par, 4)
                pool.wait_ge(low_done, b + 1)
                pool.wait_ge(high_done, b + 1)
                pool.wait_ge(route, ROUTE * b + R_IDX)
                pool.sem_inc(rows_go, 1)
                for j in range(2 * T):
                    pool.indirect_dma_start(rows, bass.IndirectOffsetOnAxis(ap=idx[:, p, j:j + 1], axis=0),
                                            xr[:, p, j % T].rearrange("p h d -> p (h d)"), None).then_inc(scattered[p], 16)

            def body(half):
                for par in range(2):
                    s0, s1, s2, s3, s4 = parts(back(half, par, 0)[0])
                    if s4:
                        scatter(half, par)
                    if s0:
                        rsqrt1(half, par)
                    if s2:
                        rsqrt2(half, par)

            steps(pool, body)

            for g in range(GROUPS):
                pool.wait_ge(indices, 3 * (g + 1))
                for q in range(2):
                    pool.wait_ge(y_saved[q], 16 * (g + 1) * NBLK // 2)
                for b in range(g * BG, (g + 1) * BG):
                    r = b % RING
                    if b >= RING:
                        pool.wait_ge(sh_add, 2 * T * (b - RING + 1))
                    for j in range(2 * T):
                        n = (b - g * BG) * 2 * T + j
                        pool.indirect_dma_start(yg[:, r, j], None, ys[g],
                                                bass.IndirectOffsetOnAxis(ap=y_idx[:, g, n:n + 1], axis=0)).then_inc(gathered[r], 16)

        @block.scalar
        def _(act):
            def adj_to_sbuf(half, par, j):
                b, turn, p = back(half, par, 1)
                act.wait_ge(adj_turned, T * b + j + 1)
                if j == 0 and not (known(b) and b < 1):
                    act.wait_ge(hom_done, b)
                act.activation(adj_t[:, j], ps[:, j % 2], ACT.Copy).then_inc(adj_out, 1)

            def high(half, par):
                b, turn, p = back(half, par, 3)
                act.wait_ge(xn2_done, b + 1)
                if not (known(b) and b < 2):
                    act.wait_ge(scattered[p], 16 * 2 * T * turn)
                    act.wait_ge(xc_turned, b - 1)
                act.activation(xr[:, p, :, 0, :], xn2[:], ACT.Copy).then_inc(high_done, 1)

            def xn_to_sbuf(half, par):
                b, turn, p = back(half, par, 1)
                act.wait_ge(xn_turned, b + 1)
                if not (known(b) and b < 1):
                    act.wait_ge(proj_done, T * b)
                act.activation(xn_t[:], ps[:, 2], ACT.Copy).then_inc(xn_out, 1)

            def messages(half, par, tiles):
                b, turn, p = back(half, par, 1)
                if tiles[0] == 0:
                    act.wait_ge(rsq1, b + 1)
                if tiles[0] == 0 and not (known(b) and b < 1):
                    act.wait_ge(hom_done, b)
                    act.wait_ge(het_done, HET * b)
                for t in tiles:
                    act.wait_ge(proj_done, T * b + t + 1)
                    act.activation(f_sb[:, t], ps[:, 3 + t % 2, 2 * D:3 * D], ACT.Copy, scale=rs1[:, p, t, 1:2])
                    act.activation(th[:, t], ps[:, 3 + t % 2, 0:D], ACT.Tanh, scale=0.5).then_inc(th_done, 1)

            def degrees(half, par):
                b, turn, p = back(half, par, 0)
                act.wait_ge(adj_in[p], 16 * (turn + 1))
                if not (known(b) and b < 2):
                    act.wait_ge(eps1, b - 1)
                if not (known(b) and b < 1):
                    act.wait_ge(deg_done, b)
                for t in range(T):
                    last = act.activation(deg_junk[:, t], adj_sb[:, p, t], ACT.Copy, accum_out=mvd[:, p, t, 2:3])
                last.then_inc(deg_done, 1)

            def gap(half, par):
                b, turn, p = back(half, par, 4)
                act.wait_ge(route, ROUTE * b + R_GAP)
                act.activation(r_exp[:], r_gap[:], ACT.Exp, scale=1.0 / WS).then_inc(gap_exp, 1)

            def elu_floor(half, par):
                b, turn, p = back(half, par, 2)
                act.wait_ge(mix, MIX * b + MIX_OUT)
                act.activation(mix_m[:], mix_o[:], ACT.Relu, scale=-1.0).then_inc(elu_min, 1)

            def elu(half, par):
                b, turn, p = back(half, par, 2)
                act.wait_ge(elu_min, b + 1)
                act.activation(mix_e[:], mix_m[:], ACT.Exp, scale=-1.0).then_inc(elu_exp, 1)

            def xc_to_sbuf(half, par):
                b, turn, p = back(half, par, 3)
                act.wait_ge(xc_turned, b + 1)
                if not (known(b) and b < 2):
                    act.wait_ge(xc_saved[p], 16 * turn)
                act.activation(xc[:, p].rearrange("p h s -> p (h s)"), ps[:, 6].bitcast(F16), ACT.Copy).then_inc(xc_out, 1)

            def cut_high(n):
                e, q = cut_order(n), n % 2
                act.wait_ge(w_in[q], 32 * (n // 2 + 1))
                act.activation(w1[:, e, 0, :], w_stage[:, q, 0, :], ACT.Copy, scale=WS)
                act.activation(w2[:, e, :, 0], w_stage[:, q, 1, :].rearrange("p (c d) -> p c d", c=FC), ACT.Copy, scale=WS).then_inc(w_high, 1)

            def body(half):
                for par in range(2):
                    b = back(half, par, 0)[0]
                    s0, s1, s2, s3, s4 = parts(b)
                    if s4:
                        gap(half, par)
                    if s0:
                        degrees(half, par)
                    if s3:
                        high(half, par)
                    if s1:
                        adj_to_sbuf(half, par, 0)
                        adj_to_sbuf(half, par, 1)
                        xn_to_sbuf(half, par)
                    if s3:
                        xc_to_sbuf(half, par)
                    if s1:
                        adj_to_sbuf(half, par, 2)
                    if s2:
                        elu_floor(half, par)
                    if s1:
                        adj_to_sbuf(half, par, 3)
                    if s2:
                        elu(half, par)
                    if s1:
                        messages(half, par, (0, 1, 2, 3))
                    for n in cut_in(b):
                        cut_high(n)

            steps(act, body)

            act.wait_ge(b1_turned, 1)
            act.activation(b1[:], ps[:, 6, 0:(E + 1) * FC], ACT.Copy).then_inc(b1_out, 1)

            act.wait_ge(b1_out, 1)
            act.wait_ge(adj_turned, T * NB)
            def shared_gelu(b, q, first):
                for c in range(FC):
                    act.wait_ge(sh_up, FC * b + c + 1)
                    if c == 0 and not first:
                        act.wait_ge(sh_split, b - 1)
                        act.wait_ge(sh_down, b - 1)
                    act.activation(h_sb[:, q, c], ps[:, c], ACT.Gelu, bias=b1[:, E * FC + c:E * FC + c + 1], scale=1.0 / WS)
                    act.activation(h_hi[:, q, c], ps[:, c], ACT.Gelu, bias=b1[:, E * FC + c:E * FC + c + 1],
                                   scale=1.0 / WS).then_inc(sh_h, 1)

            for b in range(EARLY):
                shared_gelu(b, b % 2, b < 2)

            act.wait_ge(tables, TABLES * GROUPS + 2)
            act.wait_ge(sh_split, EARLY)

            def gelu(k, q, first):
                e = act.value_load(tab_e[0:1, bass.ds(k, 1)], min_val=0, max_val=E - 1)
                if not first:
                    act.wait_ge(split_done, k - 1)
                for c in range(FC):
                    if c % 2 == 0:
                        act.wait_ge(up_done, 2 * k + c // 2 + 1)
                    last = act.activation(h_sb[:, q, c, 0:BLK], ps[:, 2 * q + c // 2, (c % 2) * BLK:(c % 2 + 1) * BLK], ACT.Gelu,
                                          bias=b1[:, bass.ds(e * FC + c, 1)], scale=1.0 / WS)
                    if c % 2:
                        last.then_inc(h_done, 1)

            def xb_to_sbuf(k, q, first):
                act.wait_ge(rows_turned, k + 1)
                if not first:
                    act.wait_ge(up_done, 2 * (k - 1))
                act.activation(xb[:, q].rearrange("p h s -> p (h s)"), ps[:, 6 + q].bitcast(F16)[:, 0:2 * BLK], ACT.Copy).then_inc(xb_out, 1)

            xb_to_sbuf(0, 0, True)
            xb_to_sbuf(1, 1, True)
            for k in range(2):
                gelu(k, k, True)
                xb_to_sbuf(k + 2, k, False)
            with act.Fori(1, NK // 2 - 1) as half:
                for q in range(2):
                    gelu(2 * half + q, q, False)
                    xb_to_sbuf(2 * half + q + 2, q, False)
            for q in range(2):
                gelu(NK - 2 + q, q, False)

            act.wait_ge(split_done, NK)
            with act.Fori(EARLY // 2, NB // 2) as half:
                for q in range(2):
                    shared_gelu(2 * half + q, q, False)

        @block.vector
        def _(dve):
            def normalise_tile(half, par, t):
                b, turn, p = back(half, par, 1)
                if t == 0:
                    dve.wait_ge(rsq1, b + 1)
                    if not (known(b) and b < 1):
                        dve.wait_ge(xn_turned, b)
                last = dve.tensor_scalar(xn[:, t], xin[:, p, t], mvd[:, p, t, 0:1], rs1[:, p, t, 0:1], ALU.subtract, ALU.mult)
                if t == T - 1:
                    last.then_inc(xn_done, 1)

            def normalise2_tile(half, par, t):
                b, turn, p = back(half, par, 3)
                if t == 0:
                    dve.wait_ge(rsq2, b + 1)
                    if not (known(b) and b < 1):
                        dve.wait_ge(high_done, b)
                last = dve.tensor_scalar(xn2[:, t], x2[:, p, t], mv2[:, p, t, 0:1], rs2[:, p, t:t + 1], ALU.subtract, ALU.mult)
                if t == T - 1:
                    last.then_inc(xn2_done, 1)

            def low(half, par):
                b, turn, p = back(half, par, 3)
                dve.wait_ge(high_done, b + 1)
                dve.tensor_tensor(xr[:, p, :, 1, :], xn2[:], xr[:, p, :, 0, :], ALU.subtract).then_inc(low_done, 1)

            def first_stats(half, par):
                b, turn, p = back(half, par, 0)
                dve.wait_ge(x_in[p], 16 * (turn + 1))
                for t in range(T):
                    last = dve.bn_stats(stats[:, t], xin[:, p, t])
                last.then_inc(stats1, 1)

            def first_stats_ready(half, par):
                b = back(half, par, 0)[0]
                dve.wait_ge(stats1, 2 * b + 1)
                if not (known(b) and b < 2):
                    dve.wait_ge(eps1, b - 1)

            def first_variances(half, par):
                b, turn, p = back(half, par, 0)
                for t in range(T):
                    last = dve.bn_aggr(mvd[:, p, t, 0:2], stats[:, t])
                last.then_inc(stats1, 1)

            def het_tile(half, par, t):
                b, turn, p = back(half, par, 1)
                dve.wait_ge(th_done, T * b + t + 1)
                dve.scalar_tensor_tensor(out=het[:, t], in0=th[:, t], scalar=1.0, in1=ps[:, 3 + t % 2, D:2 * D],
                                         op0=ALU.subtract, op1=ALU.mult).then_inc(het_done, 1)

            def gate_of(half, par):
                dve.tensor_scalar(gate[:], th[:], 0.5, 0.5, ALU.mult, ALU.add).then_inc(het_done, 1)

            def combine(half, par):
                b, turn, p = back(half, par, 2)
                m = MIX * b
                dve.wait_ge(het_done, HET * (b + 1))
                dve.wait_ge(hom_done, b + 1)
                for t in range(T):
                    dve.scalar_tensor_tensor(out=mix_o[:, t], in0=ps[:, 5, t * D:(t + 1) * D], scalar=rs1[:, p, t, 1:2],
                                             in1=gate[:, t], op0=ALU.mult, op1=ALU.mult).then_inc(mix, 1)
                dve.wait_ge(mix, m + MIX_HOM)
                dve.scalar_tensor_tensor(out=mix_o[:], in0=het[:], scalar=-0.5, in1=mix_o[:], op0=ALU.mult, op1=ALU.add).then_inc(mix, 1)

            def elu_max(half, par):
                b = back(half, par, 2)[0]
                dve.wait_ge(elu_exp, b + 1)
                dve.scalar_tensor_tensor(out=mix_o[:], in0=mix_e[:], scalar=-1.0, in1=mix_o[:], op0=ALU.add, op1=ALU.max).then_inc(mix, 1)

            def residual(half, par):
                b, turn, p = back(half, par, 2)
                dve.wait_ge(res_in[p], 16 * (turn + 1))
                dve.wait_ge(mix, MIX * b + MIX_ELU)
                dve.tensor_tensor(x2[:, p], x2[:, p], mix_o[:], ALU.add).then_inc(mix, 1)

            def second_stats(half, par, tiles):
                b, turn, p = back(half, par, 2)
                if tiles[0] == 0:
                    dve.wait_ge(mix, MIX * b + MIX_X2)
                for t in tiles:
                    last = dve.bn_stats(stats2[:, t], x2[:, p, t])
                if t == T - 1:
                    last.then_inc(mix, 1)

            def second_stats_ready(half, par):
                b = back(half, par, 2)[0]
                dve.wait_ge(mix, MIX * b + MIX_STATS)
                if not (known(b) and b < 2):
                    dve.wait_ge(eps2, b - 1)

            def second_variances(half, par):
                b, turn, p = back(half, par, 2)
                for t in range(T):
                    last = dve.bn_aggr(mv2[:, p, t], stats2[:, t])
                last.then_inc(mix, 1)

            def choose(half, par, s1, s2, s3):
                b, turn, p = back(half, par, 3)
                r = ROUTE * b
                lg = ps[:, 7, 0:T * E].rearrange("p (t e) -> p t e", e=E)
                hot = [kp[:, p, k * T * E:(k + 1) * T * E].rearrange("p (t e) -> p t e", e=E) for k in range(2)]

                def less(logit, top, n):
                    dve.wait_ge(route, r + n)
                    dve.tensor_tensor(r_ne[:], logit, r_top[:, top].unsqueeze(2).to_broadcast([P, T, E]), ALU.is_lt).then_inc(route, 1)

                def candidates(n):
                    dve.wait_ge(route, r + n)
                    dve.scalar_tensor_tensor(out=r_cand[:], in0=r_ne[:], scalar=64.0, in1=iota_e[:], op0=ALU.mult, op1=ALU.add).then_inc(route, 1)

                def least(n):
                    dve.wait_ge(route, r + n)
                    dve.tensor_reduce(r_idx[:], r_cand[:], AX.X, ALU.min).then_inc(route, 1)

                def one_hot(k, n):
                    dve.wait_ge(route, r + n)
                    dve.tensor_tensor(hot[k], iota_e[:], r_idx[:].unsqueeze(2).to_broadcast([P, T, E]), ALU.is_equal).then_inc(route, 1)

                if s3:
                    dve.wait_ge(logits_done, b + 1)
                    if not (known(b) and b < 2):
                        dve.wait_ge(keep_saved[p], 16 * turn)
                    dve.tensor_reduce(r_top[:, 0], lg, AX.X, ALU.max).then_inc(route, 1)
                    less(lg, 0, 1)
                    candidates(2)
                    least(3)
                    one_hot(0, 4)
                if s2:
                    elu_max(half, par)
                if s1:
                    het_tile(half, par, 0)
                if s3:
                    dve.wait_ge(route, r + 5)
                    dve.scalar_tensor_tensor(out=r_l2[:], in0=hot[0], scalar=-BIG, in1=lg, op0=ALU.mult, op1=ALU.add).then_inc(route, 1)
                if s2:
                    residual(half, par)
                if s1:
                    het_tile(half, par, 1)
                if s3:
                    dve.wait_ge(route, r + 6)
                    dve.tensor_reduce(r_top[:, 1], r_l2[:], AX.X, ALU.max).then_inc(route, 1)
                if s2:
                    second_stats(half, par, (0, 1))
                if s3:
                    less(r_l2[:], 1, 7)
                if s2:
                    second_stats(half, par, (2, 3))
                if s3:
                    candidates(8)
                if s1:
                    het_tile(half, par, 2)
                if s2:
                    second_stats_ready(half, par)
                if s3:
                    least(9)
                if s2:
                    second_variances(half, par)
                if s3:
                    one_hot(1, 10)
                if s1:
                    het_tile(half, par, 3)
                if s3:
                    dve.wait_ge(route, r + 11)
                    dve.tensor_tensor(r_mask[:, p], hot[0], hot[1], ALU.add).then_inc(route, 1)
                    dve.tensor_tensor(r_gap[:], r_top[:, 1], r_top[:, 0], ALU.subtract).then_inc(route, 1)
                    dve.wait_ge(route, r + 12)
                    dve.tensor_reduce(r_red[:], r_mask[:, p].rearrange("p t e -> p e t"), AX.X, ALU.add).then_inc(route, 1)
                if s1:
                    gate_of(half, par)
                if s3:
                    dve.wait_ge(route, r + 14)
                    dve.tensor_tensor(prefix[:, 1 - p], prefix[:, p], r_red[:], ALU.add).then_inc(route, 1)

            def place(half, par, s1, s3, s4):
                b, turn, p = back(half, par, 4)
                r = ROUTE * b
                hot2 = kp[:, p, 0:2 * T * E].rearrange("p (k j) -> p k j", k=2)
                pos, w = kp[:, p, 64:72], kp[:, p, 72:80]
                if s1:
                    normalise_tile(half, par, 0)
                    normalise_tile(half, par, 1)
                if s4:
                    dve.wait_ge(rank_done, b + 1)
                    dve.tensor_tensor(r_pos[:], ps[:, 7, 64:64 + T * E].rearrange("p (t e) -> p t e", e=E),
                                      reg_base[:].unsqueeze(1).to_broadcast([P, T, E]), ALU.add).then_inc(route, 1)
                if s1:
                    normalise_tile(half, par, 2)
                if s4:
                    dve.wait_ge(route, r + 16)
                    dve.tensor_tensor(r_prod[:].rearrange("p (k t) e -> p k (t e)", k=2), hot2,
                                      r_pos[:].rearrange("p t e -> p (t e)").unsqueeze(1).to_broadcast([P, 2, T * E]), ALU.mult).then_inc(route, 1)
                if s1:
                    normalise_tile(half, par, 3)
                if s4:
                    dve.wait_ge(route, r + 17)
                    dve.tensor_reduce(pos, r_prod[:], AX.X, ALU.add).then_inc(route, 1)
                    dve.wait_ge(gap_exp, b + 1)
                    dve.tensor_scalar(r_sum[:], r_exp[:], 1.0, WS, ALU.add, ALU.mult).then_inc(route, 1)
                    if not (known(b) and b < 2):
                        dve.wait_ge(scattered[p], 16 * 2 * T * turn)
                    dve.wait_ge(route, r + 18)
                    dve.tensor_copy(idx[:, p], pos).then_inc(route, 1)
                    dve.wait_ge(route, r + 19)
                    dve.reciprocal(w[:, 0:T], r_sum[:]).then_inc(route, 1)
                if s3:
                    normalise2_tile(half, par, 0)
                    normalise2_tile(half, par, 1)
                if s4:
                    dve.wait_ge(route, r + 21)
                    dve.tensor_tensor(w[:, T:2 * T], w[:, 0:T], r_exp[:], ALU.mult).then_inc(route, 1)
                if s3:
                    normalise2_tile(half, par, 2)
                    normalise2_tile(half, par, 3)

            def cut_low(n):
                e, q = cut_order(n), n % 2
                dve.wait_ge(w_high, n + 1)
                dve.scalar_tensor_tensor(out=w1[:, e, 1, :], in0=w_stage[:, q, 0, :], scalar=WS, in1=w1[:, e, 0, :],
                                         op0=ALU.mult, op1=ALU.subtract)
                dve.scalar_tensor_tensor(out=w2[:, e, :, 1], in0=w_stage[:, q, 1, :].rearrange("p (c d) -> p c d", c=FC), scalar=WS,
                                         in1=w2[:, e, :, 0], op0=ALU.mult, op1=ALU.subtract).then_inc(w_low, 1)

            def body(half):
                for par in range(2):
                    b = back(half, par, 0)[0]
                    s0, s1, s2, s3, s4 = parts(b)
                    place(half, par, s1, s3, s4)
                    if s0:
                        first_stats(half, par)
                        first_stats_ready(half, par)
                    if s3:
                        low(half, par)
                    if s0:
                        first_variances(half, par)
                    if s2:
                        combine(half, par)
                    choose(half, par, s1, s2, s3)
                    for n in cut_in(b):
                        cut_low(n)
                    if known(b) and b == 0:
                        cut_router_weights()

            def cut_router_weights():
                dve.wait_ge(const_in, 16 * 5)
                dve.wait_ge(bias_in, 16 * 4)
                dve.tensor_scalar(wr16[:, 0], wr_f[:], WS, None, ALU.mult).then_inc(setup_v, 1)
                dve.tensor_tensor(b2[:], b2[:], b2s_bc[:].unsqueeze(1).to_broadcast([P, E, D]), ALU.add).then_inc(setup_v, 1)
                dve.wait_ge(setup_v, 1)
                dve.scalar_tensor_tensor(out=wr16[:, 1], in0=wr_f[:], scalar=WS, in1=wr16[:, 0], op0=ALU.mult, op1=ALU.subtract).then_inc(setup_v, 1)
                dve.wait_ge(setup_v, 3)
                dve.tensor_scalar(b2[:], b2[:], WS, None, ALU.mult).then_inc(setup_v, 1)

            steps(dve, body)

            def make_tables(g):
                m = TABLES * g
                own = [g * NBLK, (g + 1) * NBLK]
                dve.tensor_tensor(t_cmp[:], cap_iota[:].unsqueeze(1).to_broadcast([P, E, MAXB]),
                                  t_cnt[:, g].unsqueeze(2).to_broadcast([P, E, MAXB]), ALU.is_lt).then_inc(tables, 1)
                dve.wait_ge(tables, m + 1)
                dve.tensor_reduce(t_nblk[:], t_cmp[:], AX.X, ALU.add).then_inc(tables, 1)
                dve.wait_ge(tables, m + 2)
                dve.tensor_tensor(t_low[:], lower[:], t_nblk[:].unsqueeze(1).to_broadcast([P, E, E]), ALU.mult).then_inc(tables, 1)
                dve.wait_ge(tables, m + 3)
                dve.tensor_reduce(t_start[:], t_low[:], AX.X, ALU.add).then_inc(tables, 1)
                dve.wait_ge(tables, m + 4)
                dve.tensor_tensor(t_end[:], t_start[:], t_nblk[:], ALU.add)
                dve.scalar_tensor_tensor(out=t_delta[:, g], in0=t_start[:], scalar=float(BLK), in1=t_first[:, g], op0=ALU.mult, op1=ALU.subtract).then_inc(tables, 1)
                dve.wait_ge(tables, m + 5)
                dve.tensor_tensor(t_past[:], t_end[:].unsqueeze(1).to_broadcast([P, NBLK, E]),
                                  blk_iota[:].unsqueeze(2).to_broadcast([P, NBLK, E]), ALU.is_le).then_inc(tables, 1)
                dve.wait_ge(tables, m + 6)
                dve.tensor_reduce(t_eraw[:], t_past[:], AX.X, ALU.add).then_inc(tables, 1)
                dve.wait_ge(tables, m + 7)
                dve.tensor_scalar(t_used[:], t_eraw[:], float(E), None, ALU.is_lt)
                dve.tensor_scalar(t_ef[:, own[0]:own[1]], t_eraw[:], float(E - 1), None, ALU.min)
                dve.tensor_tensor(t_past[:], t_eraw[:].unsqueeze(2).to_broadcast([P, NBLK, E]),
                                  iota_e[:, 0, :].unsqueeze(1).to_broadcast([P, NBLK, E]), ALU.is_equal)
                dve.tensor_scalar(t_row[:], blk_iota[:], float(BLK), float(-PADROW), ALU.mult, ALU.add).then_inc(tables, 1)
                dve.wait_ge(tables, m + 8)
                dve.tensor_tensor(t_past[:], t_past[:], t_delta[:, g].unsqueeze(1).to_broadcast([P, NBLK, E]), ALU.mult)
                dve.tensor_tensor(t_row[:], t_row[:], t_used[:], ALU.mult).then_inc(tables, 1)
                dve.wait_ge(tables, m + 9)
                dve.tensor_reduce(t_off[:], t_past[:], AX.X, ALU.add).then_inc(tables, 1)
                dve.wait_ge(tables, m + 10)
                dve.scalar_tensor_tensor(out=tab_row[:, own[0]:own[1]], in0=t_row[:], scalar=float(PADROW), in1=t_off[:],
                                         op0=ALU.add, op1=ALU.subtract).then_inc(tables, 1)

            def make_indices(g):
                dve.tensor_tensor(y_prod[:].rearrange("p (b k) e -> p b k e", b=BG),
                                  keep[:, g * BG:(g + 1) * BG, 0:2 * T * E].rearrange("p b (k e) -> p b k e", e=E),
                                  t_delta[:, g].unsqueeze(1).unsqueeze(1).to_broadcast([P, BG, 2 * T, E]), ALU.mult).then_inc(indices, 1)
                dve.wait_ge(indices, 3 * g + 1)
                dve.tensor_reduce(y_off[:], y_prod[:], AX.X, ALU.add).then_inc(indices, 1)
                dve.wait_ge(indices, 3 * g + 2)
                dve.tensor_tensor(y_idx[:, g].rearrange("p (b k) -> p b k", b=BG), y_off[:].rearrange("p (b k) -> p b k", b=BG),
                                  keep[:, g * BG:(g + 1) * BG, 64:72], ALU.add).then_inc(indices, 1)

            def shared_split(b):
                q = b % 2
                dve.wait_ge(sh_h, FC * (b + 1))
                if b >= 2:
                    dve.wait_ge(sh_down, b - 1)
                dve.tensor_tensor(h_lo[:, q], h_sb[:, q], h_hi[:, q], ALU.subtract).then_inc(sh_split, 1)

            def shared_out(b):
                dve.wait_ge(sh_down, b + 1)
                dve.scalar_tensor_tensor(out=x2_all[:, b], in0=ps[:, 4 + b % 2], scalar=1.0 / WS, in1=x2_all[:, b],
                                         op0=ALU.mult, op1=ALU.add).then_inc(sh_comb, 1)

            def add_up(b):
                q, r = b % 2, b % RING
                dve.tensor_copy(wb[:, q], keep[:, b, 72:80]).then_inc(wb_done, 1)
                dve.wait_ge(sh_comb, b + 1)
                if b >= 2:
                    dve.wait_ge(out_saved[q], 16 * (b // 2))
                dve.wait_ge(gathered[r], 16 * 2 * T * (b // RING + 1))
                dve.wait_ge(wb_done, b + 1)
                for k in range(2):
                    if k == 1:
                        dve.wait_ge(sh_add, 2 * T * b + T)
                    for t in range(T):
                        a = acc[:, q, t * D:(t + 1) * D]
                        dve.scalar_tensor_tensor(out=a, in0=yg[:, r, k * T + t], scalar=wb[:, q, k * T + t:k * T + t + 1],
                                                 in1=a if k else x2_all[:, b, t * D:(t + 1) * D],
                                                 op0=ALU.mult, op1=ALU.add).then_inc(sh_add, 1)

            for q in range(2):
                dve.wait_ge(keep_saved[q], 16 * NB // 2)
            for g in range(GROUPS):
                last = dve.tensor_reduce(t_sum[:, g], keep[:, g * BG:(g + 1) * BG, 0:2 * T * E].rearrange("p b (k e) -> p e b k", e=E), AX.XY, ALU.add)
            last.then_inc(counted, 1)
            dve.tensor_copy(t_first[:, 0], reg_base[:]).then_inc(counted, 1)
            dve.memset(t_ef[:, NK:NK + 4], 0.0)
            dve.wait_ge(counted, 2)
            dve.tensor_copy(t_own[:], t_sum[:]).then_inc(counted, 1)
            dve.wait_ge(count_done, 1)
            dve.tensor_copy(t_cnt[:].rearrange("p g e -> p (g e)"), ps[:, 7, 128:128 + GROUPS * E]).then_inc(counted, 1)
            for g in range(GROUPS):
                dve.wait_ge(counted, 4 + g)
                dve.tensor_tensor(t_first[:, g + 1], t_first[:, g], t_cnt[:, g], ALU.add).then_inc(counted, 1)
            dve.wait_ge(counted, 4 + GROUPS)
            dve.tensor_copy(tab_pad[:], t_first[:, GROUPS]).then_inc(pad_rows, 1)
            for g in range(GROUPS):
                make_tables(g)
                shared_split(g)
            dve.tensor_copy(tab_e[:], t_ef[:, 0:NK])
            dve.scalar_tensor_tensor(out=t_pair[:], in0=t_ef[:, 1:NK + 3], scalar=float(E), in1=t_ef[:, 0:NK + 2], op0=ALU.mult, op1=ALU.add).then_inc(tables, 1)
            dve.wait_ge(tables, TABLES * GROUPS + 1)
            dve.scalar_tensor_tensor(out=tab_four[:], in0=t_pair[:, 2:NK + 2], scalar=float(E * E), in1=t_pair[:, 0:NK],
                                     op0=ALU.mult, op1=ALU.add).then_inc(tables, 1)
            for q in range(2):
                dve.wait_ge(x2_saved[q], 16 * NB // 2)
            shared_out(0)
            for b in range(GROUPS, EARLY):
                shared_split(b)
                shared_out(b - 1)
            shared_out(EARLY - 1)
            for g in range(GROUPS):
                make_indices(g)

            dve.wait_ge(sh_down, EARLY)
            def split(k, q, first):
                dve.wait_ge(h_done, 2 * (k + 1))
                if not first:
                    dve.wait_ge(down_done, k - 1)
                dve.tensor_copy(h_hi[:, q, :, 0:BLK], h_sb[:, q, :, 0:BLK]).then_inc(split_hi, 1)
                dve.wait_ge(split_hi, k + 1)
                dve.tensor_tensor(h_lo[:, q, :, 0:BLK], h_sb[:, q, :, 0:BLK], h_hi[:, q, :, 0:BLK], ALU.subtract).then_inc(split_done, 1)

            def y_to_sbuf(k, turn, q, first):
                e = dve.value_load(tab_e[0:1, bass.ds(k, 1)], min_val=0, max_val=E - 1)
                dve.wait_ge(down_done, k + 1)
                if not first:
                    dve.wait_ge(y_saved[q], 16 * turn)
                o = ps[:, 4 + q].rearrange("p (s h d) -> p s h d", s=2, h=2)
                dve.tensor_tensor(y_half[:, q], o[:, :, 1], b2[:, bass.ds(e, 1), :].to_broadcast([P, 2, D]), ALU.add).then_inc(y_part, 1)
                dve.wait_ge(y_part, k + 1)
                dve.tensor_tensor(y_sb[:, q], o[:, :, 0], y_half[:, q], ALU.add).then_inc(y_done, 1)

            split(0, 0, True)
            split(1, 1, True)
            y_to_sbuf(0, 0, 0, True)
            split(2, 0, False)
            y_to_sbuf(1, 0, 1, True)
            split(3, 1, False)
            y_to_sbuf(2, 1, 0, False)
            with dve.Fori(2, NK // 2) as half:
                split(2 * half, 0, False)
                y_to_sbuf(2 * half - 1, half - 1, 1, False)
                split(2 * half + 1, 1, False)
                y_to_sbuf(2 * half, half, 0, False)
            y_to_sbuf(NK - 1, NK // 2 - 1, 1, False)

            dve.wait_ge(down_done, NK)
            shared_split(EARLY)
            for i in range(NB - EARLY):
                b = EARLY + i
                if b + 1 < NB:
                    shared_split(b + 1)
                shared_out(b)
                for n in adds(i):
                    add_up(n)

        @block.tensor
        def _(pe):
            def turn_adj(half, par, n, j):
                b, turn, p = back(half, par, n)
                if j == 0:
                    pe.wait_ge(adj_in[p], 16 * (turn + 1))
                if not (known(b) and b == 0 and j < 2):
                    pe.wait_ge(adj_out, T * b + j - 1)
                for t in range(T):
                    last = pe.transpose(ps[:, j % 2, t * P:(t + 1) * P], adj_sb[:, p, t, j * P:(j + 1) * P], ident[:])
                last.then_inc(adj_turned, 1)

            def turn_xn(half, par):
                b, turn, p = back(half, par, 1)
                pe.wait_ge(xn_done, b + 1)
                if not (known(b) and b == 0):
                    pe.wait_ge(xn_out, b)
                for t in range(T):
                    last = pe.transpose(ps[:, 2, t * P:(t + 1) * P], xn[:, t], ident[:])
                last.then_inc(xn_turned, 1)

            def turn_xc(half, par):
                b, turn, p = back(half, par, 3)
                pe.wait_ge(low_done, b + 1)
                if not (known(b) and b == 0):
                    pe.wait_ge(xc_out, b)
                for h in range(2):
                    for t in range(T):
                        last = pe.transpose(ps[:, 6].bitcast(F16)[:, h * S + t * P:h * S + (t + 1) * P], xr[:, p, t, h], ident16[:])
                last.then_inc(xc_turned, 1)

            def project(half, par, tiles):
                b, turn, p = back(half, par, 1)
                pe.wait_ge(xn_out, b + 1)
                for t in tiles:
                    if not (known(b) and b == 0 and t < 2):
                        tb, tt = (b, t - 2) if t >= 2 else (b - 1, t + 2)
                        pe.wait_ge(het_done, HET * tb + tt + 1)
                    lhs = xn_t[:, t * P:(t + 1) * P]
                    pe.matmul(ps[:, 3 + t % 2, 0:3 * D], lhs, w_gnn[:], start=True, stop=False)
                    pe.matmul(ps[:, 3 + t % 2, 0:D], ones_row[:], bt_row[:], start=False, stop=True).then_inc(proj_done, 1)

            def logits(half, par):
                b, turn, p = back(half, par, 3)
                pe.wait_ge(xc_out, b + 1)
                if known(b) and b == 0:
                    pe.wait_ge(setup_v, 3)
                else:
                    pe.wait_ge(route, ROUTE * (b - 1) + R_RANK_READ)
                for t in range(T):
                    o = ps[:, 7, t * E:(t + 1) * E]
                    hi, lo = (xc[:, p, h, t * P:(t + 1) * P] for h in range(2))
                    pe.matmul(o, hi, wr16[:, 0], start=True, stop=False)
                    pe.matmul(o, hi, wr16[:, 1], start=False, stop=False)
                    last = pe.matmul(o, lo, wr16[:, 0], start=False, stop=True)
                last.then_inc(logits_done, 1)

            def homophily(half, par):
                b, turn, p = back(half, par, 2)
                pe.wait_ge(adj_out, T * (b + 1))
                pe.wait_ge(th_done, T * (b + 1))
                if not (known(b) and b == 0):
                    pe.wait_ge(mix, MIX * (b - 1) + MIX_HOM)
                for t in range(T):
                    for j in range(T):
                        last = pe.matmul(ps[:, 5, t * D:(t + 1) * D], adj_t[:, j, t * P:(t + 1) * P], f_sb[:, j],
                                         start=(j == 0), stop=(j == T - 1))
                last.then_inc(hom_done, 1)

            def rank(half, par):
                b, turn, p = back(half, par, 3)
                pe.wait_ge(route, ROUTE * b + R_MASK)
                def o(t):
                    return ps[:, 7, 64 + t * E:64 + T * E]
                pe.matmul(o(0), before[:], r_mask[:, p].rearrange("p t e -> p (t e)"), start=True, stop=False)
                for t in range(T - 1):
                    for u in range(t + 1, T):
                        pe.matmul(ps[:, 7, 64 + u * E:64 + (u + 1) * E], ones16[:], r_mask[:, p, t], start=False, stop=False)
                for u in range(T):
                    last = pe.matmul(ps[:, 7, 64 + u * E:64 + (u + 1) * E], ones16[:], prefix[:, p], start=False, stop=(u == T - 1))
                last.then_inc(rank_done, 1)

            def body(half):
                for par in range(2):
                    s0, s1, s2, s3, s4 = parts(back(half, par, 0)[0])
                    if s2:
                        homophily(half, par)
                    if s1:
                        turn_xn(half, par)
                    if s3:
                        turn_xc(half, par)
                    if s1:
                        turn_adj(half, par, 1, 2)
                        turn_adj(half, par, 1, 3)
                    if s3:
                        logits(half, par)
                    if s1:
                        project(half, par, (0, 1, 2, 3))
                    if s0:
                        turn_adj(half, par, 0, 0)
                        turn_adj(half, par, 0, 1)
                    if s3:
                        rank(half, par)

            pe.wait_ge(const_made, 13)
            pe.wait_ge(const_in, 16 * 5)
            steps(pe, body)

            pe.wait_ge(bias_in, 16 * 4)
            pe.wait_ge(xc_out, NB)
            pe.transpose(ps[:, 6, 0:P], b1_rows[:], ident[:]).then_inc(b1_turned, 1)

            pe.wait_ge(counted, 3)
            last = pe.matmul(ps[:, 7, 128:128 + GROUPS * E], ones16[:], t_own[:].rearrange("p g e -> p (g e)"), start=True, stop=True)
            last.then_inc(count_done, 1)

            def shared_up(b, r, turn, first):
                pe.wait_ge(xcb_in[r], 16 * (turn + 1))
                for c in range(FC):
                    if not first:
                        pe.wait_ge(sh_h, FC * (b - 1) + c + 1)
                    hi, lo = (w1[:, E, h, c * P:(c + 1) * P] for h in range(2))
                    pe.matmul(ps[:, c], hi, xcb[r][:, 0], start=True, stop=False)
                    pe.matmul(ps[:, c], hi, xcb[r][:, 1], start=False, stop=False)
                    pe.matmul(ps[:, c], lo, xcb[r][:, 0], start=False, stop=True).then_inc(sh_up, 1)

            def shared_down(b, q, first):
                pe.wait_ge(sh_split, b + 1)
                if not first:
                    pe.wait_ge(sh_comb, b - 1)
                for t in range(T):
                    o = ps[:, 4 + q, t * D:(t + 1) * D]
                    for c in range(FC):
                        hh, hl = h_hi[:, q, c, t * P:(t + 1) * P], h_lo[:, q, c, t * P:(t + 1) * P]
                        pe.matmul(o, hh, w2[:, E, c, 0], start=(c == 0), stop=False)
                        pe.matmul(o, hh, w2[:, E, c, 1], start=False, stop=False)
                        last = pe.matmul(o, hl, w2[:, E, c, 0], start=False, stop=(c == FC - 1))
                last.then_inc(sh_down, 1)

            pe.wait_ge(w_low, 1)
            shared_up(0, 0, 0, True)
            for b in range(EARLY):
                if b + 1 < EARLY:
                    shared_up(b + 1, b + 1, 0, False)
                shared_down(b, b % 2, b < 2)

            pe.wait_ge(tables, TABLES * GROUPS + 2)
            pe.wait_ge(w_low, E + 1)
            pe.wait_ge(sh_h, FC * EARLY)
            pe.wait_ge(sh_comb, EARLY)

            def expert(k):
                return pe.value_load(tab_e[0:1, bass.ds(k, 1)], min_val=0, max_val=E - 1)

            def turn_rows(k, turn, q, first):
                pe.wait_ge(rows_in[q], 16 * (turn + 1))
                if not first:
                    pe.wait_ge(xb_out, k - 1)
                for h in range(2):
                    for t in range(BLK // P):
                        last = pe.transpose(ps[:, 6 + q].bitcast(F16)[:, h * BLK + t * P:h * BLK + (t + 1) * P],
                                            rows_sb[:, q, t, h * D:(h + 1) * D], ident16[:])
                last.then_inc(rows_turned, 1)

            def up(e, k, q, first):
                pe.wait_ge(xb_out, k + 1)
                if not first:
                    pe.wait_ge(h_done, 2 * (k - 1))
                for c in range(FC):
                    o = ps[:, 2 * q + c // 2, (c % 2) * BLK:(c % 2 + 1) * BLK]
                    hi, lo = (w1[:, bass.ds(e, 1), h, c * P:(c + 1) * P].rearrange("p a f -> p (a f)") for h in range(2))
                    pe.matmul(o, hi, xb[:, q, 0], start=True, stop=False)
                    pe.matmul(o, hi, xb[:, q, 1], start=False, stop=False)
                    last = pe.matmul(o, lo, xb[:, q, 0], start=False, stop=True)
                    if c % 2:
                        last.then_inc(up_done, 1)

            def down(e, k, q, first):
                pe.wait_ge(split_done, k + 1)
                if not first:
                    pe.wait_ge(y_done, k - 1)
                o = ps[:, 4 + q].rearrange("p (s h d) -> p s h d", s=2, h=2)
                for c in range(FC):
                    w = w2[:, bass.ds(e, 1), c].rearrange("p a h d -> p (a h d)")
                    for s in range(BLK // P):
                        pe.matmul(ps[:, 4 + q, 2 * s * D:2 * (s + 1) * D], h_hi[:, q, c, s * P:(s + 1) * P], w,
                                  start=(c == 0 and s == 0), stop=False)
                    for s in range(BLK // P):
                        last = pe.matmul(o[:, s, 0], h_lo[:, q, c, s * P:(s + 1) * P], w[:, 0:D],
                                         start=False, stop=(c == FC - 1 and s == BLK // P - 1))
                last.then_inc(down_done, 1)

            pe.wait_ge(b1_out, 1)
            turn_rows(0, 0, 0, True)
            turn_rows(1, 0, 1, True)
            for k in range(2):
                up(expert(k), k, k, True)
                turn_rows(k + 2, 1, k, False)
            for k in range(2):
                up(expert(k + 2), k + 2, k, False)
                turn_rows(k + 4, 2, k, False)
                down(expert(k), k, k, True)
            with pe.Fori(1, NK // 2 - 2) as half:
                four = pe.value_load(tab_four[0:1, bass.ds(2 * half, 1)], min_val=0, max_val=E ** 4 - 1)
                for q in range(2):
                    k = 2 * half + q
                    up(four // E ** (q + 2) % E, k + 2, q, False)
                    turn_rows(k + 4, half + 2, q, False)
                    down(four // E ** q % E, k, q, False)
            for k in range(NK - 4, NK):
                if k + 2 < NK:
                    up(expert(k + 2), k + 2, k % 2, False)
                down(expert(k), k, k % 2, False)

            pe.wait_ge(h_done, 2 * NK)
            pe.wait_ge(y_done, NK)
            shared_up(EARLY, 0, 1, True)
            with pe.Fori(1, NB // XRING - 1) as ring:
                for r in range(XRING):
                    b = XRING * ring + r
                    shared_up(b + 1, (r + 1) % XRING, ring + (r + 1) // XRING, False)
                    shared_down(b, r % 2, False)
            for b in range(NB - XRING, NB):
                if b + 1 < NB:
                    shared_up(b + 1, (b + 1) % XRING, (b + 1) // XRING, False)
                shared_down(b, b % 2, False)


_INS = ['x', 'adj', 'L0_gnn_W_t', 'L0_gnn_b_t', 'L0_gnn_W_h', 'L0_gnn_theta', 'L0_ffn_Wr', 'L0_ffn_W1s', 'L0_ffn_b1s',
        'L0_ffn_W2s', 'L0_ffn_b2s', 'L0_ffn_W1p', 'L0_ffn_b1p', 'L0_ffn_W2p', 'L0_ffn_b2p']
_OUTS = [((16, 512, 128), 'float32')]


def kernel(**inputs):
    import numpy as _np
    import concourse.bacc as _bacc
    from concourse import mybir as _mybir
    from concourse.bass_utils import run_bass_kernel_spmd as _run

    nc = _bacc.Bacc("TRN2", target_bir_lowering=False, num_devices=1)
    arrays, args = {}, []
    for name in _INS:
        a = _np.ascontiguousarray(inputs[name])
        arrays[f"in_{name}_dram"] = a
        args.append(nc.dram_tensor(f"in_{name}_dram", a.shape, _mybir.dt.from_np(a.dtype), kind="ExternalInput").ap())
    for i, (shape, dtype) in enumerate(_OUTS):
        dt = _mybir.dt.from_np(_np.dtype(dtype))
        args.append(nc.dram_tensor(f"out_{i}_dram", shape, dt, kind="ExternalOutput").ap())
    build(nc, *args)
    r = _run(nc, [arrays], core_ids=[0])
    got = tuple(r.results[0][f"out_{i}_dram"] for i in range(len(_OUTS)))
    return got[0]
```

```python
from contextlib import ExitStack

import concourse.bass as bass
from concourse import mybir

ALU = mybir.AluOpType
ACT = mybir.ActivationFunctionType
AX = mybir.AxisListType
F32 = mybir.dt.float32
F16 = mybir.dt.float16
I32 = mybir.dt.int32

P = 128
WS = 64.0
BLK = 256
GROUP_BATCHES = (10, 6)
GROUPS = len(GROUP_BATCHES)
RING = 11
AHEAD = 6
EARLY = 4
ADDS_IN_C = 4
BIG = 1.0e30
LN_EPS, DEG_EPS = 1e-5, 1e-6
HET = 5
MIX_HOM, MIX_OUT, MIX_ELU, MIX_X2, MIX_STATS, MIX = 4, 5, 6, 7, 8, 9
R_MASK, R_GAP, R_RANK_READ, R_IDX, ROUTE = 12, 13, 16, 19, 22


def build(nc, x, adj, W_t, b_t, W_h, theta, Wr, W1s, b1s, W2s, b2s, W1p, b1p, W2p, b2p, out):
    NB, S, D = x.shape
    T = S // P
    F = W1s.shape[1]
    FC = F // P
    E = Wr.shape[1]
    assert D == P and S == 512 and F == 512 and E == 8 and NB == sum(GROUP_BATCHES) and NB % 2 == EARLY % 2 == 0 and GROUPS == 2 and EARLY >= 4
    FIRST = [sum(GROUP_BATCHES[:g]) for g in range(GROUPS + 1)]
    REG = NB * S + BLK
    NBLKS = [(2 * n * S - E) // BLK + E for n in GROUP_BATCHES]
    NBLKS[-1] += sum(NBLKS) % 2
    BLK0 = [sum(NBLKS[:g]) for g in range(GROUPS + 1)]
    NK, MOST = sum(NBLKS), max(NBLKS)
    BG = max(GROUP_BATCHES)
    PADROW = E * REG
    MAXB = BG * S // BLK

    rows = nc.dram_tensor("expert_rows", (PADROW + BLK, 2 * D), F16, kind="Internal").ap()
    ys = [nc.dram_tensor(f"expert_out{g}", (NBLKS[g] * BLK, D), F32, kind="Internal").ap() for g in range(GROUPS)]
    xc_dram = nc.dram_tensor("xn2_t", (NB * P, 2 * S), F16, kind="Internal").ap()

    with ExitStack() as ctx:
        def sb(name, shape, dt=F32):
            return ctx.enter_context(nc.sbuf_tensor(name, shape, dt))

        def sem(name):
            return ctx.enter_context(nc.semaphore(name))

        def sem2(name):
            return [sem(name + "_even"), sem(name + "_odd")]

        ps = ctx.enter_context(nc.psum_tensor("ps", [P, 8, 512], F32))

        ident = sb("ident", [P, P])
        ident16 = sb("ident16", [P, P], F16)
        before = sb("before", [P, P], F16)
        ones16 = sb("ones16", [P, P], F16)
        zeros16 = sb("zeros16", [P, 2, 2 * D], F16)
        eps = sb("eps", [P, T, 2])
        mhalf = sb("mhalf", [P, T, 2])
        iota_e = sb("iota_e", [P, T, E])
        blk_iota = sb("blk_iota", [P, MOST])
        cap_iota = sb("cap_iota", [P, MAXB])
        lower = sb("lower", [P, E, E])
        reg_base = sb("reg_base", [P, E])
        w_gnn = sb("w_gnn", [P, 3 * D])
        bt_row = sb("bt_row", [1, D])
        bt16 = sb("bt16", [1, 2, D], F16)
        wr_f = sb("wr_f", [P, E])
        wr16 = sb("wr16", [P, 2, E], F16)
        w_stage = sb("w_stage", [P, 2, 2, 512])
        w1 = sb("w1", [P, E + 1, 2, F], F16)
        w2 = sb("w2", [P, E + 1, FC, 2, D], F16)
        b1_rows = sb("b1_rows", [P, P])
        b1 = sb("b1", [P, (E + 1) * FC])
        b2 = sb("b2", [P, E, D])
        b2s_bc = sb("b2s_bc", [P, D])

        work = sb("work", [P, RING * 2 * T * D])
        xin = work[:, 0:1024].rearrange("p (a t d) -> p a t d", a=2, d=D)
        x2 = work[:, 1024:2048].rearrange("p (a t d) -> p a t d", a=2, d=D)
        adj_t = work[:, 2048:4096].rearrange("p (t s) -> p t s", t=T)
        xn, f_sb, th, gate, het, mix_o, mix_m, mix_e, xn2 = (
            work[:, (8 + i) * T * D:(9 + i) * T * D].rearrange("p (t d) -> p t d", d=D) for i in range(9))
        xn_t = work[:, 17 * T * D:18 * T * D]
        adj_sb = sb("adj_sb", [P, 2, T, S])
        stats = sb("stats", [P, T, 6])
        mvd = sb("mvd", [P, 2, T, 3])
        pw1 = sb("pw1", [P, T, 2])
        rs1 = sb("rs1", [P, 2, T, 2])
        stats2 = sb("stats2", [P, T, 6])
        mv2 = sb("mv2", [P, 2, T, 2])
        pw2 = sb("pw2", [P, T])
        rs2 = sb("rs2", [P, 2, T])
        xr = sb("xr", [P, 2, T, 2, D], F16)
        xc = sb("xc", [P, 2, 2, S], F16)
        r_top = sb("r_top", [P, 2, T])
        r_ne = sb("r_ne", [P, T, E])
        r_cand = sb("r_cand", [P, T, E])
        r_idx = sb("r_idx", [P, T])
        r_l2 = sb("r_l2", [P, T, E])
        r_mask = sb("r_mask", [P, 2, T, E], F16)
        r_red = sb("r_red", [P, E])
        prefix = sb("prefix", [P, 2, E], F16)
        r_gap = sb("r_gap", [P, T])
        r_exp = sb("r_exp", [P, T])
        r_sum = sb("r_sum", [P, T])
        r_pos = sb("r_pos", [P, T, E])
        r_prod = sb("r_prod", [P, 2 * T, E])
        kp = sb("kp", [P, 2, 80])
        idx = sb("idx", [P, 2, 2 * T], I32)
        keep = sb("keep", [P, NB, 80])
        x2_all = sb("x2_all", [P, NB, T * D])

        t_sum = sb("t_sum", [P, GROUPS, E])
        t_own = sb("t_own", [P, GROUPS, E], F16)
        t_cnt = sb("t_cnt", [P, GROUPS, E])
        t_first = sb("t_first", [P, GROUPS + 1, E])
        t_cmp = sb("t_cmp", [P, E, MAXB])
        t_nblk = sb("t_nblk", [P, E])
        t_low = sb("t_low", [P, E, E])
        t_start = sb("t_start", [P, E])
        t_end = sb("t_end", [P, E])
        t_delta = sb("t_delta", [P, GROUPS, E])
        t_past_all = sb("t_past", [P, MOST, E])
        t_eraw_all = sb("t_eraw", [P, MOST])
        t_used_all = sb("t_used", [P, MOST])
        t_off_all = sb("t_off", [P, MOST])
        t_row_all = sb("t_row", [P, MOST])
        tab_e = sb("tab_e", [P, NK], I32)
        tab_four = sb("tab_four", [P, NK], I32)
        t_ef = sb("t_ef", [P, NK + 4])
        t_pair = sb("t_pair", [P, NK + 2])
        tab_row = sb("tab_row", [P, NK], I32)
        tab_pad = sb("tab_pad", [P, E], I32)
        y_prod_all = sb("y_prod", [P, BG * 2 * T, E])
        y_off_all = sb("y_off", [P, BG * 2 * T])
        y_idx = sb("y_idx", [P, GROUPS, BG * 2 * T], I32)

        h_sb = adj_sb
        h_hi = sb("h_hi", [P, 2, FC, 512], F16)
        h_lo = sb("h_lo", [P, 2, FC, 512], F16)
        deg_junk = h_hi[:, 0]
        rows_sb = sb("rows_sb", [P, 2, 2, 2 * D], F16)
        xb = sb("xb", [P, 2, 2, BLK], F16)
        y_sb = sb("y_sb", [P, 2, 2, D])
        y_half = sb("y_half", [P, 2, 2, D])
        xcb = sb("xcb", [P, 2, 2, S], F16)
        yg = work[:, 0:RING * 2 * T * D].rearrange("p (r j d) -> p r j d", r=RING, d=D)
        wb = sb("wb", [P, 2, 2 * T])

        const_in, bias_in, w_in = sem("const_in"), sem("bias_in"), sem2("w_in")
        const_made, w_high, w_low, setup_v = sem("const_made"), sem("w_high"), sem("w_low"), sem("setup_v")
        b1_turned, b1_out, pad_zeroed, empty_zeroed = sem("b1_turned"), sem("b1_out"), sem("pad_zeroed"), sem("empty_zeroed")
        x_in, adj_in, res_in = sem2("x_in"), sem2("adj_in"), sem2("res_in")
        x2_read, bt_cut = sem("x2_read"), sem("bt_cut")
        x2_saved, xc_saved, keep_saved, scattered = sem2("x2_saved"), sem2("xc_saved"), sem2("keep_saved"), sem2("scattered")
        stats1, eps1, rsq1, xn_done, deg_done = sem("stats1"), sem("eps1"), sem("rsq1"), sem("xn_done"), sem("deg_done")
        adj_turned, adj_out, xn_turned, xn_out = sem("adj_turned"), sem("adj_out"), sem("xn_turned"), sem("xn_out")
        proj_done, th_done, het_done, hom_done, mix, elu_min, elu_exp = (
            sem("proj_done"), sem("th_done"), sem("het_done"), sem("hom_done"), sem("mix"), sem("elu_min"), sem("elu_exp"))
        eps2, rsq2, xn2_done, high_done, low_done = sem("eps2"), sem("rsq2"), sem("xn2_done"), sem("high_done"), sem("low_done")
        xc_turned, xc_out, logits_done, gap_exp, rank_done, route, rows_go = (
            sem("xc_turned"), sem("xc_out"), sem("logits_done"), sem("gap_exp"), sem("rank_done"), sem("route"), sem("rows_go"))
        counted, count_done, pad_rows, tables, indices = sem("counted"), sem("count_done"), sem("pad_rows"), sem("tables"), sem("indices")
        rows_in, y_saved, rows_turned, xb_out = sem2("rows_in"), sem2("y_saved"), sem("rows_turned"), sem("xb_out")
        up_done, h_done, split_hi, split_done, down_done, y_part, y_done = (
            sem("up_done"), sem("h_done"), sem("split_hi"), sem("split_done"), sem("down_done"), sem("y_part"), sem("y_done"))
        xcb_in, out_saved, gathered = sem2("xcb_in"), sem("out_saved"), [sem(f"gathered{r}") for r in range(RING)]
        sh_up, sh_h, sh_split, sh_down, sh_comb, sh_add, wb_done = (
            sem("sh_up"), sem("sh_h"), sem("sh_split"), sem("sh_down"), sem("sh_comb"), sem("sh_add"), sem("wb_done"))

        COUNTS = 4
        TABLES = 11

        def back(half, par, n):
            q = (par - n) % 2
            h = half + (par - n - q) // 2
            return 2 * h + q, h, q

        def known(b):
            return isinstance(b, int)

        def parts(b):
            return [not (known(b) and not 0 <= b - n < NB) for n in range(5)]

        def steps(eng, body):
            for half in (0, 1):
                body(half)
            with eng.Fori(2, NB // 2 - 1) as half:
                body(half)
            for half in range(NB // 2 - 1, NB // 2 + 2):
                body(half)

        def add_after(n):
            return (n - 5) // 3 if n >= 5 and (n - 5) % 3 == 0 and (n - 5) // 3 < ADDS_IN_C else None

        def adds(i):
            left, periods = NB - ADDS_IN_C, NB - EARLY
            return [ADDS_IN_C + n for n in range(left) if round(n * (periods - 1) / (left - 1)) == i]

        def final_in(i):
            def whole(i):
                added = [b for n in range(i + 1) for b in adds(n)]
                return 0 if i < 0 else min(EARLY + i + 1, ADDS_IN_C + len(added))
            return range(whole(i - 1), whole(i))

        CUTS = {1: (0,), 2: (1, 2), 3: (3, 4), NB - 1: (5,), NB: (6,), NB + 1: (7, 8)}

        def cut_in(step):
            return CUTS.get(step, ()) if known(step) else ()

        def cut_order(n):
            return (n - 1) % (E + 1)

        block = ctx.enter_context(nc.Block())

        @block.sync
        def _(sp):
            def x_load(b, turn, p):
                if not (known(b) and b < 2):
                    sp.wait_ge(xn_done, b - 1)
                sp.dma_start(xin[:, p], x[bass.ds(b, 1)].rearrange("a (t p) d -> p (a t) d", p=P)).then_inc(x_in[p], 16)

            def adj_load(b, turn, p):
                if not (known(b) and b < 2):
                    sp.wait_ge(adj_turned, T * (b - 1))
                    sp.wait_ge(deg_done, b - 1)
                sp.dma_start(adj_sb[:, p], adj[bass.ds(b, 1)].rearrange("a (t p) m -> p (a t) m", p=P)).then_inc(adj_in[p], 16)

            def residual_load(b, turn, p):
                if not (known(b) and b < 2):
                    sp.wait_ge(xn2_done, b - 1)
                    sp.sem_inc(x2_read, 1)
                    sp.wait_ge(x2_saved[p], 16 * turn)
                sp.dma_start(x2[:, p], x[bass.ds(b, 1)].rearrange("a (t p) d -> p (a t) d", p=P)).then_inc(res_in[p], 16)

            def x2_save(b, turn, p):
                sp.wait_ge(mix, MIX * b + MIX_X2)
                sp.dma_start(x2_all[:, bass.ds(b, 1), :], x2[:, p].rearrange("p t d -> p (t d)")).then_inc(x2_saved[p], 16)

            def xc_save(b, turn, p):
                sp.wait_ge(xc_out, b + 1)
                sp.dma_start(xc_dram[bass.ds(b * P, P), :], xc[:, p].rearrange("p h s -> p (h s)")).then_inc(xc_saved[p], 16)

            def keep_save(b, turn, p):
                sp.wait_ge(route, ROUTE * (b + 1))
                sp.dma_start(keep[:, bass.ds(b, 1), :], kp[:, p]).then_inc(keep_saved[p], 16)

            def body(half):
                for par in range(2):
                    b = back(half, par, 0)[0]
                    s0, s1, s2, s3, s4 = parts(b)
                    ahead = parts(back(half, par, -1)[0])[0]
                    if ahead:
                        x_load(*back(half, par, -1))
                    if s1:
                        residual_load(*back(half, par, 1))
                    if s4:
                        keep_save(*back(half, par, 4))
                    if ahead:
                        adj_load(*back(half, par, -1))
                    if s3:
                        xc_save(*back(half, par, 3))
                    if s2:
                        x2_save(*back(half, par, 2))
                    if known(b):
                        for n in cut_in(b + 1):
                            weights_load(n)
                        if b >= NB:
                            xc_in(b - NB)

            def xc_in(b):
                sp.wait_ge(xc_saved[b % 2], 16 * (b // 2 + 1))
                if b >= 2:
                    sp.wait_ge(sh_up, FC * (b - 1))
                sp.dma_start(xcb[:, b % 2].rearrange("p h s -> p (h s)"), xc_dram[b * P:(b + 1) * P, :]).then_inc(xcb_in[b % 2], 16)

            def weights_load(n):
                e, q = cut_order(n), n % 2
                if n >= 2:
                    sp.wait_ge(w_low, n - 1)
                u, d = (W1p[e], W2p[e]) if e < E else (W1s, W2s)
                sp.dma_start(w_stage[:, q, 0, :], u).then_inc(w_in[q], 16)
                sp.dma_start(w_stage[:, q, 1, :].rearrange("p (c d) -> p c d", c=FC), d.rearrange("(c p) d -> p c d", p=P)).then_inc(w_in[q], 16)

            x_load(0, 0, 0)
            adj_load(0, 0, 0)
            for src, dst in ((W_t, w_gnn[:, 0:D]), (W_h, w_gnn[:, D:2 * D]), (theta, w_gnn[:, 2 * D:3 * D]), (Wr, wr_f[:])):
                sp.dma_start(dst, src).then_inc(const_in, 16)
            sp.dma_start(bt_row[:], b_t.rearrange("(a d) -> a d", a=1)).then_inc(const_in, 16)
            steps(sp, body)

            sp.wait_ge(pad_rows, 1)
            for e in range(E):
                row = sp.value_load(tab_pad[0:1, e:e + 1], min_val=0, max_val=PADROW - BLK)
                sp.dma_start(rows[bass.ds(row, BLK), :].rearrange("(s p) c -> p s c", p=P), zeros16[:]).then_inc(pad_zeroed, 16)
            sp.wait_ge(tables, TABLES * GROUPS + 2)
            sp.wait_ge(pad_zeroed, 16 * E)
            sp.wait_ge(empty_zeroed, 16)
            for q in range(2):
                sp.wait_ge(scattered[q], 16 * 2 * T * NB // 2)

            def block_in(k, q, first):
                row = sp.value_load(tab_row[0:1, bass.ds(k, 1)], min_val=0, max_val=PADROW)
                if not first:
                    sp.wait_ge(rows_turned, k - 1)
                sp.dma_start(rows_sb[:, q], rows[bass.ds(row, BLK), :].rearrange("(s p) c -> p s c", p=P)).then_inc(rows_in[q], 16)

            def block_out(g, n, q):
                sp.wait_ge(y_done, BLK0[g] + n + 1)
                sp.dma_start(ys[g][bass.ds(n * BLK, BLK), :].rearrange("(s p) d -> p s d", p=P), y_sb[:, q]).then_inc(y_saved[q], 16)

            for k in range(AHEAD):
                block_in(k, k % 2, k < 2)
                if k == 1:
                    for b in range(4, EARLY + 2):
                        xc_in(b)
            for g in range(GROUPS):
                pairs = (min(BLK0[g + 1], NK - AHEAD) - BLK0[g]) // 2
                with sp.Fori(0, pairs) as half:
                    for n in range(2):
                        block_in(BLK0[g] + 2 * half + n + AHEAD, (BLK0[g] + n) % 2, False)
                        block_out(g, 2 * half + n, (BLK0[g] + n) % 2)
                for k in range(BLK0[g] + 2 * pairs, BLK0[g + 1]):
                    if k + AHEAD < NK:
                        block_in(k + AHEAD, k % 2, False)
                    block_out(g, k - BLK0[g], k % 2)

            def out_to(b):
                sp.wait_ge(sh_comb, b + 1)
                sp.wait_ge(sh_add, 2 * T * (b + 1))
                sp.dma_start(out[b].rearrange("(t p) d -> p t d", p=P), x2_all[:, b].rearrange("p (t d) -> p t d", d=D)).then_inc(out_saved, 16)

            for i in range(NB - EARLY):
                if EARLY + i + 2 < NB:
                    xc_in(EARLY + i + 2)
                for b in final_in(i - 1):
                    out_to(b)
            for b in final_in(NB - EARLY - 1):
                out_to(b)
            sp.wait_ge(out_saved, 16 * NB)

        @block.gpsimd
        def _(pool):
            pool.memset(zeros16[:], 0.0).then_inc(const_made, 1)
            pool.memset(b1_rows[:], 0.0).then_inc(const_made, 1)
            pool.wait_ge(const_made, 2)
            pool.dma_start(b1_rows[0:E * FC, :], b1p.rearrange("e (c p) -> (e c) p", p=P)).then_inc(bias_in, 16)
            pool.dma_start(b1_rows[E * FC:(E + 1) * FC, :], b1s.rearrange("(c p) -> c p", p=P)).then_inc(bias_in, 16)
            pool.dma_start(b2[:], b2p.rearrange("(a e) d -> a e d", a=1).to_broadcast([P, E, D])).then_inc(bias_in, 16)
            pool.dma_start(b2s_bc[:], b2s.rearrange("(a d) -> a d", a=1).to_broadcast([P, D])).then_inc(bias_in, 16)
            pool.dma_start(rows[PADROW:PADROW + BLK, :].rearrange("(s p) c -> p s c", p=P), zeros16[:]).then_inc(empty_zeroed, 16)
            pool.memset(ident[:], 0.0).then_inc(const_made, 1)
            pool.memset(before[:], 1.0).then_inc(const_made, 1)
            pool.memset(ones16[:], 1.0).then_inc(const_made, 1)
            pool.memset(mhalf[:], -0.5).then_inc(const_made, 1)
            pool.memset(eps[:, :, 0:1], LN_EPS).then_inc(const_made, 1)
            pool.memset(eps[:, :, 1:2], DEG_EPS).then_inc(const_made, 1)
            pool.iota(iota_e[:], [[0, T], [1, E]], base=0, channel_multiplier=0, allow_small_or_imprecise_dtypes=True).then_inc(const_made, 1)
            pool.wait_ge(const_made, 9)
            pool.affine_select(out=ident[:], in_=ident[:], compare_op=ALU.not_equal, fill=1.0, base=0,
                               pattern=[[-1, P]], channel_multiplier=1).then_inc(const_made, 1)
            pool.affine_select(out=before[:], in_=before[:], compare_op=ALU.is_gt, fill=0.0, base=0,
                               pattern=[[1, P]], channel_multiplier=-1).then_inc(const_made, 1)
            pool.wait_ge(const_made, 11)
            pool.tensor_copy(ident16[:], ident[:]).then_inc(const_made, 1)

            pool.iota(blk_iota[:], [[1, MOST]], base=0, channel_multiplier=0, allow_small_or_imprecise_dtypes=True).then_inc(const_made, 1)
            pool.iota(cap_iota[:], [[BLK, MAXB]], base=0, channel_multiplier=0, allow_small_or_imprecise_dtypes=True).then_inc(const_made, 1)
            pool.iota(reg_base[:], [[REG, E]], base=0, channel_multiplier=0, allow_small_or_imprecise_dtypes=True).then_inc(const_made, 1)
            pool.memset(prefix[:], 0.0).then_inc(const_made, 1)
            pool.memset(lower[:], 0.0).then_inc(const_made, 1)
            pool.wait_ge(const_made, 17)
            for e in range(1, E):
                pool.memset(lower[:, e, 0:e], 1.0).then_inc(const_made, 1)

            def rsqrt1(half, par):
                b, turn, p = back(half, par, 0)
                pool.wait_ge(stats1, 2 * (b + 1))
                pool.wait_ge(deg_done, b + 1)
                pool.tensor_tensor(pw1[:], mvd[:, p, :, 1:3], eps[:], ALU.add).then_inc(eps1, 1)
                pool.wait_ge(eps1, b + 1)
                if not (known(b) and b < 2):
                    pool.wait_ge(mix, MIX * (b - 2) + MIX_HOM)
                pool.tensor_tensor(rs1[:, p], pw1[:], mhalf[:], ALU.pow).then_inc(rsq1, 1)

            def rsqrt2(half, par):
                b, turn, p = back(half, par, 2)
                pool.wait_ge(mix, MIX * (b + 1))
                pool.tensor_tensor(pw2[:], mv2[:, p, :, 1], eps[:, :, 0], ALU.add).then_inc(eps2, 1)
                pool.wait_ge(eps2, b + 1)
                pool.tensor_tensor(rs2[:, p], pw2[:], mhalf[:, :, 0], ALU.pow).then_inc(rsq2, 1)

            def scatter(half, par):
                b, turn, p = back(half, par, 4)
                pool.wait_ge(low_done, b + 1)
                pool.wait_ge(high_done, b + 1)
                pool.wait_ge(route, ROUTE * b + R_IDX)
                pool.sem_inc(rows_go, 1)
                for j in range(2 * T):
                    pool.indirect_dma_start(rows, bass.IndirectOffsetOnAxis(ap=idx[:, p, j:j + 1], axis=0),
                                            xr[:, p, j % T].rearrange("p h d -> p (h d)"), None).then_inc(scattered[p], 16)

            def body(half):
                for par in range(2):
                    s0, s1, s2, s3, s4 = parts(back(half, par, 0)[0])
                    if s4:
                        scatter(half, par)
                    if s0:
                        rsqrt1(half, par)
                    if s2:
                        rsqrt2(half, par)

            steps(pool, body)

            for g in range(GROUPS):
                pool.wait_ge(indices, 3 * (g + 1))
                for q in range(2):
                    pool.wait_ge(y_saved[q], 16 * ((BLK0[g + 1] + 1 - q) // 2))
                for b in range(FIRST[g], FIRST[g + 1]):
                    r = b % RING
                    if b >= RING:
                        pool.wait_ge(sh_add, 2 * T * (b - RING + 1))
                    for j in range(2 * T):
                        n = (b - FIRST[g]) * 2 * T + j
                        pool.indirect_dma_start(yg[:, r, j], None, ys[g],
                                                bass.IndirectOffsetOnAxis(ap=y_idx[:, g, n:n + 1], axis=0)).then_inc(gathered[r], 16)

        @block.scalar
        def _(act):
            def adj_to_sbuf(half, par, j):
                b, turn, p = back(half, par, 1)
                act.wait_ge(adj_turned, T * b + j + 1)
                if j == 0 and not (known(b) and b < 1):
                    act.wait_ge(hom_done, b)
                act.activation(adj_t[:, j], ps[:, j % 2], ACT.Copy).then_inc(adj_out, 1)

            def high(half, par):
                b, turn, p = back(half, par, 3)
                act.wait_ge(xn2_done, b + 1)
                if not (known(b) and b < 2):
                    act.wait_ge(scattered[p], 16 * 2 * T * turn)
                    act.wait_ge(xc_turned, b - 1)
                act.activation(xr[:, p, :, 0, :], xn2[:], ACT.Copy).then_inc(high_done, 1)

            def xn_to_sbuf(half, par):
                b, turn, p = back(half, par, 1)
                act.wait_ge(xn_turned, b + 1)
                if not (known(b) and b < 1):
                    act.wait_ge(proj_done, T * b)
                act.activation(xn_t[:], ps[:, 2], ACT.Copy).then_inc(xn_out, 1)

            def messages(half, par, tiles):
                b, turn, p = back(half, par, 1)
                if tiles[0] == 0:
                    act.wait_ge(rsq1, b + 1)
                if tiles[0] == 0 and not (known(b) and b < 1):
                    act.wait_ge(hom_done, b)
                    act.wait_ge(het_done, HET * b)
                for t in tiles:
                    act.wait_ge(proj_done, T * b + t + 1)
                    act.activation(f_sb[:, t], ps[:, 3 + t % 2, 2 * D:3 * D], ACT.Copy, scale=rs1[:, p, t, 1:2])
                    act.activation(th[:, t], ps[:, 3 + t % 2, 0:D], ACT.Tanh, scale=0.5).then_inc(th_done, 1)

            def degrees(half, par):
                b, turn, p = back(half, par, 0)
                act.wait_ge(adj_in[p], 16 * (turn + 1))
                if not (known(b) and b < 2):
                    act.wait_ge(eps1, b - 1)
                if not (known(b) and b < 1):
                    act.wait_ge(deg_done, b)
                for t in range(T):
                    last = act.activation(deg_junk[:, t], adj_sb[:, p, t], ACT.Copy, accum_out=mvd[:, p, t, 2:3])
                last.then_inc(deg_done, 1)

            def gap(half, par):
                b, turn, p = back(half, par, 4)
                act.wait_ge(route, ROUTE * b + R_GAP)
                act.activation(r_exp[:], r_gap[:], ACT.Exp, scale=1.0 / WS).then_inc(gap_exp, 1)

            def elu_floor(half, par):
                b, turn, p = back(half, par, 2)
                act.wait_ge(mix, MIX * b + MIX_OUT)
                act.activation(mix_m[:], mix_o[:], ACT.Relu, scale=-1.0).then_inc(elu_min, 1)

            def elu(half, par):
                b, turn, p = back(half, par, 2)
                act.wait_ge(elu_min, b + 1)
                act.activation(mix_e[:], mix_m[:], ACT.Exp, scale=-1.0).then_inc(elu_exp, 1)

            def xc_to_sbuf(half, par):
                b, turn, p = back(half, par, 3)
                act.wait_ge(xc_turned, b + 1)
                if not (known(b) and b < 2):
                    act.wait_ge(xc_saved[p], 16 * turn)
                act.activation(xc[:, p].rearrange("p h s -> p (h s)"), ps[:, 6].bitcast(F16), ACT.Copy).then_inc(xc_out, 1)

            def shared_gelu(b, q, first):
                for c in range(FC):
                    act.wait_ge(sh_up, FC * b + c + 1)
                    if c == 0 and not first:
                        act.wait_ge(sh_split, b - 1)
                        act.wait_ge(sh_down, b - 1)
                    act.activation(h_sb[:, q, c], ps[:, c], ACT.Gelu, bias=b1[:, E * FC + c:E * FC + c + 1], scale=1.0 / WS)
                    act.activation(h_hi[:, q, c], ps[:, c], ACT.Gelu, bias=b1[:, E * FC + c:E * FC + c + 1],
                                   scale=1.0 / WS).then_inc(sh_h, 1)

            def cut_high(n):
                e, q = cut_order(n), n % 2
                act.wait_ge(w_in[q], 32 * (n // 2 + 1))
                act.activation(w1[:, e, 0, :], w_stage[:, q, 0, :], ACT.Copy, scale=WS)
                act.activation(w2[:, e, :, 0], w_stage[:, q, 1, :].rearrange("p (c d) -> p c d", c=FC), ACT.Copy, scale=WS).then_inc(w_high, 1)

            def body(half):
                for par in range(2):
                    b = back(half, par, 0)[0]
                    s0, s1, s2, s3, s4 = parts(b)
                    if s4:
                        gap(half, par)
                    if s0:
                        degrees(half, par)
                    if s3:
                        high(half, par)
                    if s1:
                        adj_to_sbuf(half, par, 0)
                        adj_to_sbuf(half, par, 1)
                        xn_to_sbuf(half, par)
                    if s3:
                        xc_to_sbuf(half, par)
                    if known(b) and b == NB + 2:
                        act.wait_ge(b1_out, 1)
                        act.wait_ge(adj_turned, T * NB)
                        shared_gelu(0, 0, True)
                    if s1:
                        adj_to_sbuf(half, par, 2)
                    if s2:
                        elu_floor(half, par)
                    if s1:
                        adj_to_sbuf(half, par, 3)
                    if s2:
                        elu(half, par)
                    if s1:
                        messages(half, par, (0, 1, 2, 3))
                    for n in cut_in(b):
                        cut_high(n)
                    if known(b) and b == 0:
                        act.wait_ge(b1_turned, 1)
                        act.activation(b1[:], ps[:, 6, 0:(E + 1) * FC], ACT.Copy).then_inc(b1_out, 1)
                    if known(b) and b == NB + 3:
                        shared_gelu(1, 1, True)

            steps(act, body)

            for b in range(2, EARLY):
                shared_gelu(b, b % 2, b < 2)

            act.wait_ge(tables, TABLES * GROUPS + 2)
            act.wait_ge(sh_split, EARLY)

            def gelu(k, q, first):
                e = act.value_load(tab_e[0:1, bass.ds(k, 1)], min_val=0, max_val=E - 1)
                if not first:
                    act.wait_ge(split_done, k - 1)
                for c in range(FC):
                    if c % 2 == 0:
                        act.wait_ge(up_done, 2 * k + c // 2 + 1)
                    last = act.activation(h_sb[:, q, c, 0:BLK], ps[:, 2 * q + c // 2, (c % 2) * BLK:(c % 2 + 1) * BLK], ACT.Gelu,
                                          bias=b1[:, bass.ds(e * FC + c, 1)], scale=1.0 / WS)
                    if c % 2:
                        last.then_inc(h_done, 1)

            def xb_to_sbuf(k, q, first):
                act.wait_ge(rows_turned, k + 1)
                if not first:
                    act.wait_ge(up_done, 2 * (k - 1))
                act.activation(xb[:, q].rearrange("p h s -> p (h s)"), ps[:, 6 + q].bitcast(F16)[:, 0:2 * BLK], ACT.Copy).then_inc(xb_out, 1)

            xb_to_sbuf(0, 0, True)
            xb_to_sbuf(1, 1, True)
            for k in range(2):
                gelu(k, k, True)
                xb_to_sbuf(k + 2, k, False)
            with act.Fori(1, NK // 2 - 1) as half:
                for q in range(2):
                    gelu(2 * half + q, q, False)
                    xb_to_sbuf(2 * half + q + 2, q, False)
            for q in range(2):
                gelu(NK - 2 + q, q, False)

            act.wait_ge(split_done, NK)
            with act.Fori(EARLY // 2, NB // 2) as half:
                for q in range(2):
                    shared_gelu(2 * half + q, q, False)

        @block.vector
        def _(dve):
            def normalise_tile(half, par, t):
                b, turn, p = back(half, par, 1)
                if t == 0:
                    dve.wait_ge(rsq1, b + 1)
                    if not (known(b) and b < 1):
                        dve.wait_ge(xn_turned, b)
                last = dve.tensor_scalar(xn[:, t], xin[:, p, t], mvd[:, p, t, 0:1], rs1[:, p, t, 0:1], ALU.subtract, ALU.mult)
                if t == T - 1:
                    last.then_inc(xn_done, 1)

            def normalise2_tile(half, par, t):
                b, turn, p = back(half, par, 3)
                if t == 0:
                    dve.wait_ge(rsq2, b + 1)
                    if not (known(b) and b < 1):
                        dve.wait_ge(high_done, b)
                last = dve.tensor_scalar(xn2[:, t], x2[:, p, t], mv2[:, p, t, 0:1], rs2[:, p, t:t + 1], ALU.subtract, ALU.mult)
                if t == T - 1:
                    last.then_inc(xn2_done, 1)

            def low(half, par):
                b, turn, p = back(half, par, 3)
                dve.wait_ge(high_done, b + 1)
                dve.tensor_tensor(xr[:, p, :, 1, :], xn2[:], xr[:, p, :, 0, :], ALU.subtract).then_inc(low_done, 1)

            def first_stats(half, par):
                b, turn, p = back(half, par, 0)
                dve.wait_ge(x_in[p], 16 * (turn + 1))
                for t in range(T):
                    last = dve.bn_stats(stats[:, t], xin[:, p, t])
                last.then_inc(stats1, 1)

            def first_stats_ready(half, par):
                b = back(half, par, 0)[0]
                dve.wait_ge(stats1, 2 * b + 1)
                if not (known(b) and b < 2):
                    dve.wait_ge(eps1, b - 1)

            def first_variances(half, par):
                b, turn, p = back(half, par, 0)
                for t in range(T):
                    last = dve.bn_aggr(mvd[:, p, t, 0:2], stats[:, t])
                last.then_inc(stats1, 1)

            def het_tile(half, par, t):
                b, turn, p = back(half, par, 1)
                dve.wait_ge(th_done, T * b + t + 1)
                dve.scalar_tensor_tensor(out=het[:, t], in0=th[:, t], scalar=1.0, in1=ps[:, 3 + t % 2, D:2 * D],
                                         op0=ALU.subtract, op1=ALU.mult).then_inc(het_done, 1)

            def gate_of(half, par):
                dve.tensor_scalar(gate[:], th[:], 0.5, 0.5, ALU.mult, ALU.add).then_inc(het_done, 1)

            def combine(half, par):
                b, turn, p = back(half, par, 2)
                m = MIX * b
                dve.wait_ge(het_done, HET * (b + 1))
                dve.wait_ge(hom_done, b + 1)
                for t in range(T):
                    dve.scalar_tensor_tensor(out=mix_o[:, t], in0=ps[:, 5, t * D:(t + 1) * D], scalar=rs1[:, p, t, 1:2],
                                             in1=gate[:, t], op0=ALU.mult, op1=ALU.mult).then_inc(mix, 1)
                dve.wait_ge(mix, m + MIX_HOM)
                dve.scalar_tensor_tensor(out=mix_o[:], in0=het[:], scalar=-0.5, in1=mix_o[:], op0=ALU.mult, op1=ALU.add).then_inc(mix, 1)

            def elu_max(half, par):
                b = back(half, par, 2)[0]
                dve.wait_ge(elu_exp, b + 1)
                dve.scalar_tensor_tensor(out=mix_o[:], in0=mix_e[:], scalar=-1.0, in1=mix_o[:], op0=ALU.add, op1=ALU.max).then_inc(mix, 1)

            def residual(half, par):
                b, turn, p = back(half, par, 2)
                dve.wait_ge(res_in[p], 16 * (turn + 1))
                dve.wait_ge(mix, MIX * b + MIX_ELU)
                dve.tensor_tensor(x2[:, p], x2[:, p], mix_o[:], ALU.add).then_inc(mix, 1)

            def second_stats(half, par, tiles):
                b, turn, p = back(half, par, 2)
                if tiles[0] == 0:
                    dve.wait_ge(mix, MIX * b + MIX_X2)
                for t in tiles:
                    last = dve.bn_stats(stats2[:, t], x2[:, p, t])
                if t == T - 1:
                    last.then_inc(mix, 1)

            def second_stats_ready(half, par):
                b = back(half, par, 2)[0]
                dve.wait_ge(mix, MIX * b + MIX_STATS)
                if not (known(b) and b < 2):
                    dve.wait_ge(eps2, b - 1)

            def second_variances(half, par):
                b, turn, p = back(half, par, 2)
                for t in range(T):
                    last = dve.bn_aggr(mv2[:, p, t], stats2[:, t])
                last.then_inc(mix, 1)

            def choose(half, par, s1, s2, s3):
                b, turn, p = back(half, par, 3)
                r = ROUTE * b
                lg = ps[:, 7, 0:T * E].rearrange("p (t e) -> p t e", e=E)
                hot = [kp[:, p, k * T * E:(k + 1) * T * E].rearrange("p (t e) -> p t e", e=E) for k in range(2)]

                def less(logit, top, n):
                    dve.wait_ge(route, r + n)
                    dve.tensor_tensor(r_ne[:], logit, r_top[:, top].unsqueeze(2).to_broadcast([P, T, E]), ALU.is_lt).then_inc(route, 1)

                def candidates(n):
                    dve.wait_ge(route, r + n)
                    dve.scalar_tensor_tensor(out=r_cand[:], in0=r_ne[:], scalar=64.0, in1=iota_e[:], op0=ALU.mult, op1=ALU.add).then_inc(route, 1)

                def least(n):
                    dve.wait_ge(route, r + n)
                    dve.tensor_reduce(r_idx[:], r_cand[:], AX.X, ALU.min).then_inc(route, 1)

                def one_hot(k, n):
                    dve.wait_ge(route, r + n)
                    dve.tensor_tensor(hot[k], iota_e[:], r_idx[:].unsqueeze(2).to_broadcast([P, T, E]), ALU.is_equal).then_inc(route, 1)

                if s3:
                    dve.wait_ge(logits_done, b + 1)
                    if not (known(b) and b < 2):
                        dve.wait_ge(keep_saved[p], 16 * turn)
                    dve.tensor_reduce(r_top[:, 0], lg, AX.X, ALU.max).then_inc(route, 1)
                    less(lg, 0, 1)
                    candidates(2)
                    least(3)
                    one_hot(0, 4)
                if s2:
                    elu_max(half, par)
                if s1:
                    het_tile(half, par, 0)
                if s3:
                    dve.wait_ge(route, r + 5)
                    dve.scalar_tensor_tensor(out=r_l2[:], in0=hot[0], scalar=-BIG, in1=lg, op0=ALU.mult, op1=ALU.add).then_inc(route, 1)
                if s2:
                    residual(half, par)
                if s1:
                    het_tile(half, par, 1)
                if s3:
                    dve.wait_ge(route, r + 6)
                    dve.tensor_reduce(r_top[:, 1], r_l2[:], AX.X, ALU.max).then_inc(route, 1)
                if s2:
                    second_stats(half, par, (0, 1))
                if s3:
                    less(r_l2[:], 1, 7)
                if s2:
                    second_stats(half, par, (2, 3))
                if s3:
                    candidates(8)
                if s1:
                    het_tile(half, par, 2)
                if s2:
                    second_stats_ready(half, par)
                if s3:
                    least(9)
                if s2:
                    second_variances(half, par)
                if s3:
                    one_hot(1, 10)
                if s1:
                    het_tile(half, par, 3)
                if s3:
                    dve.wait_ge(route, r + 11)
                    dve.tensor_tensor(r_mask[:, p], hot[0], hot[1], ALU.add).then_inc(route, 1)
                    dve.tensor_tensor(r_gap[:], r_top[:, 1], r_top[:, 0], ALU.subtract).then_inc(route, 1)
                    dve.wait_ge(route, r + 12)
                    dve.tensor_reduce(r_red[:], r_mask[:, p].rearrange("p t e -> p e t"), AX.X, ALU.add).then_inc(route, 1)
                if s1:
                    gate_of(half, par)
                if s3:
                    dve.wait_ge(route, r + 14)
                    dve.tensor_tensor(prefix[:, 1 - p], prefix[:, p], r_red[:], ALU.add).then_inc(route, 1)

            def place(half, par, s1, s3, s4):
                b, turn, p = back(half, par, 4)
                r = ROUTE * b
                hot2 = kp[:, p, 0:2 * T * E].rearrange("p (k j) -> p k j", k=2)
                pos, w = kp[:, p, 64:72], kp[:, p, 72:80]
                if s1:
                    normalise_tile(half, par, 0)
                    normalise_tile(half, par, 1)
                if s4:
                    dve.wait_ge(rank_done, b + 1)
                    dve.tensor_tensor(r_pos[:], ps[:, 7, 64:64 + T * E].rearrange("p (t e) -> p t e", e=E),
                                      reg_base[:].unsqueeze(1).to_broadcast([P, T, E]), ALU.add).then_inc(route, 1)
                if s1:
                    normalise_tile(half, par, 2)
                if s4:
                    dve.wait_ge(route, r + 16)
                    dve.tensor_tensor(r_prod[:].rearrange("p (k t) e -> p k (t e)", k=2), hot2,
                                      r_pos[:].rearrange("p t e -> p (t e)").unsqueeze(1).to_broadcast([P, 2, T * E]), ALU.mult).then_inc(route, 1)
                if s1:
                    normalise_tile(half, par, 3)
                if s4:
                    dve.wait_ge(route, r + 17)
                    dve.tensor_reduce(pos, r_prod[:], AX.X, ALU.add).then_inc(route, 1)
                    if not (known(b) and b < 2):
                        dve.wait_ge(scattered[p], 16 * 2 * T * turn)
                    dve.wait_ge(route, r + R_IDX - 1)
                    dve.tensor_copy(idx[:, p], pos).then_inc(route, 1)
                    if known(b) and b == NB - 1:
                        shared_split(0)
                    dve.wait_ge(gap_exp, b + 1)
                    dve.tensor_scalar(r_sum[:], r_exp[:], 1.0, WS, ALU.add, ALU.mult).then_inc(route, 1)
                    dve.wait_ge(route, r + 20)
                    dve.reciprocal(w[:, 0:T], r_sum[:]).then_inc(route, 1)
                if s3:
                    normalise2_tile(half, par, 0)
                    normalise2_tile(half, par, 1)
                if s4:
                    dve.wait_ge(route, r + 21)
                    dve.tensor_tensor(w[:, T:2 * T], w[:, 0:T], r_exp[:], ALU.mult).then_inc(route, 1)
                if s3:
                    normalise2_tile(half, par, 2)
                    normalise2_tile(half, par, 3)

            def shared_split(b):
                q = b % 2
                dve.wait_ge(sh_h, FC * (b + 1))
                if b >= 2:
                    dve.wait_ge(sh_down, b - 1)
                dve.tensor_tensor(h_lo[:, q], h_sb[:, q], h_hi[:, q], ALU.subtract).then_inc(sh_split, 1)

            def shared_out(b):
                dve.wait_ge(sh_down, b + 1)
                dve.wait_ge(x2_saved[b % 2], 16 * (b // 2 + 1))
                dve.scalar_tensor_tensor(out=x2_all[:, b], in0=ps[:, 4 + b % 2], scalar=1.0 / WS, in1=x2_all[:, b],
                                         op0=ALU.mult, op1=ALU.add).then_inc(sh_comb, 1)

            def cut_low(n):
                e, q = cut_order(n), n % 2
                dve.wait_ge(w_high, n + 1)
                dve.scalar_tensor_tensor(out=w1[:, e, 1, :], in0=w_stage[:, q, 0, :], scalar=WS, in1=w1[:, e, 0, :],
                                         op0=ALU.mult, op1=ALU.subtract)
                dve.scalar_tensor_tensor(out=w2[:, e, :, 1], in0=w_stage[:, q, 1, :].rearrange("p (c d) -> p c d", c=FC), scalar=WS,
                                         in1=w2[:, e, :, 0], op0=ALU.mult, op1=ALU.subtract).then_inc(w_low, 1)

            def count_own(g):
                for q in range(2):
                    dve.wait_ge(keep_saved[q], 16 * ((FIRST[g + 1] + 1 - q) // 2))
                dve.tensor_reduce(t_sum[:, g], keep[:, FIRST[g]:FIRST[g + 1], 0:2 * T * E].rearrange("p b (k e) -> p e b k", e=E), AX.XY, ALU.add).then_inc(counted, 1)
                if g == 0:
                    dve.tensor_copy(t_first[:, 0], reg_base[:])
                    dve.memset(t_ef[:, NK:NK + 4], 0.0)
                dve.wait_ge(counted, COUNTS * g + 1)
                dve.tensor_copy(t_own[:, g], t_sum[:, g]).then_inc(counted, 1)

            def count_out(g):
                dve.wait_ge(count_done, g + 1)
                dve.tensor_copy(t_cnt[:, g], ps[:, 7, 128:128 + E]).then_inc(counted, 1)
                dve.wait_ge(counted, COUNTS * g + 3)
                dve.tensor_tensor(t_first[:, g + 1], t_first[:, g], t_cnt[:, g], ALU.add).then_inc(counted, 1)

            def make_tables(g):
                m = TABLES * g
                own, n = [BLK0[g], BLK0[g + 1]], NBLKS[g]
                t_past, t_eraw, t_used, t_off, t_row, numbers = (t[:, 0:n] for t in (t_past_all, t_eraw_all, t_used_all, t_off_all, t_row_all, blk_iota))
                dve.tensor_tensor(t_cmp[:], cap_iota[:].unsqueeze(1).to_broadcast([P, E, MAXB]),
                                  t_cnt[:, g].unsqueeze(2).to_broadcast([P, E, MAXB]), ALU.is_lt).then_inc(tables, 1)
                dve.wait_ge(tables, m + 1)
                dve.tensor_reduce(t_nblk[:], t_cmp[:], AX.X, ALU.add).then_inc(tables, 1)
                dve.wait_ge(tables, m + 2)
                dve.tensor_tensor(t_low[:], lower[:], t_nblk[:].unsqueeze(1).to_broadcast([P, E, E]), ALU.mult).then_inc(tables, 1)
                dve.wait_ge(tables, m + 3)
                dve.tensor_reduce(t_start[:], t_low[:], AX.X, ALU.add).then_inc(tables, 1)
                dve.wait_ge(tables, m + 4)
                dve.tensor_tensor(t_end[:], t_start[:], t_nblk[:], ALU.add)
                dve.scalar_tensor_tensor(out=t_delta[:, g], in0=t_start[:], scalar=float(BLK), in1=t_first[:, g], op0=ALU.mult, op1=ALU.subtract).then_inc(tables, 1)
                dve.wait_ge(tables, m + 5)
                dve.tensor_tensor(t_past, t_end[:].unsqueeze(1).to_broadcast([P, n, E]),
                                  numbers.unsqueeze(2).to_broadcast([P, n, E]), ALU.is_le).then_inc(tables, 1)
                dve.wait_ge(tables, m + 6)
                dve.tensor_reduce(t_eraw, t_past, AX.X, ALU.add).then_inc(tables, 1)
                dve.wait_ge(tables, m + 7)
                dve.tensor_scalar(t_used, t_eraw, float(E), None, ALU.is_lt)
                dve.tensor_scalar(t_ef[:, own[0]:own[1]], t_eraw, float(E - 1), None, ALU.min)
                dve.tensor_tensor(t_past, t_eraw.unsqueeze(2).to_broadcast([P, n, E]),
                                  iota_e[:, 0, :].unsqueeze(1).to_broadcast([P, n, E]), ALU.is_equal)
                dve.tensor_scalar(t_row, numbers, float(BLK), float(-PADROW), ALU.mult, ALU.add).then_inc(tables, 1)
                dve.wait_ge(tables, m + 8)
                dve.tensor_tensor(t_past, t_past, t_delta[:, g].unsqueeze(1).to_broadcast([P, n, E]), ALU.mult)
                dve.tensor_tensor(t_row, t_row, t_used, ALU.mult).then_inc(tables, 1)
                dve.wait_ge(tables, m + 9)
                dve.tensor_reduce(t_off, t_past, AX.X, ALU.add).then_inc(tables, 1)
                dve.wait_ge(tables, m + 10)
                dve.scalar_tensor_tensor(out=tab_row[:, own[0]:own[1]], in0=t_row, scalar=float(PADROW), in1=t_off,
                                         op0=ALU.add, op1=ALU.subtract).then_inc(tables, 1)

            def body(half):
                for par in range(2):
                    b = back(half, par, 0)[0]
                    s0, s1, s2, s3, s4 = parts(b)
                    place(half, par, s1, s3, s4)
                    if s0:
                        first_stats(half, par)
                        first_stats_ready(half, par)
                    if s3:
                        low(half, par)
                    if s0:
                        first_variances(half, par)
                    if s2:
                        combine(half, par)
                    if known(b) and b == NB + 1:
                        count_out(0)
                    choose(half, par, s1, s2, s3)
                    for n in cut_in(b):
                        cut_low(n)
                    if known(b) and b == NB:
                        count_own(0)
                    if known(b) and b == NB + 2:
                        dve.wait_ge(counted, COUNTS)
                        make_tables(0)
                    if known(b) and b == 0:
                        cut_router_weights()

            def cut_router_weights():
                dve.wait_ge(const_in, 16 * 5)
                dve.wait_ge(bias_in, 16 * 4)
                dve.tensor_scalar(wr16[:, 0], wr_f[:], WS, None, ALU.mult).then_inc(setup_v, 1)
                dve.tensor_tensor(b2[:], b2[:], b2s_bc[:].unsqueeze(1).to_broadcast([P, E, D]), ALU.add).then_inc(setup_v, 1)
                dve.wait_ge(setup_v, 1)
                dve.scalar_tensor_tensor(out=wr16[:, 1], in0=wr_f[:], scalar=WS, in1=wr16[:, 0], op0=ALU.mult, op1=ALU.subtract).then_inc(setup_v, 1)
                dve.wait_ge(setup_v, 3)
                dve.tensor_scalar(b2[:], b2[:], WS, None, ALU.mult).then_inc(setup_v, 1)

            dve.wait_ge(const_in, 16 * 5)
            dve.tensor_copy(bt16[:, 0], bt_row[:]).then_inc(bt_cut, 1)
            dve.wait_ge(bt_cut, 1)
            dve.tensor_tensor(bt16[:, 1], bt_row[:], bt16[:, 0], ALU.subtract).then_inc(bt_cut, 1)
            steps(dve, body)

            def make_indices(g):
                n = GROUP_BATCHES[g]
                y_prod, y_off = y_prod_all[:, 0:n * 2 * T], y_off_all[:, 0:n * 2 * T]
                dve.tensor_tensor(y_prod.rearrange("p (b k) e -> p b k e", b=n),
                                  keep[:, FIRST[g]:FIRST[g + 1], 0:2 * T * E].rearrange("p b (k e) -> p b k e", e=E),
                                  t_delta[:, g].unsqueeze(1).unsqueeze(1).to_broadcast([P, n, 2 * T, E]), ALU.mult).then_inc(indices, 1)
                dve.wait_ge(indices, 3 * g + 1)
                dve.tensor_reduce(y_off, y_prod, AX.X, ALU.add).then_inc(indices, 1)
                dve.wait_ge(indices, 3 * g + 2)
                dve.tensor_tensor(y_idx[:, g, 0:n * 2 * T].rearrange("p (b k) -> p b k", b=n), y_off.rearrange("p (b k) -> p b k", b=n),
                                  keep[:, FIRST[g]:FIRST[g + 1], 64:72], ALU.add).then_inc(indices, 1)

            def add_up(b):
                q, r = b % 2, b % RING
                dve.tensor_copy(wb[:, q], keep[:, b, 72:80]).then_inc(wb_done, 1)
                dve.wait_ge(gathered[r], 16 * 2 * T * (b // RING + 1))
                dve.wait_ge(wb_done, b + 1)
                for k in range(2):
                    if k == 1:
                        dve.wait_ge(sh_add, 2 * T * b + T)
                    for t in range(T):
                        a = x2_all[:, b, t * D:(t + 1) * D]
                        dve.scalar_tensor_tensor(out=a, in0=yg[:, r, k * T + t], scalar=wb[:, q, k * T + t:k * T + t + 1], in1=a,
                                                 op0=ALU.mult, op1=ALU.add).then_inc(sh_add, 1)

            count_own(GROUPS - 1)
            shared_split(1)
            count_out(GROUPS - 1)
            dve.wait_ge(counted, COUNTS * GROUPS)
            dve.tensor_copy(tab_pad[:], t_first[:, GROUPS]).then_inc(pad_rows, 1)
            make_tables(GROUPS - 1)
            shared_out(0)
            dve.tensor_copy(tab_e[:], t_ef[:, 0:NK])
            dve.scalar_tensor_tensor(out=t_pair[:], in0=t_ef[:, 1:NK + 3], scalar=float(E), in1=t_ef[:, 0:NK + 2], op0=ALU.mult, op1=ALU.add).then_inc(tables, 1)
            dve.wait_ge(tables, TABLES * GROUPS + 1)
            dve.scalar_tensor_tensor(out=tab_four[:], in0=t_pair[:, 2:NK + 2], scalar=float(E * E), in1=t_pair[:, 0:NK],
                                     op0=ALU.mult, op1=ALU.add).then_inc(tables, 1)
            for q in range(2):
                dve.wait_ge(x2_saved[q], 16 * NB // 2)
            for b in range(2, EARLY):
                shared_split(b)
                shared_out(b - 1)
            shared_out(EARLY - 1)
            for g in range(GROUPS):
                make_indices(g)

            dve.wait_ge(sh_down, EARLY)
            def split(k, q, first):
                dve.wait_ge(h_done, 2 * (k + 1))
                if not first:
                    dve.wait_ge(down_done, k - 1)
                dve.tensor_copy(h_hi[:, q, :, 0:BLK], h_sb[:, q, :, 0:BLK]).then_inc(split_hi, 1)
                dve.wait_ge(split_hi, k + 1)
                dve.tensor_tensor(h_lo[:, q, :, 0:BLK], h_sb[:, q, :, 0:BLK], h_hi[:, q, :, 0:BLK], ALU.subtract).then_inc(split_done, 1)

            def y_to_sbuf(k, turn, q, first):
                e = dve.value_load(tab_e[0:1, bass.ds(k, 1)], min_val=0, max_val=E - 1)
                dve.wait_ge(down_done, k + 1)
                if not first:
                    dve.wait_ge(y_saved[q], 16 * turn)
                o = ps[:, 4 + q].rearrange("p (s h d) -> p s h d", s=2, h=2)
                dve.tensor_tensor(y_half[:, q], o[:, :, 1], b2[:, bass.ds(e, 1), :].to_broadcast([P, 2, D]), ALU.add).then_inc(y_part, 1)
                dve.wait_ge(y_part, k + 1)
                dve.tensor_tensor(y_sb[:, q], o[:, :, 0], y_half[:, q], ALU.add).then_inc(y_done, 1)

            split(0, 0, True)
            split(1, 1, True)
            y_to_sbuf(0, 0, 0, True)
            split(2, 0, False)
            y_to_sbuf(1, 0, 1, True)
            split(3, 1, False)
            y_to_sbuf(2, 1, 0, False)
            with dve.Fori(2, BLK0[-2] // 2) as half:
                split(2 * half, 0, False)
                y_to_sbuf(2 * half - 1, half - 1, 1, False)
                split(2 * half + 1, 1, False)
                y_to_sbuf(2 * half, half, 0, False)
            for q in range(2):
                dve.wait_ge(x2_saved[q], 16 * NB // 2)
            for k in range(BLK0[-2] // 2 * 2, NK):
                split(k, k % 2, False)
                y_to_sbuf(k - 1, (k - 1) // 2, (k - 1) % 2, False)
                if add_after(k - BLK0[-2]) is not None:
                    add_up(add_after(k - BLK0[-2]))
            y_to_sbuf(NK - 1, NK // 2 - 1, 1, False)

            dve.wait_ge(down_done, NK)
            shared_split(EARLY)
            for i in range(NB - EARLY):
                b = EARLY + i
                if b + 1 < NB:
                    shared_split(b + 1)
                last = b == NB - 1
                if last:
                    add_up(b)
                if last or b < ADDS_IN_C + sum(len(adds(n)) for n in range(i)):
                    dve.wait_ge(sh_add, 2 * T * (b + 1))
                shared_out(b)
                for n in () if last else adds(i):
                    if n < b + 1:
                        dve.wait_ge(sh_comb, n + 1)
                    add_up(n)

        @block.tensor
        def _(pe):
            def turn_adj(half, par, n, j):
                b, turn, p = back(half, par, n)
                if j == 0:
                    pe.wait_ge(adj_in[p], 16 * (turn + 1))
                if not (known(b) and b == 0 and j < 2):
                    pe.wait_ge(adj_out, T * b + j - 1)
                for t in range(T):
                    last = pe.transpose(ps[:, j % 2, t * P:(t + 1) * P], adj_sb[:, p, t, j * P:(j + 1) * P], ident[:])
                last.then_inc(adj_turned, 1)

            def turn_xn(half, par):
                b, turn, p = back(half, par, 1)
                pe.wait_ge(xn_done, b + 1)
                if not (known(b) and b == 0):
                    pe.wait_ge(xn_out, b)
                for t in range(T):
                    last = pe.transpose(ps[:, 2, t * P:(t + 1) * P], xn[:, t], ident[:])
                last.then_inc(xn_turned, 1)

            def turn_xc(half, par):
                b, turn, p = back(half, par, 3)
                pe.wait_ge(low_done, b + 1)
                if known(b) and b == 0:
                    pe.wait_ge(b1_out, 1)
                else:
                    pe.wait_ge(xc_out, b)
                for h in range(2):
                    for t in range(T):
                        last = pe.transpose(ps[:, 6].bitcast(F16)[:, h * S + t * P:h * S + (t + 1) * P], xr[:, p, t, h], ident16[:])
                last.then_inc(xc_turned, 1)

            def project(half, par, tiles):
                b, turn, p = back(half, par, 1)
                pe.wait_ge(xn_out, b + 1)
                for t in tiles:
                    if not (known(b) and b == 0 and t < 2):
                        tb, tt = (b, t - 2) if t >= 2 else (b - 1, t + 2)
                        pe.wait_ge(het_done, HET * tb + tt + 1)
                    lhs = xn_t[:, t * P:(t + 1) * P]
                    pe.matmul(ps[:, 3 + t % 2, 0:3 * D], lhs, w_gnn[:], start=True, stop=False)
                    pe.matmul(ps[:, 3 + t % 2, 0:D], ones16[0:1, :], bt16[:, 0], start=False, stop=False)
                    pe.matmul(ps[:, 3 + t % 2, 0:D], ones16[0:1, :], bt16[:, 1], start=False, stop=True).then_inc(proj_done, 1)

            def logits(half, par):
                b, turn, p = back(half, par, 3)
                pe.wait_ge(xc_out, b + 1)
                if known(b) and b == 0:
                    pe.wait_ge(setup_v, 3)
                else:
                    pe.wait_ge(route, ROUTE * (b - 1) + R_RANK_READ)
                for t in range(T):
                    o = ps[:, 7, t * E:(t + 1) * E]
                    hi, lo = (xc[:, p, h, t * P:(t + 1) * P] for h in range(2))
                    pe.matmul(o, hi, wr16[:, 0], start=True, stop=False)
                    pe.matmul(o, hi, wr16[:, 1], start=False, stop=False)
                    last = pe.matmul(o, lo, wr16[:, 0], start=False, stop=True)
                last.then_inc(logits_done, 1)

            def homophily(half, par):
                b, turn, p = back(half, par, 2)
                pe.wait_ge(adj_out, T * (b + 1))
                pe.wait_ge(th_done, T * (b + 1))
                if not (known(b) and b == 0):
                    pe.wait_ge(mix, MIX * (b - 1) + MIX_HOM)
                for t in range(T):
                    for j in range(T):
                        last = pe.matmul(ps[:, 5, t * D:(t + 1) * D], adj_t[:, j, t * P:(t + 1) * P], f_sb[:, j],
                                         start=(j == 0), stop=(j == T - 1))
                last.then_inc(hom_done, 1)

            def count(g):
                pe.wait_ge(counted, COUNTS * g + 2)
                pe.matmul(ps[:, 7, 128:128 + E], ones16[:], t_own[:, g], start=True, stop=True).then_inc(count_done, 1)

            def rank(half, par):
                b, turn, p = back(half, par, 3)
                pe.wait_ge(route, ROUTE * b + R_MASK)
                def o(t):
                    return ps[:, 7, 64 + t * E:64 + T * E]
                pe.matmul(o(0), before[:], r_mask[:, p].rearrange("p t e -> p (t e)"), start=True, stop=False)
                for t in range(T - 1):
                    for u in range(t + 1, T):
                        pe.matmul(ps[:, 7, 64 + u * E:64 + (u + 1) * E], ones16[:], r_mask[:, p, t], start=False, stop=False)
                for u in range(T):
                    last = pe.matmul(ps[:, 7, 64 + u * E:64 + (u + 1) * E], ones16[:], prefix[:, p], start=False, stop=(u == T - 1))
                last.then_inc(rank_done, 1)

            def body(half):
                for par in range(2):
                    b = back(half, par, 0)[0]
                    s0, s1, s2, s3, s4 = parts(b)
                    if s2:
                        homophily(half, par)
                    if s1:
                        turn_xn(half, par)
                    if s3:
                        turn_xc(half, par)
                    if s1:
                        turn_adj(half, par, 1, 2)
                        turn_adj(half, par, 1, 3)
                    if s3:
                        logits(half, par)
                    if known(b) and b == NB + 1:
                        count(0)
                    if s1:
                        project(half, par, (0, 1))
                    if s0:
                        turn_adj(half, par, 0, 0)
                    if s1:
                        project(half, par, (2, 3))
                    if s0:
                        turn_adj(half, par, 0, 1)
                    if s3:
                        rank(half, par)
                    if known(b) and b == 0:
                        pe.wait_ge(bias_in, 16 * 4)
                        pe.transpose(ps[:, 6, 0:P], b1_rows[:], ident[:]).then_inc(b1_turned, 1)
                    if known(b) and b == NB + 1:
                        pe.wait_ge(w_low, 1)
                        shared_up(0, 0, 0, True)
                    if known(b) and b == NB + 2:
                        shared_up(1, 1, 0, False)

            def shared_up(b, q, turn, first):
                pe.wait_ge(xcb_in[q], 16 * (turn + 1))
                for c in range(FC):
                    if not first:
                        pe.wait_ge(sh_h, FC * (b - 1) + c + 1)
                    hi, lo = (w1[:, E, h, c * P:(c + 1) * P] for h in range(2))
                    pe.matmul(ps[:, c], hi, xcb[:, q, 0], start=True, stop=False)
                    pe.matmul(ps[:, c], hi, xcb[:, q, 1], start=False, stop=False)
                    pe.matmul(ps[:, c], lo, xcb[:, q, 0], start=False, stop=True).then_inc(sh_up, 1)

            def shared_down(b, q, first):
                pe.wait_ge(sh_split, b + 1)
                if not first:
                    pe.wait_ge(sh_comb, b - 1)
                for t in range(T):
                    o = ps[:, 4 + q, t * D:(t + 1) * D]
                    for c in range(FC):
                        hh, hl = h_hi[:, q, c, t * P:(t + 1) * P], h_lo[:, q, c, t * P:(t + 1) * P]
                        pe.matmul(o, hh, w2[:, E, c, 0], start=(c == 0), stop=False)
                        pe.matmul(o, hh, w2[:, E, c, 1], start=False, stop=False)
                        last = pe.matmul(o, hl, w2[:, E, c, 0], start=False, stop=(c == FC - 1))
                last.then_inc(sh_down, 1)

            pe.wait_ge(const_made, 12)
            pe.wait_ge(const_in, 16 * 5)
            pe.wait_ge(bt_cut, 2)
            steps(pe, body)

            for b in range(EARLY):
                shared_down(b, b % 2, b < 2)
                if b == 0:
                    count(GROUPS - 1)
                if b + 2 < EARLY:
                    shared_up(b + 2, b % 2, b // 2 + 1, False)

            pe.wait_ge(tables, TABLES * GROUPS + 2)
            pe.wait_ge(w_low, E + 1)
            pe.wait_ge(sh_h, FC * EARLY)
            pe.wait_ge(sh_comb, EARLY)

            def expert(k):
                return pe.value_load(tab_e[0:1, bass.ds(k, 1)], min_val=0, max_val=E - 1)

            def turn_rows(k, turn, q, first):
                pe.wait_ge(rows_in[q], 16 * (turn + 1))
                if not first:
                    pe.wait_ge(xb_out, k - 1)
                for h in range(2):
                    for t in range(BLK // P):
                        last = pe.transpose(ps[:, 6 + q].bitcast(F16)[:, h * BLK + t * P:h * BLK + (t + 1) * P],
                                            rows_sb[:, q, t, h * D:(h + 1) * D], ident16[:])
                last.then_inc(rows_turned, 1)

            def up(e, k, q, first):
                pe.wait_ge(xb_out, k + 1)
                if not first:
                    pe.wait_ge(h_done, 2 * (k - 1))
                for c in range(FC):
                    o = ps[:, 2 * q + c // 2, (c % 2) * BLK:(c % 2 + 1) * BLK]
                    hi, lo = (w1[:, bass.ds(e, 1), h, c * P:(c + 1) * P].rearrange("p a f -> p (a f)") for h in range(2))
                    pe.matmul(o, hi, xb[:, q, 0], start=True, stop=False)
                    pe.matmul(o, hi, xb[:, q, 1], start=False, stop=False)
                    last = pe.matmul(o, lo, xb[:, q, 0], start=False, stop=True)
                    if c % 2:
                        last.then_inc(up_done, 1)

            def down(e, k, q, first):
                pe.wait_ge(split_done, k + 1)
                if not first:
                    pe.wait_ge(y_done, k - 1)
                o = ps[:, 4 + q].rearrange("p (s h d) -> p s h d", s=2, h=2)
                for c in range(FC):
                    w = w2[:, bass.ds(e, 1), c].rearrange("p a h d -> p (a h d)")
                    for s in range(BLK // P):
                        pe.matmul(ps[:, 4 + q, 2 * s * D:2 * (s + 1) * D], h_hi[:, q, c, s * P:(s + 1) * P], w,
                                  start=(c == 0 and s == 0), stop=False)
                    for s in range(BLK // P):
                        last = pe.matmul(o[:, s, 0], h_lo[:, q, c, s * P:(s + 1) * P], w[:, 0:D],
                                         start=False, stop=(c == FC - 1 and s == BLK // P - 1))
                last.then_inc(down_done, 1)

            turn_rows(0, 0, 0, True)
            turn_rows(1, 0, 1, True)
            for k in range(2):
                up(expert(k), k, k, True)
                turn_rows(k + 2, 1, k, False)
            for k in range(2):
                up(expert(k + 2), k + 2, k, False)
                turn_rows(k + 4, 2, k, False)
                down(expert(k), k, k, True)
            with pe.Fori(1, NK // 2 - 2) as half:
                four = pe.value_load(tab_four[0:1, bass.ds(2 * half, 1)], min_val=0, max_val=E ** 4 - 1)
                for q in range(2):
                    k = 2 * half + q
                    up(four // E ** (q + 2) % E, k + 2, q, False)
                    turn_rows(k + 4, half + 2, q, False)
                    down(four // E ** q % E, k, q, False)
            for k in range(NK - 4, NK):
                if k + 2 < NK:
                    up(expert(k + 2), k + 2, k % 2, False)
                if k == NK - 1:
                    pe.wait_ge(h_done, 2 * NK)
                    shared_up(EARLY, 0, EARLY // 2, True)
                down(expert(k), k, k % 2, False)

            shared_up(EARLY + 1, 1, EARLY // 2, False)
            pe.wait_ge(y_done, NK)
            with pe.Fori(EARLY // 2, NB // 2 - 1) as half:
                shared_down(2 * half, 0, False)
                shared_up(2 * half + 2, 0, half + 1, False)
                shared_down(2 * half + 1, 1, False)
                shared_up(2 * half + 3, 1, half + 1, False)
            shared_down(NB - 2, 0, False)
            shared_down(NB - 1, 1, False)


_INS = ['x', 'adj', 'L0_gnn_W_t', 'L0_gnn_b_t', 'L0_gnn_W_h', 'L0_gnn_theta', 'L0_ffn_Wr', 'L0_ffn_W1s', 'L0_ffn_b1s',
        'L0_ffn_W2s', 'L0_ffn_b2s', 'L0_ffn_W1p', 'L0_ffn_b1p', 'L0_ffn_W2p', 'L0_ffn_b2p']
_OUTS = [((16, 512, 128), 'float32')]


def kernel(**inputs):
    import numpy as _np
    import concourse.bacc as _bacc
    from concourse import mybir as _mybir
    from concourse.bass_utils import run_bass_kernel_spmd as _run

    nc = _bacc.Bacc("TRN2", target_bir_lowering=False, num_devices=1)
    arrays, args = {}, []
    for name in _INS:
        a = _np.ascontiguousarray(inputs[name])
        arrays[f"in_{name}_dram"] = a
        args.append(nc.dram_tensor(f"in_{name}_dram", a.shape, _mybir.dt.from_np(a.dtype), kind="ExternalInput").ap())
    for i, (shape, dtype) in enumerate(_OUTS):
        dt = _mybir.dt.from_np(_np.dtype(dtype))
        args.append(nc.dram_tensor(f"out_{i}_dram", shape, dt, kind="ExternalOutput").ap())
    build(nc, *args)
    r = _run(nc, [arrays], core_ids=[0])
    got = tuple(r.results[0][f"out_{i}_dram"] for i in range(len(_OUTS)))
    return got[0]
```
